# Optimizing a Trainium2 kernel written in Bass

```python
import numpy as np
import jax
import jax.numpy as jnp

def _softmax(x, axis=-1):
    return jax.nn.softmax(x, axis=axis)

def _gelu(x):
    return jax.nn.gelu(x, approximate=True)

def _silu(x):
    return jax.nn.silu(x)

def _sigmoid(x):
    return jax.nn.sigmoid(x)

def _layernorm(x, axis=-1, eps=1e-05):
    m = jnp.mean(x, axis=axis, keepdims=True)
    v = jnp.var(x, axis=axis, keepdims=True)
    return (x - m) / jnp.sqrt(v + eps)

def _scatter_add(tgt, idx, src, axis=0):
    return tgt.at[idx].add(src)

def _segment_sum(src, seg, n):
    return jax.ops.segment_sum(src, seg, n)
kernel_name = 'mk_decoder_postln_d1_seqx_r4_506d6e'

def setup_inputs(seed: int=0):
    np.random.seed(seed)
    _w = jnp.asarray

    def _rec_inputs():
        import jax
        import jax.numpy as jnp
        _rk = jax.random.key(seed)
        x = -0.0002928 + 1 * jax.random.normal(jax.random.fold_in(_rk, 1), (32, 128, 256), jnp.float32)
        _lenS = 128 - jax.random.randint(jax.random.fold_in(_rk, 7), (32,), 0, max(1, 128 // 4) + 1, jnp.int32)
        _lenS2 = 128 - jax.random.randint(jax.random.fold_in(_rk, 8), (32,), 0, max(1, 128 // 4) + 1, jnp.int32)
        _ctx_1024P = jax.random.normal(jax.random.fold_in(_rk, 11), (32, 16, 256), jnp.float32)
        _ctx_1024c = jax.random.dirichlet(jax.random.fold_in(_rk, 511), 0.3 * jnp.ones((16,), jnp.float32), (32, 128))
        _ctx_1024t = jnp.einsum('bsk,bkd->bsd', _ctx_1024c, _ctx_1024P)
        _ctx_1024t = _ctx_1024t * jax.lax.rsqrt(jnp.mean(jnp.square(_ctx_1024t)) + 1e-12) * 0.953939
        ctx_1024 = -1.39393e-06 + 0.999914 * (_ctx_1024t + 0.3 * jax.random.normal(jax.random.fold_in(_rk, 611), (32, 128, 256), jnp.float32))
        return (x, ctx_1024)
    x, ctx_1024 = _rec_inputs()

    def _L0_attn_setup():
        import jax, jax.numpy as jnp
        import numpy as np
        import math
        D_MODEL = 256
        D_STATE = 16
        DT_RANK = 64
        DT_MIN, DT_MAX = (0.001, 0.1)

        def _selective_scan(x, delta, A, Bm, Cm):
            b, l, d = x.shape
            n = A.shape[1]
            dA = jnp.exp(delta[..., None] * A)
            dBx = (delta * x)[..., None] * Bm[:, :, None, :]

            def step(h, inp):
                dA_t, dBx_t, C_t = inp
                h = dA_t * h + dBx_t
                y = jnp.einsum('bdn,bn->bd', h, C_t)
                return (h, y)
            h0 = jnp.zeros((b, d, n), dtype=x.dtype)
            _, ys = jax.lax.scan(step, h0, (jnp.swapaxes(dA, 0, 1), jnp.swapaxes(dBx, 0, 1), jnp.swapaxes(Cm, 0, 1)))
            return jnp.swapaxes(ys, 0, 1)
        key = jax.random.key(seed)
        k1, k2, k3, k4 = jax.random.split(key, 4)
        B, L, D, N, R = (2, 512, D_MODEL, D_STATE, DT_RANK)
        hidden_states = jax.random.normal(k1, (B, L, D), dtype=jnp.float32)
        W_xproj = jax.random.normal(k2, (R + 2 * N, D), dtype=jnp.float32) * D ** (-0.5)
        dt_init_std = R ** (-0.5)
        W_dt = jax.random.uniform(k3, (D, R), dtype=jnp.float32, minval=-dt_init_std, maxval=dt_init_std)
        dt = jnp.exp(jax.random.uniform(k4, (D,), dtype=jnp.float32) * (math.log(DT_MAX) - math.log(DT_MIN)) + math.log(DT_MIN))
        dt = jnp.clip(dt, 0.0001, None)
        b_dt = dt + jnp.log(-jnp.expm1(-dt))
        A_log = jnp.log(jnp.broadcast_to(jnp.arange(1, N + 1, dtype=jnp.float32), (D, N)))
        return {'hidden_states': hidden_states, 'W_xproj': W_xproj, 'W_dt': W_dt, 'b_dt': b_dt, 'A_log': A_log}
    _L0_attn_all = _L0_attn_setup()
    _L0_attn_in = {k: v for k, v in _L0_attn_all.items() if k in ('W_xproj', 'W_dt', 'b_dt', 'A_log')}
    del _L0_attn_all

    def _L0_xattn_setup():
        import jax, jax.numpy as jnp
        import numpy as np
        D_MODEL = 256
        NUM_HEADS = 16
        D_K = D_MODEL // NUM_HEADS
        LN_EPS = 1e-05

        def _layernorm(x, gamma, beta):
            mu = jnp.mean(x, axis=-1, keepdims=True)
            var = jnp.var(x, axis=-1, keepdims=True)
            return (x - mu) * jax.lax.rsqrt(var + LN_EPS) * gamma + beta
        key = jax.random.key(seed)
        ks = jax.random.split(key, 7)
        B, S = (2, 512)
        scale = 1.0 / np.sqrt(D_MODEL)
        return {'query': jax.random.normal(ks[0], (B, S, D_MODEL), jnp.float32), 'key': jax.random.normal(ks[1], (B, S, D_MODEL), jnp.float32), 'value': jax.random.normal(ks[2], (B, S, D_MODEL), jnp.float32), 'Wq': jax.random.normal(ks[3], (D_MODEL, D_MODEL), jnp.float32) * scale, 'Wk': jax.random.normal(ks[4], (D_MODEL, D_MODEL), jnp.float32) * scale, 'Wv': jax.random.normal(ks[5], (D_MODEL, D_MODEL), jnp.float32) * scale, 'Wo': jax.random.normal(ks[6], (D_MODEL, D_MODEL), jnp.float32) * scale, 'ln_gamma': jnp.ones((D_MODEL,), jnp.float32), 'ln_beta': jnp.zeros((D_MODEL,), jnp.float32)}
    _L0_xattn_all = _L0_xattn_setup()
    _L0_xattn_in = {k: v for k, v in _L0_xattn_all.items() if k in ('Wq', 'Wk', 'Wv', 'Wo', 'ln_gamma', 'ln_beta')}
    del _L0_xattn_all

    def _L0_ffn_setup():
        import jax, jax.numpy as jnp
        import numpy as np
        B, L, H, E, FF, C = (4, 512, 256, 8, 1024, 2)
        key = jax.random.key(seed)
        ks = jax.random.split(key, 6)
        s = 0.02
        return {'x': jax.random.normal(ks[0], (B, L, H), dtype=jnp.float32), 'Wg': jax.random.normal(ks[1], (H, E), dtype=jnp.float32) * s, 'W1': jax.random.normal(ks[2], (E, H, FF), dtype=jnp.float32) * s, 'b1': jnp.zeros((E, FF), dtype=jnp.float32), 'W2': jax.random.normal(ks[3], (E, FF, H), dtype=jnp.float32) * s, 'b2': jnp.zeros((E, H), dtype=jnp.float32)}
    _L0_ffn_all = _L0_ffn_setup()
    _L0_ffn_in = {k: v for k, v in _L0_ffn_all.items() if k in ('Wg', 'W1', 'b1', 'W2', 'b2')}
    del _L0_ffn_all
    return {'x': x, 'ctx_1024': ctx_1024, 'L0_attn_W_xproj': _L0_attn_in['W_xproj'], 'L0_attn_W_dt': _L0_attn_in['W_dt'], 'L0_attn_b_dt': _L0_attn_in['b_dt'], 'L0_attn_A_log': _L0_attn_in['A_log'], 'L0_xattn_Wq': _L0_xattn_in['Wq'], 'L0_xattn_Wk': _L0_xattn_in['Wk'], 'L0_xattn_Wv': _L0_xattn_in['Wv'], 'L0_xattn_Wo': _L0_xattn_in['Wo'], 'L0_xattn_ln_gamma': _L0_xattn_in['ln_gamma'], 'L0_xattn_ln_beta': _L0_xattn_in['ln_beta'], 'L0_ffn_Wg': _L0_ffn_in['Wg'], 'L0_ffn_W1': _L0_ffn_in['W1'], 'L0_ffn_b1': _L0_ffn_in['b1'], 'L0_ffn_W2': _L0_ffn_in['W2'], 'L0_ffn_b2': _L0_ffn_in['b2']}

def reference(x, ctx_1024, L0_attn_W_xproj, L0_attn_W_dt, L0_attn_b_dt, L0_attn_A_log, L0_xattn_Wq, L0_xattn_Wk, L0_xattn_Wv, L0_xattn_Wo, L0_xattn_ln_gamma, L0_xattn_ln_beta, L0_ffn_Wg, L0_ffn_W1, L0_ffn_b1, L0_ffn_W2, L0_ffn_b2):
    import jax
    import jax.numpy as jnp

    def _L0_attn_ref(hidden_states, W_xproj, W_dt, b_dt, A_log):
        import jax, jax.numpy as jnp
        import numpy as np
        import math
        D_MODEL = 256
        D_STATE = 16
        DT_RANK = 64
        DT_MIN, DT_MAX = (0.001, 0.1)

        def _selective_scan(x, delta, A, Bm, Cm):
            b, l, d = x.shape
            n = A.shape[1]
            dA = jnp.exp(delta[..., None] * A)
            dBx = (delta * x)[..., None] * Bm[:, :, None, :]

            def step(h, inp):
                dA_t, dBx_t, C_t = inp
                h = dA_t * h + dBx_t
                y = jnp.einsum('bdn,bn->bd', h, C_t)
                return (h, y)
            h0 = jnp.zeros((b, d, n), dtype=x.dtype)
            _, ys = jax.lax.scan(step, h0, (jnp.swapaxes(dA, 0, 1), jnp.swapaxes(dBx, 0, 1), jnp.swapaxes(Cm, 0, 1)))
            return jnp.swapaxes(ys, 0, 1)
        A = -jnp.exp(A_log)
        x_dbl = jnp.einsum('bld,ed->ble', hidden_states, W_xproj)
        dt_low = x_dbl[..., :DT_RANK]
        Bm = x_dbl[..., DT_RANK:DT_RANK + D_STATE]
        Cm = x_dbl[..., DT_RANK + D_STATE:]
        delta = jax.nn.softplus(jnp.einsum('blr,dr->bld', dt_low, W_dt) + b_dt)
        return _selective_scan(hidden_states, delta, A, Bm, Cm)

    def _L0_xattn_ref(query, key, value, Wq, Wk, Wv, Wo, ln_gamma, ln_beta):
        import jax, jax.numpy as jnp
        import numpy as np
        D_MODEL = 256
        NUM_HEADS = 16
        D_K = D_MODEL // NUM_HEADS
        LN_EPS = 1e-05

        def _layernorm(x, gamma, beta):
            mu = jnp.mean(x, axis=-1, keepdims=True)
            var = jnp.var(x, axis=-1, keepdims=True)
            return (x - mu) * jax.lax.rsqrt(var + LN_EPS) * gamma + beta
        B, S, _ = query.shape
        Q = query @ Wq.T
        K = key @ Wk.T
        V = value @ Wv.T
        Q = _layernorm(Q, ln_gamma, ln_beta)
        K = _layernorm(K, ln_gamma, ln_beta)
        Q = Q.reshape(B, S, NUM_HEADS, D_K).transpose(0, 2, 1, 3)
        K = K.reshape(B, S, NUM_HEADS, D_K).transpose(0, 2, 1, 3)
        V = V.reshape(B, S, NUM_HEADS, D_K).transpose(0, 2, 1, 3)
        scores = jnp.einsum('bhqd,bhkd->bhqk', Q, K) / np.sqrt(D_K).astype(np.float32)
        attn = jax.nn.softmax(scores, axis=-1)
        context = jnp.einsum('bhqk,bhkd->bhqd', attn, V)
        context = context.transpose(0, 2, 1, 3).reshape(B, S, D_MODEL)
        return context @ Wo.T

    def _L0_ffn_ref(x, Wg, W1, b1, W2, b2):
        import jax, jax.numpy as jnp
        import numpy as np
        B, L, H, E, FF, C = (4, 512, 256, 8, 1024, 2)
        b, l, h = x.shape
        e = Wg.shape[1]
        n = b * l
        k = min(max(int(n * C / e), 1), n)
        xt = x.reshape(n, h)
        S = jax.nn.sigmoid(xt @ Wg).T
        G, I = jax.lax.top_k(S, k)
        ex = xt[I]
        hid = jax.nn.gelu(jnp.einsum('ekh,ehf->ekf', ex, W1) + b1[:, None, :], approximate=False)
        out = (jnp.einsum('ekf,efh->ekh', hid, W2) + b2[:, None, :]) * G[..., None]
        new_x = jnp.zeros_like(xt).at[I.reshape(-1)].add(out.reshape(-1, h))
        return new_x.reshape(b, l, h)
    x = _layernorm(x + _L0_attn_ref(x, L0_attn_W_xproj, L0_attn_W_dt, L0_attn_b_dt, L0_attn_A_log), axis=-1)
    x = _layernorm(x + _L0_xattn_ref(x, ctx_1024, ctx_1024, L0_xattn_Wq, L0_xattn_Wk, L0_xattn_Wv, L0_xattn_Wo, L0_xattn_ln_gamma, L0_xattn_ln_beta), axis=-1)
    x = _layernorm(x + _L0_ffn_ref(x, L0_ffn_Wg, L0_ffn_W1, L0_ffn_b1, L0_ffn_W2, L0_ffn_b2), axis=-1)
    return x

_drawn_inputs = setup_inputs


def setup_inputs(seed=0):
    import zlib

    import numpy as np

    out = dict(_drawn_inputs(seed))
    spreads = {'L0_xattn_ln_gamma': (1.0, 0.2),
     'L0_xattn_ln_beta': (0.0, 0.347),
     'L0_ffn_b1': (0.0, 0.1),
     'L0_ffn_b2': (0.0, 0.1)}
    factors = {}
    for name, (base, spread) in spreads.items():
        noise = np.random.default_rng([zlib.crc32(name.encode()), seed]).standard_normal(out[name].shape)
        drawn = base * np.exp(spread * noise) if base else spread * noise
        out[name] = jnp.asarray(drawn.astype(out[name].dtype))
    for name, factor in factors.items():
        out[name] = (out[name] * factor).astype(out[name].dtype)
    return out
```

```python
from contextlib import ExitStack

import numpy as np

import concourse.bass as bass
from concourse import mybir

F32 = mybir.dt.float32
BF16 = mybir.dt.bfloat16
I32 = mybir.dt.int32
ALU = mybir.AluOpType
ACT = mybir.ActivationFunctionType
AX = mybir.AxisListType
ds = bass.ds

P = 128
BATCH, SEQ, D = 32, 128, 256
T = BATCH * SEQ
KH = D // P
NT = T // P
NS, R = 16, 64
HEADS, DK = 16, 16
EXPERTS, FF = 8, 1024
TOPK = min(max(int(T * 2 / EXPERTS), 1), T)
EPS = 1e-5
ROW = D + EXPERTS

GB = 4
GT = GB * SEQ
GROUPS = T // GT
RING = 4
STEPS = NS


def merge_moments(dve, stats, stats_ready, stats_count, part, mean, var, done, before):
    even, odd = stats[:, :, 1], stats[:, :, 4]
    dve.wait_ge(stats_ready, stats_count)
    dve.tensor_tensor(part[:, 0, :], even, odd, ALU.add)
    dve.tensor_tensor(part[:, 1, :], even, odd, ALU.subtract)
    dve.tensor_tensor(part[:, 2, :], stats[:, :, 2], stats[:, :, 5], ALU.add).then_inc(done, 1)
    dve.wait_ge(done, 3 * before + 1)
    dve.tensor_scalar(mean[:], part[:, 0, :], 0.5, None, ALU.mult)
    dve.scalar_tensor_tensor(part[:, 3, :], part[:, 1, :], 0.25, part[:, 1, :], ALU.mult, ALU.mult).then_inc(done, 1)
    dve.wait_ge(done, 3 * before + 2)
    dve.scalar_tensor_tensor(var[:], part[:, 2, :], 1.0 / D, part[:, 3, :], ALU.mult, ALU.add).then_inc(done, 1)


class Scope:

    def __init__(self, nc, ctx, tag):
        self.nc, self.ctx, self.tag = nc, ctx, tag

    def sb(self, name, shape, dt=F32):
        return self.ctx.enter_context(self.nc.sbuf_tensor(f"{self.tag}_{name}", shape, dt))

    def ps(self, name, shape, dt=F32):
        return self.ctx.enter_context(self.nc.psum_tensor(f"{self.tag}_{name}_ps", shape, dt))

    def sem(self, name):
        return self.ctx.enter_context(self.nc.semaphore(f"{self.tag}_{name}"))


def scan_phase(nc, x1, ident, xT_dram, w_proj_dram, w_bc_dram, w_dt_dram, b_dt_dram, a_log_dram, sel_dram):
    with ExitStack() as ctx:
        s = Scope(nc, ctx, "scan")
        w_proj = s.sb("w_proj", [P, KH, R])
        w_bc = s.sb("w_bc", [P, KH, 96])
        w_dt = s.sb("w_dt", [R, D])
        b_dt = s.sb("b_dt", [P, KH])
        a_log = s.sb("a_log", [P, KH, NS])
        a_exp = s.sb("a_exp", [P, KH, NS])
        a_neg = s.sb("a_neg", [P, KH, NS])
        sel = s.sb("sel", [96, 2 * NS, P], BF16)
        xT = [s.sb(f"xT{i}", [P, KH, GT]) for i in range(2)]
        bcs = [s.sb(f"bcs{i}", [96, GT], BF16) for i in range(2)]
        bc_rest = s.sb("bc_rest", [96, GT])
        bc_mid = s.sb("bc_mid", [96, GT], BF16)
        dt_low = s.sb("dt_low", [R, GT])
        z_abs = s.sb("z_abs", [P, KH, GT])
        z_exp = s.sb("z_exp", [P, KH, GT])
        z_log = s.sb("z_log", [P, KH, GT])
        z_pos = s.sb("z_pos", [P, KH, GT])
        delta = [s.sb(f"delta{i}", [P, KH, GB, SEQ]) for i in range(2)]
        dx = [s.sb(f"dx{i}", [P, KH, GT]) for i in range(2)]
        decay = s.sb("decay", [P, RING, KH, GB, SEQ])
        drive = s.sb("drive", [P, RING, KH, GT])
        state = s.sb("state", [P, RING, KH, GT])
        c_sb = s.sb("c_sb", [P, RING, GT])
        hc = s.sb("hc", [P, RING, KH, GT])
        yT = s.sb("yT", [P, KH, GT])
        stats = s.sb("stats", [P, GB, 6])
        moment = s.sb("moment", [P, 4, GB])
        mean = s.sb("mean", [P, GB])
        var = s.sb("var", [P, GB])
        ln_var = s.sb("ln_var", [P, GB])
        rstd = s.sb("rstd", [P, GB])
        eps = s.sb("eps", [P, 1])

        b_ps = [s.ps(f"b{i}", [P, 512]) for i in range(2)]
        c_ps = [s.ps(f"c{i}", [P, 512]) for i in range(2)]
        y_ps = [s.ps(f"y{i}", [P, 512]) for i in range(KH)]
        m_ps = [s.ps(f"m{i}", [P, 512]) for i in range(2)]

        const_loaded = s.sem("const_loaded")
        x_loaded = [s.sem(f"x_loaded{i}") for i in range(2)]
        zeroed = s.sem("zeroed")
        a_ready = s.sem("a_ready")
        proj_ready = s.sem("proj_ready")
        dt_copied = s.sem("dt_copied")
        bc_high = s.sem("bc_high")
        bc_step = s.sem("bc_step")
        bcs_ready = s.sem("bcs_ready")
        z_ready = s.sem("z_ready")
        z_abs_ready = s.sem("z_abs_ready")
        z_exp_ready = s.sem("z_exp_ready")
        z_log_ready = s.sem("z_log_ready")
        z_pos_ready = s.sem("z_pos_ready")
        delta_ready = s.sem("delta_ready")
        dx_ready = s.sem("dx_ready")
        decay_ready = s.sem("decay_ready")
        b_ready = s.sem("b_ready")
        c_ready = s.sem("c_ready")
        c_copied = s.sem("c_copied")
        drive_ready = s.sem("drive_ready")
        scanned = s.sem("scanned")
        hc_ready = s.sem("hc_ready")
        hc_summed = s.sem("hc_summed")
        y_started = s.sem("y_started")
        y_copied = s.sem("y_copied")
        turned = s.sem("turned")
        stats_ready = s.sem("stats_ready")
        mv_ready = s.sem("mv_ready")
        lv_ready = s.sem("lv_ready")
        rstd_ready = s.sem("rstd_ready")
        normed = s.sem("normed")
        consts = 7

        with nc.Block() as block:

            @block.sync
            def _(sp):
                sp.dma_start(w_proj[:], w_proj_dram).then_inc(const_loaded, 16)
                sp.dma_start(w_bc[:], w_bc_dram).then_inc(const_loaded, 16)
                sp.dma_start(xT[0][:], xT_dram[:, :, 0:GT]).then_inc(x_loaded[0], 16)
                sp.dma_start(w_dt[:], w_dt_dram).then_inc(const_loaded, 16)
                sp.dma_start(b_dt[:], b_dt_dram).then_inc(const_loaded, 16)
                sp.dma_start(a_log[:], a_log_dram).then_inc(const_loaded, 16)
                sp.dma_start(sel[:], sel_dram).then_inc(const_loaded, 16)
                sp.dma_start(ident[0][:], ident[1]).then_inc(const_loaded, 16)
                sp.dma_start(xT[1][:], xT_dram[:, :, GT:2 * GT]).then_inc(x_loaded[1], 16)
                with sp.Fori(1, GROUPS // 2) as i:
                    for par in range(2):
                        g = 2 * i + par
                        sp.wait_ge(y_started, g - 1)
                        sp.wait_ge(dx_ready, g - 1)
                        sp.dma_start(xT[par][:], xT_dram[:, :, ds(g * GT, GT)]).then_inc(x_loaded[par], 16)

            @block.tensor
            def _(pe):
                def project(i, par, first=False):
                    g = 2 * i + par
                    pe.wait_ge(x_loaded[par], 16 * (i + 1))
                    if not first:
                        pe.wait_ge(normed, g + 1)
                    for k in range(KH):
                        pe.matmul(m_ps[0][0:R, :], w_proj[:, k, :], xT[par][:, k, :], start=(k == 0), stop=(k == KH - 1))
                    for k in range(KH):
                        last = pe.matmul(m_ps[1][0:96, :], w_bc[:, k, :], xT[par][:, k, :], start=(k == 0), stop=(k == KH - 1))
                    last.then_inc(proj_ready, 1)

                def step_size(i, par):
                    g = 2 * i + par
                    pe.wait_ge(dt_copied, g + 1)
                    pe.wait_ge(bc_high, g + 1)
                    pe.wait_ge(bc_step, 5 * g + 1)
                    for k in range(KH):
                        last = pe.matmul(m_ps[k][:], w_dt[:, k * P:(k + 1) * P], dt_low[:], start=True, stop=True)
                    last.then_inc(z_ready, 1)

                def broadcast(i, par, n):
                    g = 2 * i + par
                    q = STEPS * g + n
                    if n == 0:
                        pe.wait_ge(bcs_ready, g + 1)
                    pe.wait_ge(drive_ready, q + 1)
                    pe.matmul(b_ps[n % 2][:], sel[:, n, :], bcs[par][:], start=True, stop=True).then_inc(b_ready, 1)
                    pe.wait_ge(c_copied, q + 1)
                    mm = pe.matmul(c_ps[n % 2][:], sel[:, NS + n, :], bcs[par][:], start=True, stop=True)
                    mm.then_inc(c_ready, 1)

                def add_state(q, n):
                    pe.wait_ge(hc_ready, q + 2)
                    for k in range(KH):
                        last = pe.matmul(y_ps[k][:], ident[0][:], hc[:, n % RING, k, :], start=False, stop=(n == NS - 1))
                    last.then_inc(hc_summed, 1)

                def start_y(i, par):
                    g = 2 * i + par
                    pe.wait_ge(y_copied, g + 1)
                    for k in range(KH):
                        last = pe.matmul(y_ps[k][:], ident[0][:], xT[par][:, k, :], start=True, stop=False)
                    last.then_inc(y_started, 1)

                def turn(g):
                    pe.wait_ge(y_copied, g + 1)
                    pe.wait_ge(z_abs_ready, 2 * (g + 1))
                    pe.wait_ge(z_pos_ready, 2 * (g + 1))
                    for j in range(GB):
                        for k in range(KH):
                            c = (j % 2) * D + k * P
                            last = pe.transpose(m_ps[j // 2][:, c:c + P], yT[:, k, j * P:(j + 1) * P], ident[0][:])
                    last.then_inc(turned, 1)

                def group(i, par, final=False):
                    g = 2 * i + par
                    for n in range(STEPS):
                        if n + 2 < STEPS:
                            broadcast(i, par, n + 2)
                        elif not final:
                            broadcast(i + par, 1 - par, n + 2 - STEPS)
                        add_state(STEPS * g + n - 1, (n - 1) % STEPS)
                        if n == 0:
                            start_y(i, par)
                        if n == 1:
                            turn(g)
                        if not final:
                            if n == 5:
                                project(i + par, 1 - par)
                            if n == 7:
                                step_size(i + par, 1 - par)

                pe.sem_inc(c_ready, 1)
                pe.wait_ge(const_loaded, 16 * consts)
                project(0, 0, first=True)
                pe.wait_ge(zeroed, 3)
                for k in range(KH):
                    pe.matmul(y_ps[k][:], ident[0][:], hc[:, RING - 1, k, :], start=True, stop=False)
                step_size(0, 0)
                broadcast(0, 0, 0)
                broadcast(0, 0, 1)
                with pe.Fori(0, GROUPS // 2 - 1) as i:
                    group(i, 0)
                    group(i, 1)
                group(GROUPS // 2 - 1, 0)
                group(GROUPS // 2 - 1, 1, final=True)
                add_state(STEPS * GROUPS - 1, NS - 1)
                turn_last = GROUPS
                pe.wait_ge(y_copied, turn_last + 1)
                for j in range(GB):
                    for k in range(KH):
                        c = (j % 2) * D + k * P
                        last = pe.transpose(m_ps[j // 2][:, c:c + P], yT[:, k, j * P:(j + 1) * P], ident[0][:])
                last.then_inc(turned, 1)

            @block.scalar
            def _(act):
                nc.scalar.preload_act_table_set("natural_log_exp_and_others")

                def copy_low(g):
                    act.wait_ge(proj_ready, g + 1)
                    act.activation(dt_low[:], m_ps[0][0:R, :], ACT.Copy).then_inc(dt_copied, 1)

                def high_part(i, par, first=False):
                    g = 2 * i + par
                    if not first:
                        act.wait_ge(c_ready, STEPS * (g - 1) + 1)
                    act.activation(bcs[par][:], m_ps[1][0:96, :], ACT.Copy).then_inc(bc_high, 1)

                def softplus_abs(g, first=False):
                    act.wait_ge(z_ready, g + 1)
                    if not first:
                        act.wait_ge(z_log_ready, g)
                    for k in range(KH):
                        act.activation(z_abs[:, k, :], m_ps[k][:], ACT.Abs, bias=b_dt[:, k:k + 1]).then_inc(z_abs_ready, 1)

                def softplus_exp(g):
                    act.wait_ge(z_abs_ready, 2 * (g + 1))
                    act.activation(z_exp[:], z_abs[:], ACT.Exp, scale=-1.0).then_inc(z_exp_ready, 1)

                def softplus_log(g, first=False):
                    act.wait_ge(z_exp_ready, g + 1)
                    if not first:
                        act.wait_ge(delta_ready, g)
                    act.activation(z_log[:], z_exp[:], ACT.Ln, bias=1.0).then_inc(z_log_ready, 1)

                def decays(par, q, n):
                    act.wait_ge(scanned, q + 1)
                    for k in range(KH):
                        act.activation(decay[:, n % RING, k, :, 1:SEQ], delta[par][:, k, :, 1:SEQ], ACT.Exp,
                                       scale=a_neg[:, k, n:n + 1]).then_inc(decay_ready, 1)

                def copy_y(g):
                    act.wait_ge(hc_summed, STEPS * g + 4)
                    act.wait_ge(turned, g)
                    act.activation(yT[:, 0, :], y_ps[0][:], ACT.Copy)
                    act.activation(yT[:, 1, :], y_ps[1][:], ACT.Copy).then_inc(y_copied, 1)

                def inv_std(g):
                    act.wait_ge(mv_ready, 3 * (g + 1))
                    act.wait_ge(normed, g + 1)
                    act.activation(ln_var[:], var[:], ACT.Ln, bias=eps[:, 0:1]).then_inc(lv_ready, 1)
                    act.wait_ge(lv_ready, g + 1)
                    act.activation(rstd[:], ln_var[:], ACT.Exp, scale=-0.5).then_inc(rstd_ready, 1)

                def group(i, par, final=False):
                    g = 2 * i + par
                    for n in range(STEPS):
                        q = STEPS * g + n
                        if n == 0:
                            act.wait_ge(delta_ready, g + 1)
                        decays(par, q, n)
                        if n == 2:
                            copy_y(g)
                        act.wait_ge(c_ready, q + 2)
                        act.wait_ge(hc_ready, q + 1)
                        act.activation(c_sb[:, n % RING, :], c_ps[n % 2][:], ACT.Copy).then_inc(c_copied, 1)
                        if n == 4:
                            inv_std(g)
                        if not final:
                            if n == 6:
                                copy_low(g + 1)
                                high_part(i + par, 1 - par)
                            if n == 8:
                                softplus_abs(g + 1)
                            if n == 9:
                                softplus_exp(g + 1)
                            if n == 10:
                                softplus_log(g + 1)

                act.sem_inc(c_copied, 2)
                act.sem_inc(turned, 1)
                act.sem_inc(normed, 1)
                act.wait_ge(const_loaded, 16 * consts)
                act.activation(a_exp[:], a_log[:], ACT.Exp).then_inc(a_ready, 1)
                copy_low(0)
                high_part(0, 0, first=True)
                softplus_abs(0, first=True)
                softplus_exp(0)
                softplus_log(0, first=True)
                act.wait_ge(a_ready, 2)
                act.wait_ge(zeroed, 3)
                with act.Fori(0, GROUPS // 2 - 1) as i:
                    group(i, 0)
                    group(i, 1)
                group(GROUPS // 2 - 1, 0)
                group(GROUPS // 2 - 1, 1, final=True)
                copy_y(GROUPS)
                inv_std(GROUPS)

            @block.vector
            def _(dve):
                def split(i, par):
                    g = 2 * i + par
                    dve.wait_ge(bc_high, g + 1)
                    dve.tensor_tensor(bc_rest[:], m_ps[1][0:96, :], bcs[par][:], ALU.subtract).then_inc(bc_step, 1)
                    dve.wait_ge(bc_step, 5 * g + 1)
                    dve.tensor_copy(bcs[par][32:64, :], bc_rest[32:64, :]).then_inc(bc_step, 1)
                    dve.tensor_copy(bc_mid[64:96, :], bc_rest[64:96, :]).then_inc(bc_step, 1)
                    dve.wait_ge(bc_step, 5 * g + 3)
                    dve.tensor_tensor(bcs[par][64:96, :], bc_rest[64:96, :], bc_mid[64:96, :], ALU.subtract).then_inc(bc_step, 1)
                    dve.wait_ge(bc_step, 5 * g + 4)
                    dve.sem_inc(bc_step, 1)
                    dve.sem_inc(bcs_ready, 1)

                def softplus_pos(g, first=False):
                    dve.wait_ge(z_abs_ready, 2 * (g + 1))
                    if not first:
                        dve.wait_ge(delta_ready, g)
                    for k in range(KH):
                        dve.tensor_scalar(z_pos[:, k, :], m_ps[k][:], b_dt[:, k:k + 1], 0.0, ALU.add, ALU.max).then_inc(z_pos_ready, 1)

                def drives(i, par, n):
                    g = 2 * i + par
                    q = STEPS * g + n
                    if n == 0:
                        dve.wait_ge(dx_ready, g + 1)
                    dve.wait_ge(b_ready, q + 1)
                    dve.wait_ge(scanned, q + 1)
                    dve.tensor_tensor(drive[:, n % RING, :, :], dx[par][:],
                                      b_ps[n % 2][:].unsqueeze(1).broadcast_to([P, KH, GT]), ALU.mult).then_inc(drive_ready, 1)

                def scan(q, n):
                    dve.wait_ge(drive_ready, q + 3)
                    dve.wait_ge(decay_ready, KH * (q + 1) + KH)
                    dve.wait_ge(hc_ready, q + 1)
                    dve.tensor_tensor_scan(state[:, n % RING, :, :].rearrange("p k t -> p (k t)"),
                                           decay[:, n % RING, :, :, :].rearrange("p k b t -> p (k b t)"),
                                           drive[:, n % RING, :, :].rearrange("p k t -> p (k t)"),
                                           0.0, ALU.mult, ALU.add).then_inc(scanned, 1)

                def statistics(g):
                    dve.wait_ge(turned, g + 2)
                    for j in range(GB):
                        last = dve.bn_stats(stats[:, j, :], m_ps[j // 2][:, (j % 2) * D:(j % 2 + 1) * D])
                    last.then_inc(stats_ready, 1)
                    merge_moments(dve, stats, stats_ready, g + 1, moment, mean, var, mv_ready, g)

                def normalise(g):
                    dve.wait_ge(rstd_ready, g + 1)
                    for j in range(GB):
                        last = dve.tensor_scalar(x1[:, ds(GB * g + j, 1), :].rearrange("p o d -> p (o d)"),
                                                 m_ps[j // 2][:, (j % 2) * D:(j % 2 + 1) * D],
                                                 mean[:, j:j + 1], rstd[:, j:j + 1], ALU.subtract, ALU.mult)
                    last.then_inc(normed, 1)

                def group(i, par, final=False):
                    g = 2 * i + par
                    for n in range(STEPS):
                        q = STEPS * g + n
                        if n + 1 < STEPS:
                            drives(i, par, n + 1)
                        elif not final:
                            drives(i + par, 1 - par, 0)
                        scan(q, n)
                        if n == 3:
                            statistics(g)
                        if n == 4:
                            normalise(g)
                        if not final:
                            if n == 6:
                                split(i + par, 1 - par)
                            if n == 8:
                                softplus_pos(g + 1)

                dve.sem_inc(drive_ready, 2)
                dve.sem_inc(scanned, RING)
                dve.memset(decay[:].rearrange("p r k b t -> p (r k b) t")[:, :, 0], 0.0).then_inc(zeroed, 1)
                dve.memset(eps[:], EPS).then_inc(zeroed, 1)
                dve.wait_ge(a_ready, 1)
                dve.tensor_scalar(a_neg[:], a_exp[:], -1.0, None, ALU.mult).then_inc(a_ready, 1)
                split(0, 0)
                softplus_pos(0, first=True)
                drives(0, 0, 0)
                with dve.Fori(0, GROUPS // 2 - 1) as i:
                    group(i, 0)
                    group(i, 1)
                group(GROUPS // 2 - 1, 0)
                group(GROUPS // 2 - 1, 1, final=True)
                statistics(GROUPS)
                normalise(GROUPS)

            @block.gpsimd
            def _(pool):
                def step_sizes(i, par, first=False):
                    g = 2 * i + par
                    pool.wait_ge(z_log_ready, g + 1)
                    pool.wait_ge(z_pos_ready, 2 * (g + 1))
                    if not first:
                        pool.wait_ge(decay_ready, KH * STEPS * (g - 1) + KH)
                    pool.tensor_tensor(delta[par][:].rearrange("p k b t -> p k (b t)"), z_log[:], z_pos[:], ALU.add).then_inc(delta_ready, 1)

                def step_inputs(i, par, first=False):
                    g = 2 * i + par
                    pool.wait_ge(delta_ready, g + 1)
                    if not first:
                        pool.wait_ge(drive_ready, STEPS * (g - 1) + 2)
                    pool.tensor_tensor(dx[par][:], delta[par][:].rearrange("p k b t -> p k (b t)"), xT[par][:], ALU.mult).then_inc(dx_ready, 1)

                def outputs(q, n):
                    pool.wait_ge(c_copied, q + 3)
                    pool.wait_ge(scanned, q + 1 + RING)
                    pool.wait_ge(hc_summed, q + 1)
                    pool.tensor_tensor(hc[:, n % RING, :, :], state[:, n % RING, :, :],
                                       c_sb[:, n % RING, :].unsqueeze(1).broadcast_to([P, KH, GT]), ALU.mult).then_inc(hc_ready, 1)

                def group(i, par, final=False):
                    g = 2 * i + par
                    for n in range(STEPS):
                        outputs(STEPS * g + n, n)
                        if not final:
                            if n == 10:
                                step_sizes(i + par, 1 - par)
                            if n == 11:
                                step_inputs(i + par, 1 - par)

                pool.sem_inc(hc_summed, 3)
                pool.sem_inc(decay_ready, 2)
                pool.memset(hc[:, RING - 1, :, :], 0.0).then_inc(zeroed, 1)
                pool.wait_ge(zeroed, 3)
                pool.sem_inc(hc_ready, 1)
                step_sizes(0, 0, first=True)
                step_inputs(0, 0, first=True)
                with pool.Fori(0, GROUPS // 2 - 1) as i:
                    group(i, 0)
                    group(i, 1)
                group(GROUPS // 2 - 1, 0)
                group(GROUPS // 2 - 1, 1, final=True)


class Seq:

    def __init__(self, pair, offset):
        self.pair, self.offset = pair, offset
        self.parity = offset % 2
        self.half = pair + offset // 2
        self.b = 2 * pair + offset

    def plus(self, n):
        return Seq(self.pair, self.offset + n)


def since(eng, sem, count):
    if not (isinstance(count, int) and count < 1):
        eng.wait_ge(sem, count)


def attention_phase(nc, x1, ident, gate_all, ctxT_dram, w_q_dram, w_kv_dram, w_o_dram, w_g_dram, norm_dram,
                    even_odd_dram, pick_dram, table_dram, acc_dram):
    with ExitStack() as ctx:
        s = Scope(nc, ctx, "attn")
        w_q = s.sb("w_q", [P, KH, D])
        w_kv = s.sb("w_kv", [P, KH, 2 * D])
        w_o = s.sb("w_o", [P, KH, D])
        w_g = s.sb("w_g", [P, KH, EXPERTS])
        norm = s.sb("norm", [P, 2, KH])
        even_odd = s.sb("even_odd", [P, 2])
        affine = s.sb("affine", [P, 2, 2, KH])
        pick = s.sb("pick", [P, 4, P], BF16)
        eps = s.sb("eps", [P, 1])
        x1b = [s.sb(f"x1b{i}", [P, D]) for i in range(2)]
        x1T = s.sb("x1T", [P, KH, P])
        ctxT = [s.sb(f"ctxT{i}", [P, KH, P]) for i in range(2)]
        qk_stats = s.sb("qk_stats", [P, 2, 6])
        qk_part = s.sb("qk_part", [P, 4, 2])
        qk_mean = s.sb("qk_mean", [P, 2])
        qk_var = s.sb("qk_var", [P, 2])
        qk_lnv = s.sb("qk_lnv", [P, 2])
        qk_rstd = s.sb("qk_rstd", [P, 2])
        qkn = s.sb("qkn", [P, 2, D])
        qT = [s.sb(f"qT{i}", [P, KH, 2, P]) for i in range(2)]
        kT = [s.sb(f"kT{i}", [P, KH, P]) for i in range(2)]
        v1 = [s.sb(f"v1{i}", [P, HEADS, DK + 1]) for i in range(2)]
        top = s.sb("top", [P, HEADS])
        neg_top = s.sb("neg_top", [P, 4, 32], BF16)
        ntT = s.sb("ntT", [P, P], BF16)
        prob = [s.sb(f"prob{i}", [P, HEADS, P]) for i in range(2)]
        inv_sum = s.sb("inv_sum", [P, HEADS])
        mix = s.sb("mix", [P, HEADS, DK])
        mixT = s.sb("mixT", [P, KH, P])
        res = s.sb("res", [P, D])
        o_stats = s.sb("o_stats", [P, 1, 6])
        o_part = s.sb("o_part", [P, 4, 1])
        o_mean = s.sb("o_mean", [P, 1])
        o_var = s.sb("o_var", [P, 1])
        o_lnv = s.sb("o_lnv", [P, 1])
        o_rstd = s.sb("o_rstd", [P, 1])
        row = [s.sb(f"row{i}", [P, ROW]) for i in range(2)]
        x2T = s.sb("x2T", [P, KH, P])
        g_exp = s.sb("g_exp", [P, EXPERTS])
        g_den = s.sb("g_den", [P, EXPERTS])
        ident_bf = s.sb("ident_bf", [P, P], BF16)

        turn_ps = s.ps("turn", [P, 512])
        q_ps = s.ps("q", [P, D])
        kv_ps = s.ps("kv", [P, 2 * D])
        s_ps = [s.ps(f"s{i}", [P, 512]) for i in range(2)]
        st_ps = [s.ps(f"st{i}", [P, 512]) for i in range(2)]
        o_ps = s.ps("o", [P, 512])

        names = ("const_loaded set_up affine_ready x1b_ready x1_turned x1T_ready q_ready kv_ready qk_stats_ready qk_moments "
                 "qk_rstd_ready qk_lnv_ready v_ready qkn_ready qkn_turned qk_ready s_ready top_done neg_ready nt_turned nt_ready "
                 "st_ready exp_done pv_done inv_ready mix_ready mix_turned mixT_ready o_ready res_ready o_stats_ready o_moments "
                 "o_lnv_ready o_rstd_ready x2_ready x2_turned x2T_ready g_ready g_exp_ready g_den_ready gate_ready").split()
        m = {n: s.sem(n) for n in names}
        ctx_loaded = [s.sem(f"ctx_loaded{i}") for i in range(2)]
        row_stored = [s.sem(f"row_stored{i}") for i in range(2)]
        consts = 7
        LOOPED = (NT - 4) // 2

        def passes(eng, step):
            step(Seq(0, -1), True, False, False)
            step(Seq(0, 0), True, True, False)
            step(Seq(0, 1), True, True, True)
            with eng.Fori(0, LOOPED) as i:
                step(Seq(i, 2), True, True, True)
                step(Seq(i, 3), True, True, True)
            step(Seq(0, NT - 2), True, True, True)
            step(Seq(0, NT - 1), False, True, True)
            step(Seq(0, NT), False, False, True)

        with nc.Block() as block:

            @block.sync
            def _(sp):
                for sbuf, dram in ((w_q, w_q_dram), (w_kv, w_kv_dram), (w_o, w_o_dram), (w_g, w_g_dram),
                                   (norm, norm_dram), (even_odd, even_odd_dram), (pick, pick_dram)):
                    sp.dma_start(sbuf[:], dram).then_inc(m["const_loaded"], 16)

                def load_ctx(q):
                    since(sp, m["kv_ready"], q.b - 1)
                    sp.dma_start(ctxT[q.parity][:], ctxT_dram[:, :, ds(q.b * SEQ, SEQ)]).then_inc(ctx_loaded[q.parity], 16)

                def store(q):
                    sp.wait_ge(m["gate_ready"], q.b + 1)
                    sp.dma_start(table_dram[ds(q.b * SEQ, SEQ), :], row[q.parity][:]).then_inc(row_stored[q.parity], 16)
                    sp.dma_start(acc_dram[ds(q.b * SEQ, SEQ), :], row[q.parity][:, 0:D]).then_inc(row_stored[q.parity], 16)

                def step(q, a, b, c):
                    if a:
                        load_ctx(q.plus(1))
                    if c:
                        store(q.plus(-1))

                passes(sp, step)
                for r in row_stored:
                    sp.wait_ge(r, 32 * (NT // 2))

            @block.gpsimd
            def _(pool):
                for i in range(2):
                    pool.memset(v1[i][:], 1.0).then_inc(m["set_up"], 1)
                pool.memset(eps[:], EPS).then_inc(m["set_up"], 1)
                pool.memset(neg_top[:], 0.0).then_inc(m["set_up"], 1)
                pool.tensor_copy(ident_bf[:], ident[:]).then_inc(m["set_up"], 1)

                def step(q, a, b, c):
                    if a:
                        n = q.plus(1)
                        since(pool, m["x1_turned"], n.b - 1)
                        pool.tensor_copy(x1b[n.parity][:], x1[:, ds(GB + n.b, 1), :].rearrange("p o d -> p (o d)")).then_inc(m["x1b_ready"], 1)

                passes(pool, step)

            @block.tensor
            def _(pe):
                def turn_x1(q):
                    pe.wait_ge(m["x1b_ready"], q.b + 1)
                    since(pe, m["qk_ready"], q.b)
                    for k in range(KH):
                        last = pe.transpose(turn_ps[:, k * P:(k + 1) * P], x1b[q.parity][:, k * P:(k + 1) * P], ident[:])
                    last.then_inc(m["x1_turned"], 1)

                def project(q):
                    pe.wait_ge(m["x1T_ready"], q.b + 1)
                    since(pe, m["qkn_ready"], q.b)
                    for k in range(KH):
                        last = pe.matmul(q_ps[:], x1T[:, k, :], w_q[:, k, :], start=(k == 0), stop=(k == KH - 1))
                    last.then_inc(m["q_ready"], 1)
                    pe.wait_ge(ctx_loaded[q.parity], 16 * (q.half + 1))
                    for k in range(KH):
                        last = pe.matmul(kv_ps[:], ctxT[q.parity][:, k, :], w_kv[:, k, :], start=(k == 0), stop=(k == KH - 1))
                    last.then_inc(m["kv_ready"], 1)

                def turn_qk(q):
                    pe.wait_ge(m["qkn_ready"], q.b + 1)
                    for i in range(2):
                        for k in range(KH):
                            c = (i * KH + k) * P
                            last = pe.transpose(turn_ps[:, c:c + P], qkn[:, i, k * P:(k + 1) * P], ident[:])
                    last.then_inc(m["qkn_turned"], 1)

                def scores(q, j):
                    if j == 0:
                        pe.wait_ge(m["qk_ready"], q.b + 1)
                        since(pe, m["nt_ready"], q.b)
                    since(pe, m["top_done"], 4 * q.b + j - 1)
                    rows = slice(32 * j, 32 * j + 32)
                    for k in range(KH):
                        for e in range(2):
                            c = (2 * k + e) * P
                            last = pe.matmul(s_ps[j % 2][:, c:c + P], qT[q.parity][rows, k, e, :], kT[q.parity][rows, k, :],
                                             start=True, stop=True)
                    last.then_inc(m["s_ready"], 1)

                def turn_top(q):
                    pe.wait_ge(m["neg_ready"], q.b + 1)
                    pe.transpose(s_ps[0][:, 0:P // 2].bitcast(BF16), neg_top[:].rearrange("p j h -> p (j h)"), ident_bf[:]).then_inc(m["nt_turned"], 1)

                def shifted_scores(q, j):
                    if j == 0:
                        pe.wait_ge(m["nt_ready"], q.b + 1)
                    since(pe, m["exp_done"], 4 * q.b + j - 1)
                    rows = slice(32 * j, 32 * j + 32)
                    for k in range(KH):
                        c = 2 * k * P
                        pe.matmul(st_ps[j % 2][:, c:c + 2 * P], kT[q.parity][rows, k, :], qT[q.parity][rows, k, :, :],
                                  start=True, stop=True, skip_group_check=True)
                        for e in range(2):
                            c = (2 * k + e) * P
                            last = pe.matmul(st_ps[j % 2][:, c:c + P], pick[rows, 2 * k + e, :], ntT[rows, :], start=False, stop=True,
                                             skip_group_check=True)
                    last.then_inc(m["st_ready"], 1)

                def mix_values(q, j):
                    if j == 0:
                        since(pe, m["g_exp_ready"], q.b)
                    pe.wait_ge(m["exp_done"], 4 * q.b + j + 1)
                    for k in range(KH):
                        for e in range(2):
                            h = 8 * k + 2 * j + e
                            last = pe.matmul(o_ps[:, h * (DK + 1):(h + 1) * (DK + 1)], prob[q.parity][:, 4 * j + 2 * k + e, :],
                                             v1[q.parity][:, h, :], start=True, stop=True)
                    if j == 3:
                        last.then_inc(m["pv_done"], 1)

                def turn_mix(q):
                    pe.wait_ge(m["mix_ready"], q.b + 1)
                    for k in range(KH):
                        last = pe.transpose(o_ps[:, k * P:(k + 1) * P], mix[:, 8 * k:8 * k + 8, :].rearrange("p h d -> p (h d)"), ident[:])
                    last.then_inc(m["mix_turned"], 1)

                def project_out(q):
                    pe.wait_ge(m["mixT_ready"], q.b + 1)
                    for k in range(KH):
                        last = pe.matmul(o_ps[:, D:2 * D], mixT[:, k, :], w_o[:, k, :], start=(k == 0), stop=(k == KH - 1))
                    last.then_inc(m["o_ready"], 1)

                def turn_x2(q):
                    pe.wait_ge(m["x2_ready"], q.b + 1)
                    for k in range(KH):
                        last = pe.transpose(o_ps[:, k * P:(k + 1) * P], row[q.parity][:, k * P:(k + 1) * P], ident[:])
                    last.then_inc(m["x2_turned"], 1)

                def gates(q):
                    pe.wait_ge(m["x2T_ready"], q.b + 1)
                    for k in range(KH):
                        last = pe.matmul(o_ps[:, D:D + EXPERTS], x2T[:, k, :], w_g[:, k, :], start=(k == 0), stop=(k == KH - 1))
                    last.then_inc(m["g_ready"], 1)

                def step(q, a, b, c):
                    n, p = q.plus(1), q.plus(-1)
                    if b:
                        scores(q, 0)
                        scores(q, 1)
                    if c:
                        turn_mix(p)
                    if b:
                        scores(q, 2)
                        scores(q, 3)
                    if a:
                        turn_x1(n)
                    if c:
                        project_out(p)
                    if a:
                        project(n)
                    if b:
                        turn_top(q)
                        shifted_scores(q, 0)
                        shifted_scores(q, 1)
                    if c:
                        turn_x2(p)
                    if b:
                        shifted_scores(q, 2)
                        shifted_scores(q, 3)
                    if c:
                        gates(p)
                    if a:
                        turn_qk(n)
                    if b:
                        for j in range(4):
                            mix_values(q, j)

                pe.wait_ge(m["const_loaded"], 16 * consts)
                pe.wait_ge(m["set_up"], 5)
                passes(pe, step)

            @block.scalar
            def _(act):
                nc.scalar.preload_act_table_set("natural_log_exp_and_others")

                def inv_std(q, var, moments, lnv, lnv_ready, rstd, rstd_ready):
                    act.wait_ge(moments, 3 * (q.b + 1))
                    act.activation(lnv[:], var[:], ACT.Ln, bias=eps[:, 0:1]).then_inc(lnv_ready, 1)
                    act.wait_ge(lnv_ready, q.b + 1)
                    act.activation(rstd[:], lnv[:], ACT.Exp, scale=-0.5).then_inc(rstd_ready, 1)

                def copy_turned(q, turned, bank, out, ready):
                    act.wait_ge(turned, q.b + 1)
                    act.activation(out[:].rearrange("p k t -> p (k t)"), bank[:, 0:KH * P], ACT.Copy).then_inc(ready, 1)

                def scale_qk(q):
                    act.wait_ge(m["qkn_turned"], q.b + 1)
                    for k in range(KH):
                        for e in range(2):
                            act.activation(qT[q.parity][:, k, e, :], turn_ps[:, k * P:(k + 1) * P], ACT.Identity,
                                           bias=affine[:, 1, e, k:k + 1], scale=affine[:, 0, e, k:k + 1])
                        c = (KH + k) * P
                        last = act.activation(kT[q.parity][:, k, :], turn_ps[:, c:c + P], ACT.Identity,
                                              bias=norm[:, 1, k:k + 1], scale=norm[:, 0, k:k + 1])
                    last.then_inc(m["qk_ready"], 1)

                def copy_top(q):
                    act.wait_ge(m["nt_turned"], q.b + 1)
                    act.activation(ntT[:], s_ps[0][:, 0:P // 2].bitcast(BF16), ACT.Copy).then_inc(m["nt_ready"], 1)

                def exps(q, j):
                    if j == 0:
                        since(act, m["pv_done"], q.b - 1)
                    act.wait_ge(m["st_ready"], 4 * q.b + j + 1)
                    act.activation(prob[q.parity][:, 4 * j:4 * j + 4, :].rearrange("p h q -> p (h q)"), st_ps[j % 2][:], ACT.Exp,
                                   scale=DK ** -0.5).then_inc(m["exp_done"], 1)

                def gate_exp(q):
                    act.wait_ge(m["g_ready"], q.b + 1)
                    since(act, m["g_den_ready"], q.b)
                    act.activation(g_exp[:], o_ps[:, D:D + EXPERTS], ACT.Exp, scale=-1.0).then_inc(m["g_exp_ready"], 1)

                def step(q, a, b, c):
                    n, p = q.plus(1), q.plus(-1)
                    if c:
                        copy_turned(p, m["mix_turned"], o_ps, mixT, m["mixT_ready"])
                    if a:
                        copy_turned(n, m["x1_turned"], turn_ps, x1T, m["x1T_ready"])
                    if b:
                        copy_top(q)
                    if c:
                        inv_std(p, o_var, m["o_moments"], o_lnv, m["o_lnv_ready"], o_rstd, m["o_rstd_ready"])
                    if b:
                        exps(q, 0)
                    if a:
                        inv_std(n, qk_var, m["qk_moments"], qk_lnv, m["qk_lnv_ready"], qk_rstd, m["qk_rstd_ready"])
                    if b:
                        exps(q, 1)
                    if c:
                        copy_turned(p, m["x2_turned"], o_ps, x2T, m["x2T_ready"])
                    if b:
                        exps(q, 2)
                        exps(q, 3)
                    if c:
                        gate_exp(p)
                    if a:
                        scale_qk(n)

                act.wait_ge(m["const_loaded"], 16 * consts)
                act.wait_ge(m["affine_ready"], 4)
                act.wait_ge(m["set_up"], 5)
                passes(act, step)

            @block.vector
            def _(dve):
                def moments(q):
                    since(dve, m["qk_rstd_ready"], q.b)
                    dve.wait_ge(m["q_ready"], q.b + 1)
                    dve.bn_stats(qk_stats[:, 0, :], q_ps[:])
                    dve.wait_ge(m["kv_ready"], q.b + 1)
                    dve.bn_stats(qk_stats[:, 1, :], kv_ps[:, 0:D]).then_inc(m["qk_stats_ready"], 1)
                    dve.tensor_copy(v1[q.parity][:, :, 0:DK], kv_ps[:, D:2 * D].rearrange("p (h d) -> p h d", d=DK)).then_inc(m["v_ready"], 1)
                    merge_moments(dve, qk_stats, m["qk_stats_ready"], q.b + 1, qk_part, qk_mean, qk_var, m["qk_moments"], q.b)

                def normalise_qk(q):
                    dve.wait_ge(m["qk_rstd_ready"], q.b + 1)
                    since(dve, m["qkn_turned"], q.b)
                    dve.tensor_scalar(qkn[:, 0, :], q_ps[:], qk_mean[:, 0:1], qk_rstd[:, 0:1], ALU.subtract, ALU.mult)
                    dve.tensor_scalar(qkn[:, 1, :], kv_ps[:, 0:D], qk_mean[:, 1:2], qk_rstd[:, 1:2], ALU.subtract,
                                      ALU.mult).then_inc(m["qkn_ready"], 1)

                def maximum(q, j):
                    dve.wait_ge(m["s_ready"], 4 * q.b + j + 1)
                    dve.tensor_reduce(top[:, 4 * j:4 * j + 4], s_ps[j % 2][:].rearrange("p (h k) -> p h k", k=P), AX.X,
                                      ALU.max).then_inc(m["top_done"], 1)

                def negate(q):
                    dve.wait_ge(m["top_done"], 4 * (q.b + 1))
                    dve.tensor_scalar(neg_top[:, :, 0:4], top[:].rearrange("p (j h) -> p j h", h=4), -1.0, None, ALU.mult).then_inc(m["neg_ready"], 1)

                def divide(q):
                    dve.wait_ge(m["pv_done"], q.b + 1)
                    pv = o_ps[:, 0:HEADS * (DK + 1)].rearrange("p (h d) -> p h d", d=DK + 1)
                    dve.reciprocal(inv_sum[:], pv[:, :, DK]).then_inc(m["inv_ready"], 1)
                    dve.wait_ge(m["inv_ready"], q.b + 1)
                    dve.tensor_tensor(mix[:], pv[:, :, 0:DK], inv_sum[:].unsqueeze(2).broadcast_to([P, HEADS, DK]),
                                      ALU.mult).then_inc(m["mix_ready"], 1)

                def residual(q):
                    dve.wait_ge(m["o_ready"], q.b + 1)
                    dve.tensor_tensor(res[:], o_ps[:, D:2 * D], x1[:, ds(GB + q.b, 1), :].rearrange("p o d -> p (o d)"),
                                      ALU.add).then_inc(m["res_ready"], 1)
                    dve.wait_ge(m["res_ready"], q.b + 1)
                    dve.bn_stats(o_stats[:, 0, :], res[:]).then_inc(m["o_stats_ready"], 1)
                    merge_moments(dve, o_stats, m["o_stats_ready"], q.b + 1, o_part, o_mean, o_var, m["o_moments"], q.b)

                def normalise(q):
                    dve.wait_ge(m["o_rstd_ready"], q.b + 1)
                    since(dve, row_stored[q.parity], 32 * q.half)
                    dve.tensor_scalar(row[q.parity][:, 0:D], res[:], o_mean[:, 0:1], o_rstd[:, 0:1], ALU.subtract,
                                      ALU.mult).then_inc(m["x2_ready"], 1)

                def sigmoid(q):
                    dve.wait_ge(m["g_exp_ready"], q.b + 1)
                    dve.tensor_scalar(g_den[:], g_exp[:], 1.0, None, ALU.add).then_inc(m["g_den_ready"], 1)
                    dve.wait_ge(m["g_den_ready"], q.b + 1)
                    dve.reciprocal(row[q.parity][:, D:D + EXPERTS], g_den[:])
                    dve.reciprocal(gate_all[:, q.parity, :, ds(q.half, 1)].rearrange("p e o -> p (e o)"), g_den[:]).then_inc(m["gate_ready"], 1)

                def step(q, a, b, c):
                    n, p = q.plus(1), q.plus(-1)
                    if c:
                        divide(p)
                    if b:
                        for j in range(4):
                            maximum(q, j)
                        negate(q)
                    if c:
                        residual(p)
                    if a:
                        moments(n)
                    if c:
                        normalise(p)
                    if a:
                        normalise_qk(n)
                    if c:
                        sigmoid(p)

                dve.wait_ge(m["const_loaded"], 16 * consts)
                for i in range(2):
                    for e in range(2):
                        dve.tensor_scalar(affine[:, i, e, :], norm[:, i, :], even_odd[:, e:e + 1], None, ALU.mult).then_inc(m["affine_ready"], 1)
                dve.wait_ge(m["set_up"], 5)
                passes(dve, step)



def choose_phase(nc, ident, gate_all, lists_dram, bits_i_dram, bits_f_dram, same_dram, before_dram, iota_dram, place_dram):
    CH = P // EXPERTS
    J = T // CH
    NBITS = 30
    LO = 32
    HI = TOPK // LO
    M = 2 * P
    with ExitStack() as ctx:
        s = Scope(nc, ctx, "choose")
        bits_i = s.sb("bits_i", [P, NBITS + 1], I32)
        bits_f = s.sb("bits_f", [P, NBITS])
        same = s.sb("same", [P, P])
        before = s.sb("before", [P, P])
        iota = s.sb("iota", [P, LO])
        place = s.sb("place", [P, 1 + 2 * 16])
        gate = s.sb("gate", [P, J])
        hit = s.sb("hit", [P, J])
        count = s.sb("count", [P, 1])
        limit = s.sb("limit", [P, 1], I32)
        trial = s.sb("trial", [P, 1], I32)
        gain = s.sb("gain", [P, 1], I32)
        above = s.sb("above", [P, J])
        n_above = s.sb("n_above", [P, 1])
        equal = s.sb("equal", [P, J])
        ones = s.sb("ones", [P, J])
        cum = s.sb("cum", [P, J])
        room = s.sb("room", [P, 1])
        start = s.sb("start", [P, 1])
        taken = s.sb("taken", [P, J])
        chosen = s.sb("chosen", [P, J])
        cum2 = s.sb("cum2", [P, J])
        start2 = s.sb("start2", [P, 1])
        slot = s.sb("slot", [P, J])
        slot_i = s.sb("slot_i", [P, J], I32)
        part_i = s.sb("part_i", [P, 2, J], I32)
        part_f = s.sb("part_f", [P, 2, J])
        turned = s.sb("turned", [P, 2, M])
        hi_hot = s.sb("hi_hot", [P, M, HI], BF16)
        lo_hot = s.sb("lo_hot", [P, M, LO], BF16)
        lo_val = s.sb("lo_val", [P, M, 2, LO], BF16)
        tiles = s.sb("tiles", [P, EXPERTS, 2, LO])
        token = s.sb("token", [HI, EXPERTS, LO], I32)

        gate_ps = s.ps("gate", [P, J])
        count_ps = s.ps("count", [P, 4])
        turn_ps = s.ps("turn", [P, 2 * M])
        list_ps = s.ps("list", [HI, EXPERTS, 2 * LO])

        loaded = s.sem("loaded")
        gate_turned = s.sem("gate_turned")
        started = s.sem("started")
        counted = s.sem("counted")
        totalled = s.sem("totalled")
        stepped = s.sem("stepped")
        chain = s.sem("chain")
        stage = s.sem("stage")
        above_summed = s.sem("above_summed")
        starts_ready = s.sem("starts_ready")
        starts2_ready = s.sem("starts2_ready")
        parts_turned = s.sem("parts_turned")
        turned_ready = s.sem("turned_ready")
        hi_ready = s.sem("hi_ready")
        lo_ready = s.sem("lo_ready")
        list_ready = s.sem("list_ready")
        token_ready = s.sem("token_ready")
        list_stored = s.sem("list_stored")

        with nc.Block() as block:

            @block.sync
            def _(sp):
                for sbuf, dram in ((same, same_dram), (bits_i, bits_i_dram), (bits_f, bits_f_dram), (before, before_dram),
                                   (iota, iota_dram), (place, place_dram)):
                    sp.dma_start(sbuf[:], dram).then_inc(loaded, 16)
                sp.wait_ge(token_ready, 1)
                sp.dma_start(lists_dram.rearrange("e (h l) -> h e l", l=LO), token[:]).then_inc(list_stored, 16)
                sp.wait_ge(list_stored, 16)

            @block.tensor
            def _(pe):
                for par in range(2):
                    last = pe.transpose(gate_ps[:, par * P:(par + 1) * P], gate_all[:, par, :, :].rearrange("p e c -> p (e c)"), ident[:])
                last.then_inc(gate_turned, 1)
                pe.wait_ge(loaded, 16 * 6)
                with pe.Fori(0, NBITS) as i:
                    pe.wait_ge(counted, i + 1)
                    pe.matmul(count_ps[:, 0:1], same[:], count[:], start=True, stop=True).then_inc(totalled, 1)
                pe.wait_ge(stage, 3)
                pe.matmul(count_ps[:, 0:1], same[:], n_above[:], start=True, stop=True).then_inc(above_summed, 1)
                pe.wait_ge(stage, 4)
                pe.matmul(count_ps[:, 1:2], before[:], cum[:, J - 1:J], start=True, stop=True).then_inc(starts_ready, 1)
                pe.wait_ge(stage, 8)
                pe.matmul(count_ps[:, 2:3], before[:], cum2[:, J - 1:J], start=True, stop=True).then_inc(starts2_ready, 1)
                pe.wait_ge(stage, 13)
                for h in range(2):
                    for par in range(2):
                        c = (2 * h + par) * P
                        last = pe.transpose(turn_ps[:, c:c + P], part_f[:, h, par * P:(par + 1) * P], ident[:])
                last.then_inc(parts_turned, 1)
                pe.wait_ge(hi_ready, 1)
                pe.wait_ge(lo_ready, 3)
                for e in range(EXPERTS):
                    for par in range(2):
                        for c in range(CH):
                            col = par * P + e * CH + c
                            last = pe.matmul(list_ps[:, e, :], hi_hot[:, col, :], lo_val[:, col, :, :],
                                             start=(par == 0 and c == 0), stop=(par == 1 and c == CH - 1))
                last.then_inc(list_ready, 1)

            @block.gpsimd
            def _(pool):
                pool.memset(ones[:], 1.0).then_inc(started, 1)

            @block.vector
            def _(dve):
                dve.memset(limit[:], 0)
                dve.wait_ge(loaded, 16 * 6)
                dve.tensor_copy(trial[:], bits_i[:, 0:1])
                dve.wait_ge(gate_turned, 1)
                dve.tensor_copy(gate[:], gate_ps[:]).then_inc(stepped, 1)
                with dve.Fori(0, NBITS) as i:
                    dve.wait_ge(stepped, i + 1)
                    dve.tensor_scalar(hit[:], gate[:], trial[:].bitcast(F32), None, ALU.is_ge, ALU.add, accum_out=count[:]).then_inc(counted, 1)
                    dve.wait_ge(totalled, i + 1)
                    dve.tensor_scalar(gain[:], count_ps[:, 0:1], float(TOPK), bits_f[:, ds(i, 1)], ALU.is_ge, ALU.mult).then_inc(chain, 1)
                    dve.wait_ge(chain, 2 * i + 1)
                    dve.tensor_tensor(limit[:], limit[:], gain[:], ALU.bitwise_or).then_inc(chain, 1)
                    dve.wait_ge(chain, 2 * i + 2)
                    dve.tensor_tensor(trial[:], limit[:], bits_i[:, ds(i + 1, 1)], ALU.bitwise_or).then_inc(stepped, 1)
                dve.wait_ge(stepped, NBITS + 1)
                dve.tensor_scalar(above[:], gate[:], trial[:].bitcast(F32), None, ALU.is_gt, ALU.add, accum_out=n_above[:]).then_inc(stage, 3)
                dve.tensor_scalar(equal[:], gate[:], trial[:].bitcast(F32), None, ALU.is_equal).then_inc(started, 1)
                dve.wait_ge(started, 2)
                dve.tensor_tensor_scan(cum[:], ones[:], equal[:], 0.0, ALU.mult, ALU.add).then_inc(stage, 1)
                dve.wait_ge(above_summed, 1)
                dve.wait_ge(starts_ready, 1)
                dve.tensor_scalar(room[:], count_ps[:, 0:1], -1.0, float(TOPK), ALU.mult, ALU.add)
                dve.tensor_copy(start[:], count_ps[:, 1:2]).then_inc(stage, 1)
                dve.wait_ge(stage, 5)
                dve.tensor_scalar(taken[:], cum[:], start[:, 0:1], room[:, 0:1], ALU.add, ALU.is_le).then_inc(stage, 1)
                dve.wait_ge(stage, 6)
                dve.tensor_tensor(equal[:], equal[:], taken[:], ALU.mult).then_inc(stage, 1)
                dve.wait_ge(stage, 7)
                dve.tensor_tensor(chosen[:], above[:], equal[:], ALU.add).then_inc(started, 1)
                dve.wait_ge(started, 3)
                dve.tensor_tensor_scan(cum2[:], ones[:], chosen[:], 0.0, ALU.mult, ALU.add).then_inc(stage, 1)
                dve.wait_ge(starts2_ready, 1)
                dve.tensor_copy(start2[:], count_ps[:, 2:3]).then_inc(stage, 1)
                dve.wait_ge(stage, 9)
                dve.scalar_tensor_tensor(slot[:], cum2[:], start2[:, 0:1], chosen[:], ALU.add, ALU.mult).then_inc(stage, 1)
                dve.wait_ge(stage, 10)
                dve.tensor_scalar(slot_i[:], slot[:], -1.0, None, ALU.add).then_inc(stage, 1)
                dve.wait_ge(stage, 11)
                dve.tensor_scalar(part_i[:, 0, :], slot_i[:], 5, None, ALU.arith_shift_right)
                dve.tensor_scalar(part_i[:, 1, :], slot_i[:], LO - 1, None, ALU.bitwise_and).then_inc(stage, 1)
                dve.wait_ge(stage, 12)
                dve.tensor_copy(part_f[:], part_i[:]).then_inc(stage, 1)
                dve.wait_ge(parts_turned, 1)
                dve.tensor_copy(turned[:].rearrange("p h m -> p (h m)"), turn_ps[:]).then_inc(turned_ready, 1)
                dve.wait_ge(turned_ready, 1)
                dve.tensor_tensor(lo_hot[:], turned[:, 1, :].unsqueeze(2).broadcast_to([P, M, LO]),
                                  iota[:].unsqueeze(1).broadcast_to([P, M, LO]), ALU.is_equal).then_inc(lo_ready, 1)
                dve.tensor_tensor(hi_hot[:], turned[:, 0, :].unsqueeze(2).broadcast_to([P, M, HI]),
                                  iota[:].unsqueeze(1).broadcast_to([P, M, HI]), ALU.is_equal).then_inc(hi_ready, 1)
                dve.wait_ge(lo_ready, 1)
                dve.tensor_scalar(lo_val[:, :, 0, :], lo_hot[:], place[:, 0:1], None, ALU.mult).then_inc(lo_ready, 1)
                for par in range(2):
                    for e in range(EXPERTS):
                        col = par * P + e * CH
                        last = dve.tensor_tensor(lo_val[:, col:col + CH, 1, :], lo_hot[:, col:col + CH, :],
                                                 place[:, 1 + par * CH:1 + (par + 1) * CH].unsqueeze(2).broadcast_to([P, CH, LO]), ALU.mult)
                last.then_inc(lo_ready, 1)
                dve.wait_ge(list_ready, 1)
                dve.tensor_copy(tiles[:HI].rearrange("p e a l -> p e (a l)"), list_ps[:]).then_inc(stepped, 1)
                dve.wait_ge(stepped, NBITS + 2)
                dve.scalar_tensor_tensor(token[:], tiles[:HI, :, 1, :], float(P), tiles[:HI, :, 0, :], ALU.mult, ALU.add).then_inc(token_ready, 1)


class Half:

    def __init__(self, pair, number):
        self.pair, self.number = pair + number // 4, number % 4
        self.parity = self.number // 2
        self.part = self.number % 2
        self.expert = 2 * self.pair + self.parity
        self.u = 4 * self.pair + self.number


def expert_phase(nc, ident, lists_dram, table_dram, acc_dram, w1_dram, b1_dram, w2_dram, b2_dram):
    FT = FF // P
    ST = TOPK // P
    HS = ST // 2
    W = HS * P
    with ExitStack() as ctx:
        s = Scope(nc, ctx, "expert")
        lists = s.sb("lists", [P, EXPERTS, ST], I32)
        lst = [s.sb(f"lst{i}", [P, ST], I32) for i in range(2)]
        w1 = [s.sb(f"w1{i}", [P, KH, FF]) for i in range(2)]
        b1 = [s.sb(f"b1{i}", [P, FT]) for i in range(2)]
        w2 = [s.sb(f"w2{i}", [P, FT, D]) for i in range(2)]
        b2 = [s.sb(f"b2{i}", [1, D]) for i in range(2)]
        one = s.sb("one", [1, P])
        xg = [s.sb(f"xg{i}", [P, ST, ROW]) for i in range(2)]
        gate = [s.sb(f"gate{i}", [P, ST]) for i in range(2)]
        xgT = [s.sb(f"xgT{i}", [P, KH, TOPK]) for i in range(2)]
        hid = [s.sb(f"hid{i}", [P, FT, W]) for i in range(2)]
        rows = [s.sb(f"rows{i}", [P, ST, D]) for i in range(2)]

        h_ps = [s.ps(f"h{i}", [P, W]) for i in range(4)]
        o_ps = [s.ps(f"o{i}", [P, D]) for i in range(2)]
        t_ps = [s.ps(f"t{i}", [P, W]) for i in range(2)]

        lists_loaded = s.sem("lists_loaded")
        set_up = s.sem("set_up")
        w_loaded = [s.sem(f"w_loaded{i}") for i in range(2)]
        gathered = [s.sem(f"gathered{i}") for i in range(2)]
        scattered = [s.sem(f"scattered{i}") for i in range(2)]
        lst_ready = s.sem("lst_ready")
        turned = s.sem("turned")
        xgT_ready = s.sem("xgT_ready")
        gate_ready = s.sem("gate_ready")
        h_ready = s.sem("h_ready")
        hid_ready = s.sem("hid_ready")
        o_ready = s.sem("o_ready")
        rows_ready = s.sem("rows_ready")
        waited = s.sem("waited")
        PAIRS = EXPERTS // 2
        LAST = 4 * PAIRS - 1

        with nc.Block() as block:

            @block.sync
            def _(sp):
                sp.dma_start(lists[:], lists_dram.rearrange("e (p s) -> p e s", s=ST)).then_inc(lists_loaded, 16)

                def load(pair, par, first=False):
                    e = 2 * pair + par
                    if not first:
                        sp.wait_ge(o_ready, ST * (e - 1))
                    for sbuf, dram in ((w1[par], w1_dram), (b1[par], b1_dram), (w2[par], w2_dram), (b2[par], b2_dram)):
                        src = dram[ds(e, 1)]
                        src = src.rearrange("o p a b -> (o p) a b") if len(dram.shape) == 4 else (
                            src.rearrange("o p a -> (o p) a") if len(dram.shape) == 3 else src)
                        sp.dma_start(sbuf[:], src).then_inc(w_loaded[par], 16)

                load(0, 0, first=True)
                load(0, 1, first=True)
                with sp.Fori(1, PAIRS) as i:
                    load(i, 0)
                    load(i, 1)

            @block.gpsimd
            def _(pool):
                def gather(pair, par, first=False):
                    e = 2 * pair + par
                    if not first:
                        pool.wait_ge(scattered[par], 16 * ST * pair)
                        pool.wait_ge(turned, 4 * (e - 1))
                        pool.wait_ge(gate_ready, e - 1)
                    pool.tensor_copy(lst[par][:], lists[:, ds(e, 1), :].rearrange("p o s -> p (o s)")).then_inc(lst_ready, 1)
                    pool.wait_ge(lst_ready, e + 1)
                    pool.sem_inc(waited, 1)
                    for t in range(ST):
                        pool.indirect_dma_start(out=xg[par][:, t, :], out_offset=None, in_=table_dram,
                                                in_offset=bass.IndirectOffsetOnAxis(ap=lst[par][:, t:t + 1], axis=0)
                                                ).then_inc(gathered[par], 16)

                def scatter(pair, par):
                    e = 2 * pair + par
                    for t in range(ST):
                        pool.wait_ge(rows_ready, ST * e + t + 1)
                        if t == 0:
                            if par == 0:
                                since(pool, scattered[1], 16 * ST * pair)
                            else:
                                pool.wait_ge(scattered[0], 16 * ST * (pair + 1))
                        pool.sem_inc(waited, 1)
                        pool.indirect_dma_start(out=acc_dram, out_offset=bass.IndirectOffsetOnAxis(ap=lst[par][:, t:t + 1], axis=0),
                                                in_=rows[par][:, t, :], in_offset=None, compute_op=ALU.add
                                                ).then_inc(scattered[par], 16)

                pool.memset(one[:], 1.0).then_inc(set_up, 1)
                pool.wait_ge(lists_loaded, 16)
                gather(0, 0, first=True)
                gather(0, 1, first=True)
                scatter(0, 0)
                with pool.Fori(1, PAIRS) as i:
                    gather(i, 0)
                    scatter(i - 1, 1)
                    gather(i, 1)
                    scatter(i, 0)
                scatter(PAIRS - 1, 1)
                for par in range(2):
                    pool.wait_ge(scattered[par], 16 * ST * PAIRS)

            @block.tensor
            def _(pe):
                def turn(pair, par):
                    e = 2 * pair + par
                    pe.wait_ge(gathered[par], 16 * ST * (pair + 1))
                    for part in range(2):
                        for k in range(KH):
                            n = 2 * part + k
                            since(pe, xgT_ready, 4 * e + n - 1)
                            for t in range(HS):
                                last = pe.transpose(t_ps[k][:, t * P:(t + 1) * P], xg[par][:, HS * part + t, k * P:(k + 1) * P], ident[:])
                            last.then_inc(turned, 1)

                def first(h):
                    if h.part == 0:
                        pe.wait_ge(w_loaded[h.parity], 64 * (h.pair + 1))
                    pe.wait_ge(xgT_ready, 4 * h.expert + 2 * h.part + 2)
                    for f in range(FT):
                        since(pe, hid_ready, FT * h.u + f - 3)
                        for k in range(KH):
                            last = pe.matmul(h_ps[f % 4][:], w1[h.parity][:, k, f * P:(f + 1) * P],
                                             xgT[h.parity][:, k, h.part * W:(h.part + 1) * W], start=(k == 0), stop=(k == KH - 1))
                        last.then_inc(h_ready, 1)

                def second(h):
                    pe.wait_ge(hid_ready, FT * (h.u + 1))
                    for t in range(HS):
                        since(pe, rows_ready, HS * h.u + t - 1)
                        pe.matmul(o_ps[t % 2][:], one[:], b2[h.parity][:], start=True, stop=False)
                        for f in range(FT):
                            last = pe.matmul(o_ps[t % 2][:], hid[h.part][:, f, t * P:(t + 1) * P], w2[h.parity][:, f, :],
                                             start=False, stop=(f == FT - 1))
                        last.then_inc(o_ready, 1)

                def pair(i, last=False):
                    for n in range(4):
                        if not (last and n == 3):
                            first(Half(i, n + 1))
                        if n % 2 == 0 and not (last and n == 2):
                            turn(i + n // 2, 1 - n // 2)
                        second(Half(i, n))

                pe.wait_ge(set_up, 1)
                turn(0, 0)
                first(Half(0, 0))
                pair(0)
                with pe.Fori(1, PAIRS - 1) as i:
                    pair(i)
                pair(PAIRS - 1, last=True)

            @block.scalar
            def _(act):
                nc.scalar.preload_act_table_set("gelu_and_others")

                def gelu(h):
                    if h.part == 0:
                        act.wait_ge(w_loaded[h.parity], 64 * (h.pair + 1))
                    since(act, o_ready, HS * (h.u - 1))
                    for f in range(FT):
                        act.wait_ge(h_ready, FT * h.u + f + 1)
                        act.activation(hid[h.part][:, f, :], h_ps[f % 4][:], ACT.Gelu, bias=b1[h.parity][:, f:f + 1]).then_inc(hid_ready, 1)

                for n in range(4):
                    gelu(Half(0, n))
                with act.Fori(1, PAIRS) as i:
                    for n in range(4):
                        gelu(Half(i, n))

            @block.vector
            def _(dve):
                def take(pair, par):
                    e = 2 * pair + par
                    dve.wait_ge(gathered[par], 16 * ST * (pair + 1))
                    dve.tensor_copy(gate[par][:], xg[par][:, :, ds(D + e, 1)].rearrange("p s o -> p (s o)")).then_inc(gate_ready, 1)
                    for n in range(4):
                        part, k = n // 2, n % 2
                        dve.wait_ge(turned, 4 * e + n + 1)
                        if n == 0:
                            since(dve, h_ready, 2 * FT * (e - 1))
                        dve.tensor_copy(xgT[par][:, k, part * W:(part + 1) * W], t_ps[k][:]).then_inc(xgT_ready, 1)

                def weigh(h):
                    if h.part == 0:
                        dve.wait_ge(gate_ready, h.expert + 1)
                        since(dve, scattered[h.parity], 16 * ST * h.pair)
                    for t in range(HS):
                        dve.wait_ge(o_ready, HS * h.u + t + 1)
                        n = HS * h.part + t
                        dve.tensor_scalar(rows[h.parity][:, n, :], o_ps[t % 2][:], gate[h.parity][:, n:n + 1], None,
                                          ALU.mult).then_inc(rows_ready, 1)

                def pair(i, last=False):
                    for n in range(4):
                        if n % 2 == 0 and not (last and n == 2):
                            take(i + n // 2, 1 - n // 2)
                        weigh(Half(i, n))

                take(0, 0)
                pair(0)
                with dve.Fori(1, PAIRS - 1) as i:
                    pair(i)
                pair(PAIRS - 1, last=True)


def final_phase(nc, acc_dram, out_dram):
    C = 8
    CHUNKS = T // (P * C)
    with ExitStack() as ctx:
        s = Scope(nc, ctx, "final")
        a = [s.sb(f"a{i}", [P, C, D]) for i in range(2)]
        o = [s.sb(f"o{i}", [P, C, D]) for i in range(2)]
        stats = s.sb("stats", [P, C, 6])
        part = s.sb("part", [P, 4, C])
        mean = s.sb("mean", [P, C])
        var = s.sb("var", [P, C])
        lnv = s.sb("lnv", [P, C])
        rstd = s.sb("rstd", [P, C])
        eps = s.sb("eps", [P, 1])
        loaded = [s.sem(f"loaded{i}") for i in range(2)]
        stored = [s.sem(f"stored{i}") for i in range(2)]
        stats_ready = s.sem("stats_ready")
        moments = s.sem("moments")
        lnv_ready = s.sem("lnv_ready")
        rstd_ready = s.sem("rstd_ready")
        normed = s.sem("normed")
        set_up = s.sem("set_up")

        def both(eng, step):
            step(0, 0)
            step(0, 1)
            with eng.Fori(1, CHUNKS // 2) as i:
                step(i, 0)
                step(i, 1)

        with nc.Block() as block:

            @block.sync
            def _(sp):
                def load(i, par):
                    c = 2 * i + par
                    since(sp, normed, c - 1)
                    sp.dma_start(a[par][:], acc_dram[ds(c * P * C, P * C), :].rearrange("(p t) d -> p t d", t=C)).then_inc(loaded[par], 16)

                both(sp, load)

            @block.scalar
            def _(act):
                def step(i, par):
                    c = 2 * i + par
                    act.wait_ge(moments, 3 * (c + 1))
                    act.activation(lnv[:], var[:], ACT.Ln, bias=eps[:, 0:1]).then_inc(lnv_ready, 1)
                    act.wait_ge(lnv_ready, c + 1)
                    since(act, normed, c)
                    act.activation(rstd[:], lnv[:], ACT.Exp, scale=-0.5).then_inc(rstd_ready, 1)
                    act.wait_ge(normed, c + 1)
                    act.dma_start(out_dram[ds(c * P * C, P * C), :].rearrange("(p t) d -> p t d", t=C), o[par][:]).then_inc(stored[par], 16)

                nc.scalar.preload_act_table_set("natural_log_exp_and_others")
                act.wait_ge(set_up, 1)
                both(act, step)
                for q in stored:
                    act.wait_ge(q, 16 * (CHUNKS // 2))

            @block.vector
            def _(dve):
                def step(i, par):
                    c = 2 * i + par
                    dve.wait_ge(loaded[par], 16 * (i + 1))
                    for t in range(C):
                        last = dve.bn_stats(stats[:, t, :], a[par][:, t, :])
                    last.then_inc(stats_ready, 1)
                    merge_moments(dve, stats, stats_ready, c + 1, part, mean, var, moments, c)
                    dve.wait_ge(rstd_ready, c + 1)
                    since(dve, stored[par], 16 * i)
                    for t in range(C):
                        last = dve.tensor_scalar(o[par][:, t, :], a[par][:, t, :], mean[:, t:t + 1], rstd[:, t:t + 1], ALU.subtract, ALU.mult)
                    last.then_inc(normed, 1)

                dve.memset(eps[:], EPS).then_inc(set_up, 1)
                both(dve, step)


def build(nc, xT, w_proj, w_bc, w_dt, b_dt, a_log, sel, ident_dram, ctxT, w_q, w_kv, w_o, w_g, norm, even_odd, pick,
          bits_i, bits_f, same, before, iota, place, w1, b1, w2, b2, out):
    table = nc.dram_tensor("table", (T, ROW), F32, kind="Internal").ap()
    acc = nc.dram_tensor("acc", (T, D), F32, kind="Internal").ap()
    lists = nc.dram_tensor("lists", (EXPERTS, TOPK), I32, kind="Internal").ap()
    with ExitStack() as ctx:
        s = Scope(nc, ctx, "all")
        ident = s.sb("ident", [P, P])
        gate_all = s.sb("gate_all", [P, 2, EXPERTS, NT // 2])
        with ExitStack() as front:
            x1 = Scope(nc, front, "front").sb("x1", [P, GB + NT, D])
            scan_phase(nc, x1, (ident, ident_dram), xT, w_proj, w_bc, w_dt, b_dt, a_log, sel)
            attention_phase(nc, x1, ident, gate_all, ctxT, w_q, w_kv, w_o, w_g, norm, even_odd, pick, table, acc)
        choose_phase(nc, ident, gate_all, lists, bits_i, bits_f, same, before, iota, place)
        expert_phase(nc, ident, lists, table, acc, w1, b1, w2, b2)
        final_phase(nc, acc, out)


def kernel(x, ctx_1024, L0_attn_W_xproj, L0_attn_W_dt, L0_attn_b_dt, L0_attn_A_log, L0_xattn_Wq, L0_xattn_Wk,
           L0_xattn_Wv, L0_xattn_Wo, L0_xattn_ln_gamma, L0_xattn_ln_beta, L0_ffn_Wg, L0_ffn_W1, L0_ffn_b1,
           L0_ffn_W2, L0_ffn_b2):
    import ml_dtypes
    import concourse.bacc as bacc
    from concourse.bass_utils import run_bass_kernel_spmd

    def halves(a):
        return np.ascontiguousarray(a.reshape(KH, P, -1).transpose(1, 0, 2))

    x = np.asarray(x)
    w_xproj = np.asarray(L0_attn_W_xproj)
    w_bc = np.concatenate([w_xproj[R:]] * 3, axis=0)
    sel = np.zeros((96, 2 * NS, P), ml_dtypes.bfloat16)
    for part in range(3):
        for n in range(2 * NS):
            sel[32 * part + n, n, :] = 1
    bits = np.array([1 << b for b in range(29, -1, -1)] + [0], np.int32)
    expert_of = np.arange(P) // (P // EXPERTS)
    same = expert_of[:, None] == expert_of[None, :]
    place = np.zeros((P, 1 + NT), np.float32)
    place[:, 0] = np.arange(P)
    for parity in range(2):
        place[:, 1 + parity * 16:1 + (parity + 1) * 16] = 2 * np.arange(16) + parity
    head_of = np.arange(P) // DK % 2
    even_odd = np.stack([head_of == 0, head_of == 1], axis=1).astype(np.float32)
    pick = np.zeros((P, 4, P), ml_dtypes.bfloat16)
    for j in range(4):
        for i in range(4):
            pick[32 * j + i, i, :] = 1
    arrays = {
        "xT": halves(x.reshape(T, D).T),
        "w_proj": halves(w_xproj[:R].T),
        "w_bc": halves(w_bc.T),
        "w_dt": np.ascontiguousarray(np.asarray(L0_attn_W_dt).T),
        "b_dt": np.ascontiguousarray(np.asarray(L0_attn_b_dt).reshape(KH, P).T),
        "a_log": halves(np.asarray(L0_attn_A_log)),
        "sel": sel,
        "ident": np.eye(P, dtype=np.float32),
        "ctxT": halves(np.asarray(ctx_1024).reshape(T, D).T),
        "w_q": halves(np.asarray(L0_xattn_Wq).T),
        "w_kv": halves(np.concatenate([np.asarray(L0_xattn_Wk).T, np.asarray(L0_xattn_Wv).T], axis=1)),
        "w_o": halves(np.asarray(L0_xattn_Wo).T),
        "w_g": halves(np.asarray(L0_ffn_Wg)),
        "norm": np.ascontiguousarray(np.stack([np.asarray(a).reshape(KH, P) for a in (L0_xattn_ln_gamma, L0_xattn_ln_beta)]).transpose(2, 0, 1)),
        "even_odd": even_odd,
        "pick": pick,
        "bits_i": np.tile(bits, (P, 1)),
        "bits_f": np.tile(bits[:-1].astype(np.float32), (P, 1)),
        "same": same.astype(np.float32),
        "before": (same & (np.arange(P)[:, None] < np.arange(P)[None, :])).astype(np.float32),
        "iota": np.tile(np.arange(32, dtype=np.float32), (P, 1)),
        "place": place,
        "w1": np.ascontiguousarray(np.asarray(L0_ffn_W1).reshape(EXPERTS, KH, P, FF).transpose(0, 2, 1, 3)),
        "b1": np.ascontiguousarray(np.asarray(L0_ffn_b1).reshape(EXPERTS, FF // P, P).transpose(0, 2, 1)),
        "w2": np.ascontiguousarray(np.asarray(L0_ffn_W2).reshape(EXPERTS, FF // P, P, D).transpose(0, 2, 1, 3)),
        "b2": np.ascontiguousarray(np.asarray(L0_ffn_b2)),
    }
    nc = bacc.Bacc("TRN2", target_bir_lowering=False, num_devices=1)
    args = [nc.dram_tensor(n, a.shape, mybir.dt.from_np(a.dtype), kind="ExternalInput").ap() for n, a in arrays.items()]
    out = nc.dram_tensor("out", (T, D), F32, kind="ExternalOutput").ap()
    build(nc, *args, out)
    r = run_bass_kernel_spmd(nc, [arrays], core_ids=[0])
    return np.asarray(r.results[0]["out"]).reshape(BATCH, SEQ, D)
```

```python
from contextlib import ExitStack

import numpy as np

import concourse.bass as bass
from concourse import mybir

F32 = mybir.dt.float32
BF16 = mybir.dt.bfloat16
I32 = mybir.dt.int32
ALU = mybir.AluOpType
ACT = mybir.ActivationFunctionType
AX = mybir.AxisListType
ds = bass.ds

P = 128
BATCH, SEQ, D = 32, 128, 256
T = BATCH * SEQ
KH = D // P
NT = T // P
NS, R = 16, 64
HEADS, DK = 16, 16
EXPERTS, FF = 8, 1024
TOPK = min(max(int(T * 2 / EXPERTS), 1), T)
EPS = 1e-5
ROW = D + EXPERTS

GB = 4
GT = GB * SEQ
GROUPS = T // GT
RING = 4
STEPS = NS


def merge_moments(dve, stats, stats_ready, stats_count, part, mean, var, done, before):
    even, odd = stats[:, :, 1], stats[:, :, 4]
    dve.wait_ge(stats_ready, stats_count)
    dve.tensor_tensor(part[:, 0, :], even, odd, ALU.add)
    dve.tensor_tensor(part[:, 1, :], even, odd, ALU.subtract)
    dve.tensor_tensor(part[:, 2, :], stats[:, :, 2], stats[:, :, 5], ALU.add).then_inc(done, 1)
    dve.wait_ge(done, 3 * before + 1)
    dve.tensor_scalar(mean[:], part[:, 0, :], 0.5, None, ALU.mult)
    dve.scalar_tensor_tensor(part[:, 3, :], part[:, 1, :], 0.25, part[:, 1, :], ALU.mult, ALU.mult).then_inc(done, 1)
    dve.wait_ge(done, 3 * before + 2)
    dve.scalar_tensor_tensor(var[:], part[:, 2, :], 1.0 / D, part[:, 3, :], ALU.mult, ALU.add).then_inc(done, 1)


class Scope:

    def __init__(self, nc, ctx, tag):
        self.nc, self.ctx, self.tag = nc, ctx, tag

    def sb(self, name, shape, dt=F32):
        return self.ctx.enter_context(self.nc.sbuf_tensor(f"{self.tag}_{name}", shape, dt))

    def ps(self, name, shape, dt=F32):
        return self.ctx.enter_context(self.nc.psum_tensor(f"{self.tag}_{name}_ps", shape, dt))

    def sem(self, name):
        return self.ctx.enter_context(self.nc.semaphore(f"{self.tag}_{name}"))


def scan_phase(nc, x1, ident, xT_dram, w_proj_dram, w_bc_dram, w_dt_dram, b_dt_dram, a_log_dram, sel_dram):
    with ExitStack() as ctx:
        s = Scope(nc, ctx, "scan")
        w_proj = s.sb("w_proj", [P, KH, R])
        w_bc = s.sb("w_bc", [P, KH, 96])
        w_dt = s.sb("w_dt", [R, D])
        b_dt = s.sb("b_dt", [P, KH])
        a_log = s.sb("a_log", [P, KH, NS])
        a_exp = s.sb("a_exp", [P, KH, NS])
        a_neg = s.sb("a_neg", [P, KH, NS])
        sel = s.sb("sel", [96, 2 * NS, P], BF16)
        xT = [s.sb(f"xT{i}", [P, KH, GT]) for i in range(2)]
        bcs = [s.sb(f"bcs{i}", [96, GT], BF16) for i in range(2)]
        bc_rest = s.sb("bc_rest", [96, GT])
        bc_mid = s.sb("bc_mid", [96, GT], BF16)
        dt_low = s.sb("dt_low", [R, GT])
        z_abs = s.sb("z_abs", [P, KH, GT])
        z_exp = s.sb("z_exp", [P, KH, GT])
        z_log = s.sb("z_log", [P, KH, GT])
        z_pos = s.sb("z_pos", [P, KH, GT])
        delta = [s.sb(f"delta{i}", [P, KH, GB, SEQ]) for i in range(2)]
        dx = [s.sb(f"dx{i}", [P, KH, GT]) for i in range(2)]
        decay = s.sb("decay", [P, RING, KH, GB, SEQ])
        drive = s.sb("drive", [P, RING, KH, GT])
        state = s.sb("state", [P, RING, KH, GT])
        c_sb = s.sb("c_sb", [P, RING, GT])
        hc = s.sb("hc", [P, RING, KH, GT])
        yT = s.sb("yT", [P, KH, GT])
        stats = s.sb("stats", [P, GB, 6])
        moment = s.sb("moment", [P, 4, GB])
        mean = s.sb("mean", [P, GB])
        var = s.sb("var", [P, GB])
        ln_var = s.sb("ln_var", [P, GB])
        rstd = s.sb("rstd", [P, GB])
        eps = s.sb("eps", [P, 1])

        b_ps = [s.ps(f"b{i}", [P, 512]) for i in range(2)]
        c_ps = [s.ps(f"c{i}", [P, 512]) for i in range(2)]
        y_ps = [s.ps(f"y{i}", [P, 512]) for i in range(KH)]
        m_ps = [s.ps(f"m{i}", [P, 512]) for i in range(2)]

        const_loaded = s.sem("const_loaded")
        x_loaded = [s.sem(f"x_loaded{i}") for i in range(2)]
        zeroed = s.sem("zeroed")
        a_ready = s.sem("a_ready")
        proj_ready = s.sem("proj_ready")
        dt_copied = s.sem("dt_copied")
        bc_high = s.sem("bc_high")
        bc_step = s.sem("bc_step")
        bcs_ready = s.sem("bcs_ready")
        z_ready = s.sem("z_ready")
        z_abs_ready = s.sem("z_abs_ready")
        z_exp_ready = s.sem("z_exp_ready")
        z_log_ready = s.sem("z_log_ready")
        z_pos_ready = s.sem("z_pos_ready")
        delta_ready = s.sem("delta_ready")
        dx_ready = s.sem("dx_ready")
        decay_ready = s.sem("decay_ready")
        b_ready = s.sem("b_ready")
        c_ready = s.sem("c_ready")
        c_copied = s.sem("c_copied")
        drive_ready = s.sem("drive_ready")
        scanned = s.sem("scanned")
        hc_ready = s.sem("hc_ready")
        hc_summed = s.sem("hc_summed")
        y_started = s.sem("y_started")
        y_copied = s.sem("y_copied")
        turned = s.sem("turned")
        stats_ready = s.sem("stats_ready")
        mv_ready = s.sem("mv_ready")
        lv_ready = s.sem("lv_ready")
        rstd_ready = s.sem("rstd_ready")
        normed = s.sem("normed")
        consts = 7

        with nc.Block() as block:

            @block.sync
            def _(sp):
                sp.dma_start(w_proj[:], w_proj_dram).then_inc(const_loaded, 16)
                sp.dma_start(w_bc[:], w_bc_dram).then_inc(const_loaded, 16)
                sp.dma_start(xT[0][:], xT_dram[:, :, 0:GT]).then_inc(x_loaded[0], 16)
                sp.dma_start(w_dt[:], w_dt_dram).then_inc(const_loaded, 16)
                sp.dma_start(b_dt[:], b_dt_dram).then_inc(const_loaded, 16)
                sp.dma_start(a_log[:], a_log_dram).then_inc(const_loaded, 16)
                sp.dma_start(sel[:], sel_dram).then_inc(const_loaded, 16)
                sp.dma_start(ident[0][:], ident[1]).then_inc(const_loaded, 16)
                sp.dma_start(xT[1][:], xT_dram[:, :, GT:2 * GT]).then_inc(x_loaded[1], 16)
                with sp.Fori(1, GROUPS // 2) as i:
                    for par in range(2):
                        g = 2 * i + par
                        sp.wait_ge(y_started, g - 1)
                        sp.wait_ge(dx_ready, g - 1)
                        sp.dma_start(xT[par][:], xT_dram[:, :, ds(g * GT, GT)]).then_inc(x_loaded[par], 16)

            @block.tensor
            def _(pe):
                def project(i, par, first=False):
                    g = 2 * i + par
                    pe.wait_ge(x_loaded[par], 16 * (i + 1))
                    if not first:
                        pe.wait_ge(normed, g + 1)
                    for k in range(KH):
                        pe.matmul(m_ps[0][0:R, :], w_proj[:, k, :], xT[par][:, k, :], start=(k == 0), stop=(k == KH - 1))
                    for k in range(KH):
                        last = pe.matmul(m_ps[1][0:96, :], w_bc[:, k, :], xT[par][:, k, :], start=(k == 0), stop=(k == KH - 1))
                    last.then_inc(proj_ready, 1)

                def step_size(i, par):
                    g = 2 * i + par
                    pe.wait_ge(dt_copied, g + 1)
                    pe.wait_ge(bc_high, g + 1)
                    pe.wait_ge(bc_step, 5 * g + 1)
                    for k in range(KH):
                        last = pe.matmul(m_ps[k][:], w_dt[:, k * P:(k + 1) * P], dt_low[:], start=True, stop=True)
                    last.then_inc(z_ready, 1)

                def broadcast_b(i, par, n):
                    g = 2 * i + par
                    q = STEPS * g + n
                    if n == 0:
                        pe.wait_ge(bcs_ready, g + 1)
                    pe.wait_ge(drive_ready, q + 1)
                    pe.matmul(b_ps[n % 2][:], sel[:, n, :], bcs[par][:], start=True, stop=True).then_inc(b_ready, 1)

                def broadcast_c(i, par, n):
                    q = STEPS * (2 * i + par) + n
                    pe.wait_ge(c_copied, q + 1)
                    mm = pe.matmul(c_ps[n % 2][:], sel[:, NS + n, :], bcs[par][:], start=True, stop=True)
                    mm.then_inc(c_ready, 1)

                def add_state(q, n):
                    pe.wait_ge(hc_ready, q + 1 + RING)
                    for k in range(KH):
                        last = pe.matmul(y_ps[k][:], ident[0][:], hc[:, n % RING, k, :], start=False, stop=(n == NS - 1))
                    last.then_inc(hc_summed, 1)

                def start_y(i, par):
                    g = 2 * i + par
                    pe.wait_ge(y_copied, g + 1)
                    for k in range(KH):
                        last = pe.matmul(y_ps[k][:], ident[0][:], xT[par][:, k, :], start=True, stop=False)
                    last.then_inc(y_started, 1)

                def turn(g):
                    pe.wait_ge(y_copied, g + 1)
                    pe.wait_ge(z_abs_ready, 2 * (g + 1))
                    pe.wait_ge(z_pos_ready, 2 * (g + 1))
                    for j in range(GB):
                        for k in range(KH):
                            c = (j % 2) * D + k * P
                            last = pe.transpose(m_ps[j // 2][:, c:c + P], yT[:, k, j * P:(j + 1) * P], ident[0][:])
                    last.then_inc(turned, 1)

                def group(i, par, final=False):
                    g = 2 * i + par
                    for n in range(STEPS):
                        ahead = (i, par, n + 2) if n + 2 < STEPS else None if final else (i + par, 1 - par, n + 2 - STEPS)
                        if ahead:
                            broadcast_b(*ahead)
                        if n == 2:
                            start_y(i, par)
                        add_state(STEPS * g + n - 2, (n - 2) % STEPS)
                        if ahead:
                            broadcast_c(*ahead)
                        if n == 3:
                            turn(g)
                        if not final:
                            if n == 6:
                                project(i + par, 1 - par)
                            if n == 8:
                                step_size(i + par, 1 - par)

                pe.sem_inc(c_ready, 1)
                pe.wait_ge(const_loaded, 16 * consts)
                project(0, 0, first=True)
                pe.wait_ge(zeroed, 3)
                for k in range(KH):
                    pe.matmul(y_ps[k][:], ident[0][:], hc[:, RING - 1, k, :], start=True, stop=False)
                step_size(0, 0)
                for n in range(2):
                    broadcast_b(0, 0, n)
                    broadcast_c(0, 0, n)
                with pe.Fori(0, GROUPS // 2 - 1) as i:
                    group(i, 0)
                    group(i, 1)
                group(GROUPS // 2 - 1, 0)
                group(GROUPS // 2 - 1, 1, final=True)
                add_state(STEPS * GROUPS - 2, NS - 2)
                add_state(STEPS * GROUPS - 1, NS - 1)
                turn_last = GROUPS
                pe.wait_ge(y_copied, turn_last + 1)
                for j in range(GB):
                    for k in range(KH):
                        c = (j % 2) * D + k * P
                        last = pe.transpose(m_ps[j // 2][:, c:c + P], yT[:, k, j * P:(j + 1) * P], ident[0][:])
                last.then_inc(turned, 1)

            @block.scalar
            def _(act):
                nc.scalar.preload_act_table_set("natural_log_exp_and_others")

                def copy_low(g):
                    act.wait_ge(proj_ready, g + 1)
                    act.activation(dt_low[:], m_ps[0][0:R, :], ACT.Copy).then_inc(dt_copied, 1)

                def high_part(i, par, first=False):
                    g = 2 * i + par
                    if not first:
                        act.wait_ge(c_ready, STEPS * (g - 1) + 1)
                    act.activation(bcs[par][:], m_ps[1][0:96, :], ACT.Copy).then_inc(bc_high, 1)

                def softplus_parts(g, first=False):
                    act.wait_ge(z_ready, g + 1)
                    if not first:
                        act.wait_ge(z_log_ready, g)
                        act.wait_ge(delta_ready, g)
                    for k in range(KH):
                        act.activation(z_abs[:, k, :], m_ps[k][:], ACT.Abs, bias=b_dt[:, k:k + 1]).then_inc(z_abs_ready, 1)
                        act.activation(z_pos[:, k, :], m_ps[k][:], ACT.Relu, bias=b_dt[:, k:k + 1]).then_inc(z_pos_ready, 1)

                def softplus_exp(g):
                    act.wait_ge(z_abs_ready, 2 * (g + 1))
                    act.activation(z_exp[:], z_abs[:], ACT.Exp, scale=-1.0).then_inc(z_exp_ready, 1)

                def softplus_log(g, first=False):
                    act.wait_ge(z_exp_ready, g + 1)
                    if not first:
                        act.wait_ge(delta_ready, g)
                    act.activation(z_log[:], z_exp[:], ACT.Ln, bias=1.0).then_inc(z_log_ready, 1)

                def decays(par, q, n):
                    act.wait_ge(scanned, q + 1)
                    for k in range(KH):
                        act.activation(decay[:, n % RING, k, :, 1:SEQ], delta[par][:, k, :, 1:SEQ], ACT.Exp,
                                       scale=a_neg[:, k, n:n + 1]).then_inc(decay_ready, 1)

                def copy_y(g):
                    act.wait_ge(hc_summed, STEPS * g + 4)
                    act.wait_ge(turned, g)
                    act.activation(yT[:, 0, :], y_ps[0][:], ACT.Copy)
                    act.activation(yT[:, 1, :], y_ps[1][:], ACT.Copy).then_inc(y_copied, 1)

                def inv_std(g):
                    act.wait_ge(mv_ready, 3 * (g + 1))
                    act.wait_ge(normed, g + 1)
                    act.activation(ln_var[:], var[:], ACT.Ln, bias=eps[:, 0:1]).then_inc(lv_ready, 1)
                    act.wait_ge(lv_ready, g + 1)
                    act.activation(rstd[:], ln_var[:], ACT.Exp, scale=-0.5).then_inc(rstd_ready, 1)

                def group(i, par, final=False):
                    g = 2 * i + par
                    for n in range(STEPS):
                        q = STEPS * g + n
                        if n + 2 < STEPS:
                            decays(par, q + 2, n + 2)
                        elif not final:
                            if n + 2 == STEPS:
                                act.wait_ge(delta_ready, g + 2)
                            decays(1 - par, q + 2, n + 2 - STEPS)
                        act.wait_ge(c_ready, q + 2)
                        act.wait_ge(hc_ready, q + 1)
                        act.activation(c_sb[:, n % RING, :], c_ps[n % 2][:], ACT.Copy).then_inc(c_copied, 1)
                        if n == 2:
                            copy_y(g)
                        if n == 5:
                            inv_std(g)
                        if not final:
                            if n == 7:
                                copy_low(g + 1)
                                high_part(i + par, 1 - par)
                            if n == 9:
                                softplus_parts(g + 1)
                            if n == 10:
                                softplus_exp(g + 1)
                            if n == 11:
                                softplus_log(g + 1)

                act.sem_inc(c_copied, 2)
                act.sem_inc(turned, 1)
                act.sem_inc(normed, 1)
                act.wait_ge(const_loaded, 16 * consts)
                act.activation(a_exp[:], a_log[:], ACT.Exp).then_inc(a_ready, 1)
                copy_low(0)
                high_part(0, 0, first=True)
                softplus_parts(0, first=True)
                softplus_exp(0)
                softplus_log(0, first=True)
                act.wait_ge(a_ready, 2)
                act.wait_ge(zeroed, 3)
                act.wait_ge(delta_ready, 1)
                for n in range(2):
                    decays(0, n, n)
                with act.Fori(0, GROUPS // 2 - 1) as i:
                    group(i, 0)
                    group(i, 1)
                group(GROUPS // 2 - 1, 0)
                group(GROUPS // 2 - 1, 1, final=True)
                copy_y(GROUPS)
                inv_std(GROUPS)

            @block.vector
            def _(dve):
                def split(i, par):
                    g = 2 * i + par
                    dve.wait_ge(bc_high, g + 1)
                    dve.tensor_tensor(bc_rest[:], m_ps[1][0:96, :], bcs[par][:], ALU.subtract).then_inc(bc_step, 1)
                    dve.wait_ge(bc_step, 5 * g + 1)
                    dve.tensor_copy(bcs[par][32:64, :], bc_rest[32:64, :]).then_inc(bc_step, 1)
                    dve.tensor_copy(bc_mid[64:96, :], bc_rest[64:96, :]).then_inc(bc_step, 1)
                    dve.wait_ge(bc_step, 5 * g + 3)
                    dve.tensor_tensor(bcs[par][64:96, :], bc_rest[64:96, :], bc_mid[64:96, :], ALU.subtract).then_inc(bc_step, 1)
                    dve.wait_ge(bc_step, 5 * g + 4)
                    dve.sem_inc(bc_step, 1)
                    dve.sem_inc(bcs_ready, 1)

                def step_inputs(i, par):
                    g = 2 * i + par
                    dve.wait_ge(delta_ready, g + 1)
                    dve.tensor_tensor(dx[par][:], delta[par][:].rearrange("p k b t -> p k (b t)"), xT[par][:], ALU.mult).then_inc(dx_ready, 1)

                def drives(i, par, n):
                    g = 2 * i + par
                    q = STEPS * g + n
                    if n == 0:
                        dve.wait_ge(dx_ready, g + 1)
                    dve.wait_ge(b_ready, q + 1)
                    dve.wait_ge(scanned, q + 1)
                    dve.tensor_tensor(drive[:, n % RING, :, :], dx[par][:],
                                      b_ps[n % 2][:].unsqueeze(1).broadcast_to([P, KH, GT]), ALU.mult).then_inc(drive_ready, 1)

                def scan(q, n):
                    dve.wait_ge(drive_ready, q + 3)
                    dve.wait_ge(decay_ready, KH * (q + 1) + KH)
                    dve.wait_ge(hc_ready, q + 1)
                    dve.tensor_tensor_scan(state[:, n % RING, :, :].rearrange("p k t -> p (k t)"),
                                           decay[:, n % RING, :, :, :].rearrange("p k b t -> p (k b t)"),
                                           drive[:, n % RING, :, :].rearrange("p k t -> p (k t)"),
                                           0.0, ALU.mult, ALU.add).then_inc(scanned, 1)

                def statistics(g):
                    dve.wait_ge(turned, g + 2)
                    for j in range(GB):
                        last = dve.bn_stats(stats[:, j, :], m_ps[j // 2][:, (j % 2) * D:(j % 2 + 1) * D])
                    last.then_inc(stats_ready, 1)
                    merge_moments(dve, stats, stats_ready, g + 1, moment, mean, var, mv_ready, g)

                def normalise(g):
                    dve.wait_ge(rstd_ready, g + 1)
                    for j in range(GB):
                        last = dve.tensor_scalar(x1[:, ds(GB * g + j, 1), :].rearrange("p o d -> p (o d)"),
                                                 m_ps[j // 2][:, (j % 2) * D:(j % 2 + 1) * D],
                                                 mean[:, j:j + 1], rstd[:, j:j + 1], ALU.subtract, ALU.mult)
                    last.then_inc(normed, 1)

                def group(i, par, final=False):
                    g = 2 * i + par
                    for n in range(STEPS):
                        q = STEPS * g + n
                        if n + 1 < STEPS:
                            drives(i, par, n + 1)
                        elif not final:
                            drives(i + par, 1 - par, 0)
                        scan(q, n)
                        if n == 4:
                            statistics(g)
                        if n == 5:
                            normalise(g)
                        if n == 7 and not final:
                            split(i + par, 1 - par)
                        if n == 13 and not final:
                            step_inputs(i + par, 1 - par)

                dve.sem_inc(drive_ready, 2)
                dve.sem_inc(scanned, RING)
                dve.memset(decay[:].rearrange("p r k b t -> p (r k b) t")[:, :, 0], 0.0).then_inc(zeroed, 1)
                dve.memset(eps[:], EPS).then_inc(zeroed, 1)
                dve.wait_ge(a_ready, 1)
                dve.tensor_scalar(a_neg[:], a_exp[:], -1.0, None, ALU.mult).then_inc(a_ready, 1)
                split(0, 0)
                step_inputs(0, 0)
                drives(0, 0, 0)
                with dve.Fori(0, GROUPS // 2 - 1) as i:
                    group(i, 0)
                    group(i, 1)
                group(GROUPS // 2 - 1, 0)
                group(GROUPS // 2 - 1, 1, final=True)
                statistics(GROUPS)
                normalise(GROUPS)

            @block.gpsimd
            def _(pool):
                def step_sizes(i, par, first=False):
                    g = 2 * i + par
                    pool.wait_ge(z_log_ready, g + 1)
                    pool.wait_ge(z_pos_ready, 2 * (g + 1))
                    if not first:
                        pool.wait_ge(decay_ready, KH * STEPS * (g - 1) + KH)
                    pool.tensor_tensor(delta[par][:].rearrange("p k b t -> p k (b t)"), z_log[:], z_pos[:], ALU.add).then_inc(delta_ready, 1)

                def outputs(q, n):
                    pool.wait_ge(c_copied, q + 3)
                    pool.wait_ge(scanned, q + 1 + RING)
                    pool.wait_ge(hc_summed, q + 1)
                    pool.tensor_tensor(hc[:, n % RING, :, :], state[:, n % RING, :, :],
                                       c_sb[:, n % RING, :].unsqueeze(1).broadcast_to([P, KH, GT]), ALU.mult).then_inc(hc_ready, 1)

                def group(i, par, final=False):
                    g = 2 * i + par
                    for n in range(STEPS):
                        outputs(STEPS * g + n, n)
                        if not final:
                            if n == 11:
                                step_sizes(i + par, 1 - par)

                pool.sem_inc(hc_summed, RING - 2)
                pool.sem_inc(decay_ready, 2)
                pool.memset(hc[:, RING - 2:RING, :, :], 0.0).then_inc(zeroed, 1)
                pool.wait_ge(zeroed, 3)
                pool.sem_inc(hc_ready, RING)
                step_sizes(0, 0, first=True)
                with pool.Fori(0, GROUPS // 2 - 1) as i:
                    group(i, 0)
                    group(i, 1)
                group(GROUPS // 2 - 1, 0)
                group(GROUPS // 2 - 1, 1, final=True)


class Seq:

    def __init__(self, pair, offset):
        self.pair, self.offset = pair, offset
        self.parity = offset % 2
        self.half = pair + offset // 2
        self.b = 2 * pair + offset

    def plus(self, n):
        return Seq(self.pair, self.offset + n)


def since(eng, sem, count):
    if not (isinstance(count, int) and count < 1):
        eng.wait_ge(sem, count)


def attention_phase(nc, x1, ident, gate_all, ctxT_dram, w_q_dram, w_kv_dram, w_o_dram, w_g_dram, norm_dram,
                    even_odd_dram, pick_dram, table_dram, acc_dram):
    with ExitStack() as ctx:
        s = Scope(nc, ctx, "attn")
        w_q = s.sb("w_q", [P, KH, D])
        w_kv = s.sb("w_kv", [P, KH, 2 * D])
        w_o = s.sb("w_o", [P, KH, D])
        w_g = s.sb("w_g", [P, KH, EXPERTS])
        norm = s.sb("norm", [P, 2, KH])
        even_odd = s.sb("even_odd", [P, 2])
        affine = s.sb("affine", [P, 2, 2, KH])
        pick = s.sb("pick", [P, HEADS, P], BF16)
        eps = s.sb("eps", [P, 1])
        x1b = [s.sb(f"x1b{i}", [P, D]) for i in range(2)]
        x1T = s.sb("x1T", [P, KH, P])
        ctxT = [s.sb(f"ctxT{i}", [P, KH, P]) for i in range(2)]
        qk_stats = s.sb("qk_stats", [P, 2, 6])
        qk_part = s.sb("qk_part", [P, 4, 2])
        qk_mean = s.sb("qk_mean", [P, 2])
        qk_var = s.sb("qk_var", [P, 2])
        qk_lnv = s.sb("qk_lnv", [P, 2])
        qk_rstd = s.sb("qk_rstd", [P, 2])
        qkn = s.sb("qkn", [P, 2, D])
        qT = [s.sb(f"qT{i}", [P, KH, 2, P]) for i in range(2)]
        kT = [s.sb(f"kT{i}", [P, KH, P]) for i in range(2)]
        qz = [s.sb(f"qz{i}", [P, KH, HEADS // KH, P]) for i in range(2)]
        qb = s.sb("qb", [P, KH, 2, P], BF16)
        kb = s.sb("kb", [P, KH, P], BF16)
        v1 = [s.sb(f"v1{i}", [P, HEADS, DK + 1]) for i in range(2)]
        top = s.sb("top", [P, HEADS])
        neg_top = s.sb("neg_top", [P, 4, 32], BF16)
        ntT = s.sb("ntT", [P, P], BF16)
        prob = [s.sb(f"prob{i}", [P, HEADS, P]) for i in range(2)]
        inv_sum = s.sb("inv_sum", [P, HEADS])
        mix = s.sb("mix", [P, HEADS, DK])
        mixT = s.sb("mixT", [P, KH, P])
        res = s.sb("res", [P, D])
        o_stats = s.sb("o_stats", [P, 1, 6])
        o_part = s.sb("o_part", [P, 4, 1])
        o_mean = s.sb("o_mean", [P, 1])
        o_var = s.sb("o_var", [P, 1])
        o_lnv = s.sb("o_lnv", [P, 1])
        o_rstd = s.sb("o_rstd", [P, 1])
        row = [s.sb(f"row{i}", [P, ROW]) for i in range(2)]
        x2T = s.sb("x2T", [P, KH, P])
        g_exp = s.sb("g_exp", [P, EXPERTS])
        g_den = s.sb("g_den", [P, EXPERTS])
        ident_bf = s.sb("ident_bf", [P, P], BF16)

        turn_ps = s.ps("turn", [P, 512])
        q_ps = s.ps("q", [P, D])
        kv_ps = s.ps("kv", [P, 2 * D])
        s_ps = [s.ps(f"s{j}", [P, 512]) for j in range(4)]
        o_ps = s.ps("o", [P, 512])

        names = ("const_loaded set_up affine_ready x1b_ready x1_turned x1T_ready q_ready kv_ready qk_stats_ready qk_moments "
                 "qk_rstd_ready qk_lnv_ready v_ready qkn_ready qkn_turned qk_ready qk_seen qkb_ready s_ready top_done neg_ready nt_turned nt_ready "
                 "st_ready exp_done pv_done inv_ready mix_ready mix_turned mixT_ready o_ready res_ready o_stats_ready o_moments "
                 "o_lnv_ready o_rstd_ready x2_ready x2_turned x2T_ready g_ready g_exp_ready g_den_ready gate_ready").split()
        m = {n: s.sem(n) for n in names}
        ctx_loaded = [s.sem(f"ctx_loaded{i}") for i in range(2)]
        qz_moved = [s.sem(f"qz_moved{i}") for i in range(2)]
        row_stored = [s.sem(f"row_stored{i}") for i in range(2)]
        consts = 7
        LOOPED = (NT - 4) // 2

        def passes(eng, step):
            step(Seq(0, -1), "XA")
            step(Seq(0, 0), "XAB")
            step(Seq(0, 1), "XABC")
            with eng.Fori(0, LOOPED) as i:
                step(Seq(i, 2), "XABCD")
                step(Seq(i, 3), "XABCD")
            step(Seq(0, NT - 2), "ABCD")
            step(Seq(0, NT - 1), "BCD")
            step(Seq(0, NT), "CD")
            step(Seq(0, NT + 1), "D")

        with nc.Block() as block:

            @block.sync
            def _(sp):
                for sbuf, dram in ((w_q, w_q_dram), (w_kv, w_kv_dram), (w_o, w_o_dram), (w_g, w_g_dram),
                                   (norm, norm_dram), (even_odd, even_odd_dram), (pick, pick_dram)):
                    sp.dma_start(sbuf[:], dram).then_inc(m["const_loaded"], 16)

                def load_ctx(q):
                    since(sp, m["kv_ready"], q.b - 1)
                    sp.dma_start(ctxT[q.parity][:], ctxT_dram[:, :, ds(q.b * SEQ, SEQ)]).then_inc(ctx_loaded[q.parity], 16)

                def spread_queries(q):
                    sp.wait_ge(m["qk_ready"], q.b + 1)
                    for j in range(4):
                        rows = slice(32 * j, 32 * j + 32)
                        sp.dma_start(qz[q.parity][rows, :, 2 * j:2 * j + 2, :], qT[q.parity][rows]).then_inc(qz_moved[q.parity], 16)

                def store(q):
                    sp.wait_ge(m["gate_ready"], q.b + 1)
                    sp.dma_start(table_dram[ds(q.b * SEQ, SEQ), :], row[q.parity][:]).then_inc(row_stored[q.parity], 16)
                    sp.dma_start(acc_dram[ds(q.b * SEQ, SEQ), :], row[q.parity][:, 0:D]).then_inc(row_stored[q.parity], 16)

                def step(q, stages):
                    if "A" in stages:
                        load_ctx(q.plus(1))
                    if "D" in stages:
                        store(q.plus(-2))
                    if "A" in stages:
                        spread_queries(q.plus(1))

                sp.wait_ge(m["set_up"], 7)
                passes(sp, step)
                for r in row_stored:
                    sp.wait_ge(r, 32 * (NT // 2))

            @block.gpsimd
            def _(pool):
                for i in range(2):
                    pool.memset(v1[i][:], 1.0).then_inc(m["set_up"], 1)
                    pool.memset(qz[i][:], 0.0).then_inc(m["set_up"], 1)
                pool.memset(eps[:], EPS).then_inc(m["set_up"], 1)
                pool.memset(neg_top[:], 0.0).then_inc(m["set_up"], 1)
                pool.tensor_copy(ident_bf[:], ident[:]).then_inc(m["set_up"], 1)

                def copy_x1(q):
                    since(pool, m["x1_turned"], q.b - 1)
                    pool.tensor_copy(x1b[q.parity][:], x1[:, ds(GB + q.b, 1), :].rearrange("p o d -> p (o d)")).then_inc(m["x1b_ready"], 1)

                def round_qk(q):
                    pool.wait_ge(m["qk_ready"], q.b + 1)
                    pool.sem_inc(m["qk_seen"], 1)
                    pool.tensor_copy(kb[:], kT[q.parity][:])
                    pool.tensor_copy(qb[:], qT[q.parity][:]).then_inc(m["qkb_ready"], 1)

                def step(q, stages):
                    if "X" in stages:
                        copy_x1(q.plus(2))
                    if "A" in stages:
                        round_qk(q.plus(1))

                copy_x1(Seq(0, 0))
                passes(pool, step)

            @block.tensor
            def _(pe):
                def turn_x1(q):
                    pe.wait_ge(m["x1b_ready"], q.b + 1)
                    since(pe, m["qk_ready"], q.b)
                    for k in range(KH):
                        last = pe.transpose(turn_ps[:, k * P:(k + 1) * P], x1b[q.parity][:, k * P:(k + 1) * P], ident[:])
                    last.then_inc(m["x1_turned"], 1)

                def project_q(q):
                    pe.wait_ge(m["x1T_ready"], q.b + 1)
                    since(pe, m["qkn_ready"], q.b)
                    for k in range(KH):
                        last = pe.matmul(q_ps[:], x1T[:, k, :], w_q[:, k, :], start=(k == 0), stop=(k == KH - 1))
                    last.then_inc(m["q_ready"], 1)

                def project_kv(q, k):
                    if k == 0:
                        pe.wait_ge(ctx_loaded[q.parity], 16 * (q.half + 1))
                        since(pe, m["v_ready"], q.b)
                    last = pe.matmul(kv_ps[:], ctxT[q.parity][:, k, :], w_kv[:, k, :], start=(k == 0), stop=(k == KH - 1))
                    if k == KH - 1:
                        last.then_inc(m["kv_ready"], 1)

                def turn_qk(q):
                    pe.wait_ge(m["qkn_ready"], q.b + 1)
                    since(pe, m["nt_ready"], q.b)
                    for i in range(2):
                        for k in range(KH):
                            c = (i * KH + k) * P
                            last = pe.transpose(turn_ps[:, c:c + P], qkn[:, i, k * P:(k + 1) * P], ident[:])
                    last.then_inc(m["qkn_turned"], 1)

                def scores(q):
                    pe.wait_ge(m["qkb_ready"], q.b + 1)
                    since(pe, m["exp_done"], 4 * q.b)
                    for k in range(KH):
                        for e in range(2):
                            c = (2 * k + e) * P
                            for j in range(4):
                                rows = slice(32 * j, 32 * j + 32)
                                last = pe.matmul(s_ps[j][:, c:c + P], qb[rows, k, e, :], kb[rows, k, :], start=True, stop=True)
                                if k == KH - 1 and e == 1:
                                    last.then_inc(m["s_ready"], 1)

                def turn_top(q):
                    pe.wait_ge(m["neg_ready"], q.b + 1)
                    since(pe, m["g_exp_ready"], q.b - 1)
                    pe.transpose(turn_ps[:, 0:P // 2].bitcast(BF16), neg_top[:].rearrange("p j h -> p (j h)"), ident_bf[:]).then_inc(m["nt_turned"], 1)

                def shifted_scores(q, i):
                    k, h = i // 2, i % 2 * 4
                    if i == 0:
                        pe.wait_ge(m["nt_ready"], q.b + 1)
                        pe.wait_ge(qz_moved[q.parity], 64 * (q.half + 1))
                    pe.matmul(s_ps[i][:], kT[q.parity][:, k, :], qz[q.parity][:, k, h:h + 4, :].rearrange("p h t -> p (h t)"),
                              start=True, stop=True, skip_group_check=True)
                    for c in range(4):
                        last = pe.matmul(s_ps[i][:, c * P:(c + 1) * P], pick[:, 4 * i + c, :], ntT[:], start=False, stop=True,
                                         skip_group_check=True)
                    last.then_inc(m["st_ready"], 1)

                def mix_values(q, pair):
                    if pair == 0:
                        since(pe, m["res_ready"], q.b)
                        pe.wait_ge(m["v_ready"], q.b + 1)
                    if pair % 2 == 0:
                        pe.wait_ge(m["exp_done"], 4 * q.b + pair // 2 + 1)
                    for h in (2 * pair, 2 * pair + 1):
                        last = pe.matmul(o_ps[:, h * (DK + 1):(h + 1) * (DK + 1)], prob[q.parity][:, h, :],
                                         v1[q.parity][:, h, :], start=True, stop=True)
                    if 2 * pair == HEADS - 2:
                        last.then_inc(m["pv_done"], 1)

                def turn_mix(q):
                    pe.wait_ge(m["mix_ready"], q.b + 1)
                    for k in range(KH):
                        last = pe.transpose(o_ps[:, k * P:(k + 1) * P], mix[:, 8 * k:8 * k + 8, :].rearrange("p h d -> p (h d)"), ident[:])
                    last.then_inc(m["mix_turned"], 1)

                def project_out(q):
                    pe.wait_ge(m["mixT_ready"], q.b + 1)
                    for k in range(KH):
                        last = pe.matmul(o_ps[:, D:2 * D], mixT[:, k, :], w_o[:, k, :], start=(k == 0), stop=(k == KH - 1))
                    last.then_inc(m["o_ready"], 1)

                def turn_x2(q):
                    pe.wait_ge(m["x2_ready"], q.b + 1)
                    pe.wait_ge(m["x1T_ready"], min(q.b + 4, NT) if isinstance(q.b, int) else q.b + 4)
                    for k in range(KH):
                        last = pe.transpose(turn_ps[:, (KH + k) * P:(KH + k + 1) * P], row[q.parity][:, k * P:(k + 1) * P], ident[:])
                    last.then_inc(m["x2_turned"], 1)

                def gates(q):
                    pe.wait_ge(m["x2T_ready"], q.b + 1)
                    for k in range(KH):
                        last = pe.matmul(turn_ps[:, 0:EXPERTS], x2T[:, k, :], w_g[:, k, :], start=(k == 0), stop=(k == KH - 1))
                    last.then_inc(m["g_ready"], 1)

                def step(q, stages):
                    n, p, g = q.plus(1), q.plus(-1), q.plus(-2)
                    if "A" in stages:
                        turn_x1(n)
                    if "C" in stages:
                        mix_values(p, 0)
                    if "A" in stages:
                        project_q(n)
                    if "B" in stages:
                        scores(q)
                    if "C" in stages:
                        mix_values(p, 1)
                    if "A" in stages:
                        project_kv(n, 0)
                    if "C" in stages:
                        mix_values(p, 2)
                    if "A" in stages:
                        project_kv(n, 1)
                    if "C" in stages:
                        mix_values(p, 3)
                    if "D" in stages:
                        turn_x2(g)
                    if "C" in stages:
                        mix_values(p, 4)
                        mix_values(p, 5)
                    if "D" in stages:
                        gates(g)
                    if "C" in stages:
                        mix_values(p, 6)
                    if "B" in stages:
                        turn_top(q)
                    if "C" in stages:
                        mix_values(p, 7)
                    if "B" in stages:
                        shifted_scores(q, 0)
                    if "A" in stages:
                        turn_qk(n)
                    if "B" in stages:
                        shifted_scores(q, 1)
                    if "C" in stages:
                        turn_mix(p)
                    if "B" in stages:
                        shifted_scores(q, 2)
                    if "C" in stages:
                        project_out(p)
                    if "B" in stages:
                        shifted_scores(q, 3)

                pe.wait_ge(m["const_loaded"], 16 * consts)
                pe.wait_ge(m["set_up"], 7)
                passes(pe, step)

            @block.scalar
            def _(act):
                nc.scalar.preload_act_table_set("natural_log_exp_and_others")

                def inv_std(q, var, moments, lnv, lnv_ready, rstd, rstd_ready):
                    act.wait_ge(moments, 3 * (q.b + 1))
                    act.activation(lnv[:], var[:], ACT.Ln, bias=eps[:, 0:1]).then_inc(lnv_ready, 1)
                    act.wait_ge(lnv_ready, q.b + 1)
                    act.activation(rstd[:], lnv[:], ACT.Exp, scale=-0.5).then_inc(rstd_ready, 1)

                def copy_turned(q, turned, bank, k, out, ready):
                    act.wait_ge(turned, q.b + 1)
                    act.activation(out[:].rearrange("p k t -> p (k t)"), bank[:, k * P:(k + KH) * P], ACT.Copy).then_inc(ready, 1)

                def scale_qk(q):
                    act.wait_ge(m["qkn_turned"], q.b + 1)
                    for k in range(KH):
                        for e in range(2):
                            act.activation(qT[q.parity][:, k, e, :], turn_ps[:, k * P:(k + 1) * P], ACT.Identity,
                                           bias=affine[:, 1, e, k:k + 1], scale=affine[:, 0, e, k:k + 1])
                        c = (KH + k) * P
                        last = act.activation(kT[q.parity][:, k, :], turn_ps[:, c:c + P], ACT.Identity,
                                              bias=norm[:, 1, k:k + 1], scale=norm[:, 0, k:k + 1])
                    last.then_inc(m["qk_ready"], 1)

                def copy_top(q):
                    act.wait_ge(m["nt_turned"], q.b + 1)
                    act.activation(ntT[:], turn_ps[:, 0:P // 2].bitcast(BF16), ACT.Copy).then_inc(m["nt_ready"], 1)

                def exps(q, j):
                    if j == 0:
                        since(act, m["pv_done"], q.b - 1)
                    act.wait_ge(m["st_ready"], 4 * q.b + j + 1)
                    act.activation(prob[q.parity][:, 4 * j:4 * j + 4, :].rearrange("p h q -> p (h q)"), s_ps[j][:], ACT.Exp,
                                   scale=DK ** -0.5).then_inc(m["exp_done"], 1)

                def gate_exp(q):
                    act.wait_ge(m["g_ready"], q.b + 1)
                    since(act, m["g_den_ready"], q.b)
                    act.activation(g_exp[:], turn_ps[:, 0:EXPERTS], ACT.Exp, scale=-1.0).then_inc(m["g_exp_ready"], 1)

                def step(q, stages):
                    n, p, g = q.plus(1), q.plus(-1), q.plus(-2)
                    if "A" in stages:
                        copy_turned(n, m["x1_turned"], turn_ps, 0, x1T, m["x1T_ready"])
                    if "D" in stages:
                        inv_std(g, o_var, m["o_moments"], o_lnv, m["o_lnv_ready"], o_rstd, m["o_rstd_ready"])
                        copy_turned(g, m["x2_turned"], turn_ps, KH, x2T, m["x2T_ready"])
                        gate_exp(g)
                    if "B" in stages:
                        copy_top(q)
                    if "A" in stages:
                        inv_std(n, qk_var, m["qk_moments"], qk_lnv, m["qk_lnv_ready"], qk_rstd, m["qk_rstd_ready"])
                    if "B" in stages:
                        exps(q, 0)
                    if "A" in stages:
                        scale_qk(n)
                    if "C" in stages:
                        copy_turned(p, m["mix_turned"], o_ps, 0, mixT, m["mixT_ready"])
                    if "B" in stages:
                        exps(q, 1)
                        exps(q, 2)
                        exps(q, 3)

                act.wait_ge(m["const_loaded"], 16 * consts)
                act.wait_ge(m["affine_ready"], 4)
                act.wait_ge(m["set_up"], 7)
                passes(act, step)

            @block.vector
            def _(dve):
                def moments(q):
                    since(dve, m["qk_rstd_ready"], q.b)
                    dve.wait_ge(m["q_ready"], q.b + 1)
                    dve.bn_stats(qk_stats[:, 0, :], q_ps[:])
                    dve.wait_ge(m["kv_ready"], q.b + 1)
                    dve.bn_stats(qk_stats[:, 1, :], kv_ps[:, 0:D]).then_inc(m["qk_stats_ready"], 1)
                    merge_moments(dve, qk_stats, m["qk_stats_ready"], q.b + 1, qk_part, qk_mean, qk_var, m["qk_moments"], q.b)

                def normalise_qk(q):
                    dve.wait_ge(m["qk_rstd_ready"], q.b + 1)
                    since(dve, m["qkn_turned"], q.b)
                    dve.tensor_scalar(qkn[:, 0, :], q_ps[:], qk_mean[:, 0:1], qk_rstd[:, 0:1], ALU.subtract, ALU.mult)
                    dve.tensor_scalar(qkn[:, 1, :], kv_ps[:, 0:D], qk_mean[:, 1:2], qk_rstd[:, 1:2], ALU.subtract,
                                      ALU.mult).then_inc(m["qkn_ready"], 1)

                def copy_values(q):
                    since(dve, m["pv_done"], q.b - 1)
                    dve.tensor_copy(v1[q.parity][:, :, 0:DK], kv_ps[:, D:2 * D].rearrange("p (h d) -> p h d", d=DK)).then_inc(m["v_ready"], 1)

                def maximum(q, j):
                    dve.wait_ge(m["s_ready"], 4 * q.b + j + 1)
                    dve.tensor_reduce(top[:, 4 * j:4 * j + 4], s_ps[j][:].rearrange("p (h k) -> p h k", k=P), AX.X,
                                      ALU.max).then_inc(m["top_done"], 1)

                def negate(q):
                    dve.wait_ge(m["top_done"], 4 * (q.b + 1))
                    dve.tensor_scalar(neg_top[:, :, 0:4], top[:].rearrange("p (j h) -> p j h", h=4), -1.0, None, ALU.mult).then_inc(m["neg_ready"], 1)

                def divide(q):
                    dve.wait_ge(m["pv_done"], q.b + 1)
                    pv = o_ps[:, 0:HEADS * (DK + 1)].rearrange("p (h d) -> p h d", d=DK + 1)
                    dve.reciprocal(inv_sum[:], pv[:, :, DK]).then_inc(m["inv_ready"], 1)
                    dve.wait_ge(m["inv_ready"], q.b + 1)
                    dve.tensor_tensor(mix[:], pv[:, :, 0:DK], inv_sum[:].unsqueeze(2).broadcast_to([P, HEADS, DK]),
                                      ALU.mult).then_inc(m["mix_ready"], 1)

                def residual(q):
                    dve.wait_ge(m["o_ready"], q.b + 1)
                    dve.tensor_tensor(res[:], o_ps[:, D:2 * D], x1[:, ds(GB + q.b, 1), :].rearrange("p o d -> p (o d)"),
                                      ALU.add).then_inc(m["res_ready"], 1)
                    dve.wait_ge(m["res_ready"], q.b + 1)
                    dve.bn_stats(o_stats[:, 0, :], res[:]).then_inc(m["o_stats_ready"], 1)
                    merge_moments(dve, o_stats, m["o_stats_ready"], q.b + 1, o_part, o_mean, o_var, m["o_moments"], q.b)

                def normalise(q):
                    dve.wait_ge(m["o_rstd_ready"], q.b + 1)
                    since(dve, row_stored[q.parity], 32 * q.half)
                    dve.tensor_scalar(row[q.parity][:, 0:D], res[:], o_mean[:, 0:1], o_rstd[:, 0:1], ALU.subtract,
                                      ALU.mult).then_inc(m["x2_ready"], 1)

                def sigmoid(q):
                    dve.wait_ge(m["g_exp_ready"], q.b + 1)
                    dve.tensor_scalar(g_den[:], g_exp[:], 1.0, None, ALU.add).then_inc(m["g_den_ready"], 1)
                    dve.wait_ge(m["g_den_ready"], q.b + 1)
                    dve.reciprocal(row[q.parity][:, D:D + EXPERTS], g_den[:])
                    dve.reciprocal(gate_all[:, q.parity, :, ds(q.half, 1)].rearrange("p e o -> p (e o)"), g_den[:]).then_inc(m["gate_ready"], 1)

                def step(q, stages):
                    n, p, g = q.plus(1), q.plus(-1), q.plus(-2)
                    if "D" in stages:
                        normalise(g)
                    if "B" in stages:
                        maximum(q, 0)
                        maximum(q, 1)
                        maximum(q, 2)
                        maximum(q, 3)
                        negate(q)
                    if "A" in stages:
                        moments(n)
                        normalise_qk(n)
                    if "C" in stages:
                        divide(p)
                    if "A" in stages:
                        copy_values(n)
                    if "D" in stages:
                        sigmoid(g)
                    if "C" in stages:
                        residual(p)

                dve.wait_ge(m["const_loaded"], 16 * consts)
                for i in range(2):
                    for e in range(2):
                        dve.tensor_scalar(affine[:, i, e, :], norm[:, i, :], even_odd[:, e:e + 1], None, ALU.mult).then_inc(m["affine_ready"], 1)
                dve.wait_ge(m["set_up"], 7)
                passes(dve, step)



def choose_phase(nc, ident, gate_all, lists_dram, bits_i_dram, bits_f_dram, same_dram, before_dram, iota_dram, place_dram):
    CH = P // EXPERTS
    J = T // CH
    NBITS = 30
    LO = 32
    HI = TOPK // LO
    M = 2 * P
    with ExitStack() as ctx:
        s = Scope(nc, ctx, "choose")
        bits_i = s.sb("bits_i", [P, NBITS + 1], I32)
        bits_f = s.sb("bits_f", [P, NBITS])
        same = s.sb("same", [P, P])
        before = s.sb("before", [P, P])
        iota = s.sb("iota", [P, LO])
        place = s.sb("place", [P, 1 + 2 * 16])
        gate = s.sb("gate", [P, J])
        hit = s.sb("hit", [P, J])
        count = s.sb("count", [P, 1])
        limit = s.sb("limit", [P, 1], I32)
        trial = s.sb("trial", [P, 1], I32)
        gain = s.sb("gain", [P, 1], I32)
        above = s.sb("above", [P, J])
        n_above = s.sb("n_above", [P, 1])
        equal = s.sb("equal", [P, J])
        ones = s.sb("ones", [P, J])
        cum = s.sb("cum", [P, J])
        room = s.sb("room", [P, 1])
        start = s.sb("start", [P, 1])
        taken = s.sb("taken", [P, J])
        chosen = s.sb("chosen", [P, J])
        cum2 = s.sb("cum2", [P, J])
        start2 = s.sb("start2", [P, 1])
        slot = s.sb("slot", [P, J])
        slot_i = s.sb("slot_i", [P, J], I32)
        part_i = s.sb("part_i", [P, 2, J], I32)
        part_f = s.sb("part_f", [P, 2, J])
        turned = s.sb("turned", [P, 2, M])
        hi_hot = s.sb("hi_hot", [P, M, HI], BF16)
        lo_hot = s.sb("lo_hot", [P, M, LO], BF16)
        lo_val = s.sb("lo_val", [P, M, 2, LO], BF16)
        tiles = s.sb("tiles", [P, EXPERTS, 2, LO])
        token = s.sb("token", [HI, EXPERTS, LO], I32)

        gate_ps = s.ps("gate", [P, J])
        count_ps = s.ps("count", [P, 4])
        turn_ps = s.ps("turn", [P, 2 * M])
        list_ps = s.ps("list", [HI, EXPERTS, 2 * LO])

        loaded = s.sem("loaded")
        gate_turned = s.sem("gate_turned")
        started = s.sem("started")
        counted = s.sem("counted")
        totalled = s.sem("totalled")
        stepped = s.sem("stepped")
        chain = s.sem("chain")
        stage = s.sem("stage")
        above_summed = s.sem("above_summed")
        starts_ready = s.sem("starts_ready")
        starts2_ready = s.sem("starts2_ready")
        parts_turned = s.sem("parts_turned")
        turned_ready = s.sem("turned_ready")
        hi_ready = s.sem("hi_ready")
        lo_ready = s.sem("lo_ready")
        list_ready = s.sem("list_ready")
        token_ready = s.sem("token_ready")
        list_stored = s.sem("list_stored")

        with nc.Block() as block:

            @block.sync
            def _(sp):
                for sbuf, dram in ((same, same_dram), (bits_i, bits_i_dram), (bits_f, bits_f_dram), (before, before_dram),
                                   (iota, iota_dram), (place, place_dram)):
                    sp.dma_start(sbuf[:], dram).then_inc(loaded, 16)
                sp.wait_ge(token_ready, 1)
                sp.dma_start(lists_dram.rearrange("e (h l) -> h e l", l=LO), token[:]).then_inc(list_stored, 16)
                sp.wait_ge(list_stored, 16)

            @block.tensor
            def _(pe):
                for par in range(2):
                    last = pe.transpose(gate_ps[:, par * P:(par + 1) * P], gate_all[:, par, :, :].rearrange("p e c -> p (e c)"), ident[:])
                last.then_inc(gate_turned, 1)
                pe.wait_ge(loaded, 16 * 6)
                with pe.Fori(0, NBITS) as i:
                    pe.wait_ge(counted, i + 1)
                    pe.matmul(count_ps[:, 0:1], same[:], count[:], start=True, stop=True).then_inc(totalled, 1)
                pe.wait_ge(stage, 3)
                pe.matmul(count_ps[:, 0:1], same[:], n_above[:], start=True, stop=True).then_inc(above_summed, 1)
                pe.wait_ge(stage, 4)
                pe.matmul(count_ps[:, 1:2], before[:], cum[:, J - 1:J], start=True, stop=True).then_inc(starts_ready, 1)
                pe.wait_ge(stage, 8)
                pe.matmul(count_ps[:, 2:3], before[:], cum2[:, J - 1:J], start=True, stop=True).then_inc(starts2_ready, 1)
                pe.wait_ge(stage, 13)
                for h in range(2):
                    for par in range(2):
                        c = (2 * h + par) * P
                        last = pe.transpose(turn_ps[:, c:c + P], part_f[:, h, par * P:(par + 1) * P], ident[:])
                last.then_inc(parts_turned, 1)
                pe.wait_ge(hi_ready, 1)
                pe.wait_ge(lo_ready, 3)
                for e in range(EXPERTS):
                    for par in range(2):
                        for c in range(CH):
                            col = par * P + e * CH + c
                            last = pe.matmul(list_ps[:, e, :], hi_hot[:, col, :], lo_val[:, col, :, :],
                                             start=(par == 0 and c == 0), stop=(par == 1 and c == CH - 1))
                last.then_inc(list_ready, 1)

            @block.gpsimd
            def _(pool):
                pool.memset(ones[:], 1.0).then_inc(started, 1)

            @block.vector
            def _(dve):
                dve.memset(limit[:], 0)
                dve.wait_ge(loaded, 16 * 6)
                dve.tensor_copy(trial[:], bits_i[:, 0:1])
                dve.wait_ge(gate_turned, 1)
                dve.tensor_copy(gate[:], gate_ps[:]).then_inc(stepped, 1)
                with dve.Fori(0, NBITS) as i:
                    dve.wait_ge(stepped, i + 1)
                    dve.tensor_scalar(hit[:], gate[:], trial[:].bitcast(F32), None, ALU.is_ge, ALU.add, accum_out=count[:]).then_inc(counted, 1)
                    dve.wait_ge(totalled, i + 1)
                    dve.tensor_scalar(gain[:], count_ps[:, 0:1], float(TOPK), bits_f[:, ds(i, 1)], ALU.is_ge, ALU.mult).then_inc(chain, 1)
                    dve.wait_ge(chain, 2 * i + 1)
                    dve.tensor_tensor(limit[:], limit[:], gain[:], ALU.bitwise_or).then_inc(chain, 1)
                    dve.wait_ge(chain, 2 * i + 2)
                    dve.tensor_tensor(trial[:], limit[:], bits_i[:, ds(i + 1, 1)], ALU.bitwise_or).then_inc(stepped, 1)
                dve.wait_ge(stepped, NBITS + 1)
                dve.tensor_scalar(above[:], gate[:], trial[:].bitcast(F32), None, ALU.is_gt, ALU.add, accum_out=n_above[:]).then_inc(stage, 3)
                dve.tensor_scalar(equal[:], gate[:], trial[:].bitcast(F32), None, ALU.is_equal).then_inc(started, 1)
                dve.wait_ge(started, 2)
                dve.tensor_tensor_scan(cum[:], ones[:], equal[:], 0.0, ALU.mult, ALU.add).then_inc(stage, 1)
                dve.wait_ge(above_summed, 1)
                dve.wait_ge(starts_ready, 1)
                dve.tensor_scalar(room[:], count_ps[:, 0:1], -1.0, float(TOPK), ALU.mult, ALU.add)
                dve.tensor_copy(start[:], count_ps[:, 1:2]).then_inc(stage, 1)
                dve.wait_ge(stage, 5)
                dve.tensor_scalar(taken[:], cum[:], start[:, 0:1], room[:, 0:1], ALU.add, ALU.is_le).then_inc(stage, 1)
                dve.wait_ge(stage, 6)
                dve.tensor_tensor(equal[:], equal[:], taken[:], ALU.mult).then_inc(stage, 1)
                dve.wait_ge(stage, 7)
                dve.tensor_tensor(chosen[:], above[:], equal[:], ALU.add).then_inc(started, 1)
                dve.wait_ge(started, 3)
                dve.tensor_tensor_scan(cum2[:], ones[:], chosen[:], 0.0, ALU.mult, ALU.add).then_inc(stage, 1)
                dve.wait_ge(starts2_ready, 1)
                dve.tensor_copy(start2[:], count_ps[:, 2:3]).then_inc(stage, 1)
                dve.wait_ge(stage, 9)
                dve.scalar_tensor_tensor(slot[:], cum2[:], start2[:, 0:1], chosen[:], ALU.add, ALU.mult).then_inc(stage, 1)
                dve.wait_ge(stage, 10)
                dve.tensor_scalar(slot_i[:], slot[:], -1.0, None, ALU.add).then_inc(stage, 1)
                dve.wait_ge(stage, 11)
                dve.tensor_scalar(part_i[:, 0, :], slot_i[:], 5, None, ALU.arith_shift_right)
                dve.tensor_scalar(part_i[:, 1, :], slot_i[:], LO - 1, None, ALU.bitwise_and).then_inc(stage, 1)
                dve.wait_ge(stage, 12)
                dve.tensor_copy(part_f[:], part_i[:]).then_inc(stage, 1)
                dve.wait_ge(parts_turned, 1)
                dve.tensor_copy(turned[:].rearrange("p h m -> p (h m)"), turn_ps[:]).then_inc(turned_ready, 1)
                dve.wait_ge(turned_ready, 1)
                dve.tensor_tensor(lo_hot[:], turned[:, 1, :].unsqueeze(2).broadcast_to([P, M, LO]),
                                  iota[:].unsqueeze(1).broadcast_to([P, M, LO]), ALU.is_equal).then_inc(lo_ready, 1)
                dve.tensor_tensor(hi_hot[:], turned[:, 0, :].unsqueeze(2).broadcast_to([P, M, HI]),
                                  iota[:].unsqueeze(1).broadcast_to([P, M, HI]), ALU.is_equal).then_inc(hi_ready, 1)
                dve.wait_ge(lo_ready, 1)
                dve.tensor_scalar(lo_val[:, :, 0, :], lo_hot[:], place[:, 0:1], None, ALU.mult).then_inc(lo_ready, 1)
                for par in range(2):
                    for e in range(EXPERTS):
                        col = par * P + e * CH
                        last = dve.tensor_tensor(lo_val[:, col:col + CH, 1, :], lo_hot[:, col:col + CH, :],
                                                 place[:, 1 + par * CH:1 + (par + 1) * CH].unsqueeze(2).broadcast_to([P, CH, LO]), ALU.mult)
                last.then_inc(lo_ready, 1)
                dve.wait_ge(list_ready, 1)
                dve.tensor_copy(tiles[:HI].rearrange("p e a l -> p e (a l)"), list_ps[:]).then_inc(stepped, 1)
                dve.wait_ge(stepped, NBITS + 2)
                dve.scalar_tensor_tensor(token[:], tiles[:HI, :, 1, :], float(P), tiles[:HI, :, 0, :], ALU.mult, ALU.add).then_inc(token_ready, 1)


class Half:

    def __init__(self, pair, number):
        self.pair, self.number = pair + number // 4, number % 4
        self.parity = self.number // 2
        self.part = self.number % 2
        self.expert = 2 * self.pair + self.parity
        self.u = 4 * self.pair + self.number


def expert_phase(nc, ident, lists_dram, table_dram, acc_dram, w1_dram, b1_dram, w2_dram, b2_dram):
    FT = FF // P
    ST = TOPK // P
    HS = ST // 2
    W = HS * P
    with ExitStack() as ctx:
        s = Scope(nc, ctx, "expert")
        lists = s.sb("lists", [P, EXPERTS, ST], I32)
        lst = [s.sb(f"lst{i}", [P, ST], I32) for i in range(2)]
        w1 = [s.sb(f"w1{i}", [P, KH, FF]) for i in range(2)]
        b1 = [s.sb(f"b1{i}", [P, FT]) for i in range(2)]
        w2 = [s.sb(f"w2{i}", [P, FT, D]) for i in range(2)]
        b2 = [s.sb(f"b2{i}", [1, D]) for i in range(2)]
        one = s.sb("one", [1, P])
        xg = [s.sb(f"xg{i}", [P, ST, ROW]) for i in range(2)]
        gate = [s.sb(f"gate{i}", [P, ST]) for i in range(2)]
        xgT = [s.sb(f"xgT{i}", [P, KH, TOPK]) for i in range(2)]
        hid = [s.sb(f"hid{i}", [P, FT, W]) for i in range(2)]
        rows = [s.sb(f"rows{i}", [P, ST, D]) for i in range(2)]

        h_ps = [s.ps(f"h{i}", [P, W]) for i in range(4)]
        o_ps = [s.ps(f"o{i}", [P, D]) for i in range(2)]
        t_ps = [s.ps(f"t{i}", [P, W]) for i in range(2)]

        lists_loaded = s.sem("lists_loaded")
        set_up = s.sem("set_up")
        w_loaded = [s.sem(f"w_loaded{i}") for i in range(2)]
        gathered = [s.sem(f"gathered{i}") for i in range(2)]
        scattered = [s.sem(f"scattered{i}") for i in range(2)]
        lst_ready = s.sem("lst_ready")
        turned = s.sem("turned")
        xgT_ready = s.sem("xgT_ready")
        gate_ready = s.sem("gate_ready")
        h_ready = s.sem("h_ready")
        hid_ready = s.sem("hid_ready")
        o_ready = s.sem("o_ready")
        rows_ready = s.sem("rows_ready")
        waited = s.sem("waited")
        PAIRS = EXPERTS // 2
        LAST = 4 * PAIRS - 1

        with nc.Block() as block:

            @block.sync
            def _(sp):
                sp.dma_start(lists[:], lists_dram.rearrange("e (p s) -> p e s", s=ST)).then_inc(lists_loaded, 16)

                def load(pair, par, first=False):
                    e = 2 * pair + par
                    if not first:
                        sp.wait_ge(o_ready, ST * (e - 1))
                    for sbuf, dram in ((w1[par], w1_dram), (b1[par], b1_dram), (w2[par], w2_dram), (b2[par], b2_dram)):
                        src = dram[ds(e, 1)]
                        src = src.rearrange("o p a b -> (o p) a b") if len(dram.shape) == 4 else (
                            src.rearrange("o p a -> (o p) a") if len(dram.shape) == 3 else src)
                        sp.dma_start(sbuf[:], src).then_inc(w_loaded[par], 16)

                load(0, 0, first=True)
                load(0, 1, first=True)
                with sp.Fori(1, PAIRS) as i:
                    load(i, 0)
                    load(i, 1)

            @block.gpsimd
            def _(pool):
                def gather(pair, par, first=False):
                    e = 2 * pair + par
                    if not first:
                        pool.wait_ge(scattered[par], 16 * ST * pair)
                        pool.wait_ge(turned, 4 * (e - 1))
                        pool.wait_ge(gate_ready, e - 1)
                    pool.tensor_copy(lst[par][:], lists[:, ds(e, 1), :].rearrange("p o s -> p (o s)")).then_inc(lst_ready, 1)
                    pool.wait_ge(lst_ready, e + 1)
                    pool.sem_inc(waited, 1)
                    for t in range(ST):
                        pool.indirect_dma_start(out=xg[par][:, t, :], out_offset=None, in_=table_dram,
                                                in_offset=bass.IndirectOffsetOnAxis(ap=lst[par][:, t:t + 1], axis=0)
                                                ).then_inc(gathered[par], 16)

                def scatter(pair, par):
                    e = 2 * pair + par
                    for t in range(ST):
                        pool.wait_ge(rows_ready, ST * e + t + 1)
                        if t == 0:
                            if par == 0:
                                since(pool, scattered[1], 16 * ST * pair)
                            else:
                                pool.wait_ge(scattered[0], 16 * ST * (pair + 1))
                        pool.sem_inc(waited, 1)
                        pool.indirect_dma_start(out=acc_dram, out_offset=bass.IndirectOffsetOnAxis(ap=lst[par][:, t:t + 1], axis=0),
                                                in_=rows[par][:, t, :], in_offset=None, compute_op=ALU.add
                                                ).then_inc(scattered[par], 16)

                pool.memset(one[:], 1.0).then_inc(set_up, 1)
                pool.wait_ge(lists_loaded, 16)
                gather(0, 0, first=True)
                gather(0, 1, first=True)
                scatter(0, 0)
                with pool.Fori(1, PAIRS) as i:
                    gather(i, 0)
                    scatter(i - 1, 1)
                    gather(i, 1)
                    scatter(i, 0)
                scatter(PAIRS - 1, 1)
                for par in range(2):
                    pool.wait_ge(scattered[par], 16 * ST * PAIRS)

            @block.tensor
            def _(pe):
                def turn(pair, par):
                    e = 2 * pair + par
                    pe.wait_ge(gathered[par], 16 * ST * (pair + 1))
                    for part in range(2):
                        for k in range(KH):
                            n = 2 * part + k
                            since(pe, xgT_ready, 4 * e + n - 1)
                            for t in range(HS):
                                last = pe.transpose(t_ps[k][:, t * P:(t + 1) * P], xg[par][:, HS * part + t, k * P:(k + 1) * P], ident[:])
                            last.then_inc(turned, 1)

                def first(h):
                    if h.part == 0:
                        pe.wait_ge(w_loaded[h.parity], 64 * (h.pair + 1))
                    pe.wait_ge(xgT_ready, 4 * h.expert + 2 * h.part + 2)
                    for f in range(FT):
                        since(pe, hid_ready, FT * h.u + f - 3)
                        for k in range(KH):
                            last = pe.matmul(h_ps[f % 4][:], w1[h.parity][:, k, f * P:(f + 1) * P],
                                             xgT[h.parity][:, k, h.part * W:(h.part + 1) * W], start=(k == 0), stop=(k == KH - 1))
                        last.then_inc(h_ready, 1)

                def second(h):
                    pe.wait_ge(hid_ready, FT * (h.u + 1))
                    for t in range(HS):
                        since(pe, rows_ready, HS * h.u + t - 1)
                        pe.matmul(o_ps[t % 2][:], one[:], b2[h.parity][:], start=True, stop=False)
                        for f in range(FT):
                            last = pe.matmul(o_ps[t % 2][:], hid[h.part][:, f, t * P:(t + 1) * P], w2[h.parity][:, f, :],
                                             start=False, stop=(f == FT - 1))
                        last.then_inc(o_ready, 1)

                def pair(i, last=False):
                    for n in range(4):
                        if not (last and n == 3):
                            first(Half(i, n + 1))
                        if n % 2 == 0 and not (last and n == 2):
                            turn(i + n // 2, 1 - n // 2)
                        second(Half(i, n))

                pe.wait_ge(set_up, 1)
                turn(0, 0)
                first(Half(0, 0))
                pair(0)
                with pe.Fori(1, PAIRS - 1) as i:
                    pair(i)
                pair(PAIRS - 1, last=True)

            @block.scalar
            def _(act):
                nc.scalar.preload_act_table_set("gelu_and_others")

                def gelu(h):
                    if h.part == 0:
                        act.wait_ge(w_loaded[h.parity], 64 * (h.pair + 1))
                    since(act, o_ready, HS * (h.u - 1))
                    for f in range(FT):
                        act.wait_ge(h_ready, FT * h.u + f + 1)
                        act.activation(hid[h.part][:, f, :], h_ps[f % 4][:], ACT.Gelu, bias=b1[h.parity][:, f:f + 1]).then_inc(hid_ready, 1)

                for n in range(4):
                    gelu(Half(0, n))
                with act.Fori(1, PAIRS) as i:
                    for n in range(4):
                        gelu(Half(i, n))

            @block.vector
            def _(dve):
                def take(pair, par):
                    e = 2 * pair + par
                    dve.wait_ge(gathered[par], 16 * ST * (pair + 1))
                    dve.tensor_copy(gate[par][:], xg[par][:, :, ds(D + e, 1)].rearrange("p s o -> p (s o)")).then_inc(gate_ready, 1)
                    for n in range(4):
                        part, k = n // 2, n % 2
                        dve.wait_ge(turned, 4 * e + n + 1)
                        if n == 0:
                            since(dve, h_ready, 2 * FT * (e - 1))
                        dve.tensor_copy(xgT[par][:, k, part * W:(part + 1) * W], t_ps[k][:]).then_inc(xgT_ready, 1)

                def weigh(h):
                    if h.part == 0:
                        dve.wait_ge(gate_ready, h.expert + 1)
                        since(dve, scattered[h.parity], 16 * ST * h.pair)
                    for t in range(HS):
                        dve.wait_ge(o_ready, HS * h.u + t + 1)
                        n = HS * h.part + t
                        dve.tensor_scalar(rows[h.parity][:, n, :], o_ps[t % 2][:], gate[h.parity][:, n:n + 1], None,
                                          ALU.mult).then_inc(rows_ready, 1)

                def pair(i, last=False):
                    for n in range(4):
                        if n % 2 == 0 and not (last and n == 2):
                            take(i + n // 2, 1 - n // 2)
                        weigh(Half(i, n))

                take(0, 0)
                pair(0)
                with dve.Fori(1, PAIRS - 1) as i:
                    pair(i)
                pair(PAIRS - 1, last=True)


def final_phase(nc, acc_dram, out_dram):
    C = 8
    CHUNKS = T // (P * C)
    with ExitStack() as ctx:
        s = Scope(nc, ctx, "final")
        a = [s.sb(f"a{i}", [P, C, D]) for i in range(2)]
        o = [s.sb(f"o{i}", [P, C, D]) for i in range(2)]
        stats = s.sb("stats", [P, C, 6])
        part = s.sb("part", [P, 4, C])
        mean = s.sb("mean", [P, C])
        var = s.sb("var", [P, C])
        lnv = s.sb("lnv", [P, C])
        rstd = s.sb("rstd", [P, C])
        eps = s.sb("eps", [P, 1])
        loaded = [s.sem(f"loaded{i}") for i in range(2)]
        stored = [s.sem(f"stored{i}") for i in range(2)]
        stats_ready = s.sem("stats_ready")
        moments = s.sem("moments")
        lnv_ready = s.sem("lnv_ready")
        rstd_ready = s.sem("rstd_ready")
        normed = s.sem("normed")
        set_up = s.sem("set_up")

        def both(eng, step):
            step(0, 0)
            step(0, 1)
            with eng.Fori(1, CHUNKS // 2) as i:
                step(i, 0)
                step(i, 1)

        with nc.Block() as block:

            @block.sync
            def _(sp):
                def load(i, par):
                    c = 2 * i + par
                    since(sp, normed, c - 1)
                    sp.dma_start(a[par][:], acc_dram[ds(c * P * C, P * C), :].rearrange("(p t) d -> p t d", t=C)).then_inc(loaded[par], 16)

                both(sp, load)

            @block.scalar
            def _(act):
                def step(i, par):
                    c = 2 * i + par
                    act.wait_ge(moments, 3 * (c + 1))
                    act.activation(lnv[:], var[:], ACT.Ln, bias=eps[:, 0:1]).then_inc(lnv_ready, 1)
                    act.wait_ge(lnv_ready, c + 1)
                    since(act, normed, c)
                    act.activation(rstd[:], lnv[:], ACT.Exp, scale=-0.5).then_inc(rstd_ready, 1)
                    act.wait_ge(normed, c + 1)
                    act.dma_start(out_dram[ds(c * P * C, P * C), :].rearrange("(p t) d -> p t d", t=C), o[par][:]).then_inc(stored[par], 16)

                nc.scalar.preload_act_table_set("natural_log_exp_and_others")
                act.wait_ge(set_up, 1)
                both(act, step)
                for q in stored:
                    act.wait_ge(q, 16 * (CHUNKS // 2))

            @block.vector
            def _(dve):
                def step(i, par):
                    c = 2 * i + par
                    dve.wait_ge(loaded[par], 16 * (i + 1))
                    for t in range(C):
                        last = dve.bn_stats(stats[:, t, :], a[par][:, t, :])
                    last.then_inc(stats_ready, 1)
                    merge_moments(dve, stats, stats_ready, c + 1, part, mean, var, moments, c)
                    dve.wait_ge(rstd_ready, c + 1)
                    since(dve, stored[par], 16 * i)
                    for t in range(C):
                        last = dve.tensor_scalar(o[par][:, t, :], a[par][:, t, :], mean[:, t:t + 1], rstd[:, t:t + 1], ALU.subtract, ALU.mult)
                    last.then_inc(normed, 1)

                dve.memset(eps[:], EPS).then_inc(set_up, 1)
                both(dve, step)


def build(nc, xT, w_proj, w_bc, w_dt, b_dt, a_log, sel, ident_dram, ctxT, w_q, w_kv, w_o, w_g, norm, even_odd, pick,
          bits_i, bits_f, same, before, iota, place, w1, b1, w2, b2, out):
    table = nc.dram_tensor("table", (T, ROW), F32, kind="Internal").ap()
    acc = nc.dram_tensor("acc", (T, D), F32, kind="Internal").ap()
    lists = nc.dram_tensor("lists", (EXPERTS, TOPK), I32, kind="Internal").ap()
    with ExitStack() as ctx:
        s = Scope(nc, ctx, "all")
        ident = s.sb("ident", [P, P])
        gate_all = s.sb("gate_all", [P, 2, EXPERTS, NT // 2])
        with ExitStack() as front:
            x1 = Scope(nc, front, "front").sb("x1", [P, GB + NT, D])
            scan_phase(nc, x1, (ident, ident_dram), xT, w_proj, w_bc, w_dt, b_dt, a_log, sel)
            attention_phase(nc, x1, ident, gate_all, ctxT, w_q, w_kv, w_o, w_g, norm, even_odd, pick, table, acc)
        choose_phase(nc, ident, gate_all, lists, bits_i, bits_f, same, before, iota, place)
        expert_phase(nc, ident, lists, table, acc, w1, b1, w2, b2)
        final_phase(nc, acc, out)


def kernel(x, ctx_1024, L0_attn_W_xproj, L0_attn_W_dt, L0_attn_b_dt, L0_attn_A_log, L0_xattn_Wq, L0_xattn_Wk,
           L0_xattn_Wv, L0_xattn_Wo, L0_xattn_ln_gamma, L0_xattn_ln_beta, L0_ffn_Wg, L0_ffn_W1, L0_ffn_b1,
           L0_ffn_W2, L0_ffn_b2):
    import ml_dtypes
    import concourse.bacc as bacc
    from concourse.bass_utils import run_bass_kernel_spmd

    def halves(a):
        return np.ascontiguousarray(a.reshape(KH, P, -1).transpose(1, 0, 2))

    x = np.asarray(x)
    w_xproj = np.asarray(L0_attn_W_xproj)
    w_bc = np.concatenate([w_xproj[R:]] * 3, axis=0)
    sel = np.zeros((96, 2 * NS, P), ml_dtypes.bfloat16)
    for part in range(3):
        for n in range(2 * NS):
            sel[32 * part + n, n, :] = 1
    bits = np.array([1 << b for b in range(29, -1, -1)] + [0], np.int32)
    expert_of = np.arange(P) // (P // EXPERTS)
    same = expert_of[:, None] == expert_of[None, :]
    place = np.zeros((P, 1 + NT), np.float32)
    place[:, 0] = np.arange(P)
    for parity in range(2):
        place[:, 1 + parity * 16:1 + (parity + 1) * 16] = 2 * np.arange(16) + parity
    head_of = np.arange(P) // DK % 2
    even_odd = np.stack([head_of == 0, head_of == 1], axis=1).astype(np.float32)
    pick = np.zeros((P, HEADS, P), ml_dtypes.bfloat16)
    for h in range(HEADS):
        strip, k, e = h % 8 // 2, h // 8, h % 2
        pick[32 * strip + 2 * k + e, h, :] = 1
    arrays = {
        "xT": halves(x.reshape(T, D).T),
        "w_proj": halves(w_xproj[:R].T),
        "w_bc": halves(w_bc.T),
        "w_dt": np.ascontiguousarray(np.asarray(L0_attn_W_dt).T),
        "b_dt": np.ascontiguousarray(np.asarray(L0_attn_b_dt).reshape(KH, P).T),
        "a_log": halves(np.asarray(L0_attn_A_log)),
        "sel": sel,
        "ident": np.eye(P, dtype=np.float32),
        "ctxT": halves(np.asarray(ctx_1024).reshape(T, D).T),
        "w_q": halves(np.asarray(L0_xattn_Wq).T),
        "w_kv": halves(np.concatenate([np.asarray(L0_xattn_Wk).T, np.asarray(L0_xattn_Wv).T], axis=1)),
        "w_o": halves(np.asarray(L0_xattn_Wo).T),
        "w_g": halves(np.asarray(L0_ffn_Wg)),
        "norm": np.ascontiguousarray(np.stack([np.asarray(a).reshape(KH, P) for a in (L0_xattn_ln_gamma, L0_xattn_ln_beta)]).transpose(2, 0, 1)),
        "even_odd": even_odd,
        "pick": pick,
        "bits_i": np.tile(bits, (P, 1)),
        "bits_f": np.tile(bits[:-1].astype(np.float32), (P, 1)),
        "same": same.astype(np.float32),
        "before": (same & (np.arange(P)[:, None] < np.arange(P)[None, :])).astype(np.float32),
        "iota": np.tile(np.arange(32, dtype=np.float32), (P, 1)),
        "place": place,
        "w1": np.ascontiguousarray(np.asarray(L0_ffn_W1).reshape(EXPERTS, KH, P, FF).transpose(0, 2, 1, 3)),
        "b1": np.ascontiguousarray(np.asarray(L0_ffn_b1).reshape(EXPERTS, FF // P, P).transpose(0, 2, 1)),
        "w2": np.ascontiguousarray(np.asarray(L0_ffn_W2).reshape(EXPERTS, FF // P, P, D).transpose(0, 2, 1, 3)),
        "b2": np.ascontiguousarray(np.asarray(L0_ffn_b2)),
    }
    nc = bacc.Bacc("TRN2", target_bir_lowering=False, num_devices=1)
    args = [nc.dram_tensor(n, a.shape, mybir.dt.from_np(a.dtype), kind="ExternalInput").ap() for n, a in arrays.items()]
    out = nc.dram_tensor("out", (T, D), F32, kind="ExternalOutput").ap()
    build(nc, *args, out)
    r = run_bass_kernel_spmd(nc, [arrays], core_ids=[0])
    return np.asarray(r.results[0]["out"]).reshape(BATCH, SEQ, D)
```

```python
from contextlib import ExitStack

import numpy as np

import concourse.bass as bass
from concourse import mybir

F32 = mybir.dt.float32
BF16 = mybir.dt.bfloat16
F32R = mybir.dt.float32r
I32 = mybir.dt.int32
ALU = mybir.AluOpType
ACT = mybir.ActivationFunctionType
AX = mybir.AxisListType
ds = bass.ds

P = 128
BATCH, SEQ, D = 32, 128, 256
T = BATCH * SEQ
KH = D // P
NT = T // P
NS, R = 16, 64
HEADS, DK = 16, 16
EXPERTS, FF = 8, 1024
TOPK = min(max(int(T * 2 / EXPERTS), 1), T)
EPS = 1e-5
ROW = D + EXPERTS

GB = 4
GT = GB * SEQ
GROUPS = T // GT
RING = 4
STEPS = NS


def merge_moments(dve, stats, stats_ready, stats_count, part, mean, var, done, before):
    even, odd = stats[:, :, 1], stats[:, :, 4]
    dve.wait_ge(stats_ready, stats_count)
    dve.tensor_tensor(part[:, 0, :], even, odd, ALU.add)
    dve.tensor_tensor(part[:, 1, :], even, odd, ALU.subtract)
    dve.tensor_tensor(part[:, 2, :], stats[:, :, 2], stats[:, :, 5], ALU.add).then_inc(done, 1)
    dve.wait_ge(done, 3 * before + 1)
    dve.tensor_scalar(mean[:], part[:, 0, :], 0.5, None, ALU.mult)
    dve.scalar_tensor_tensor(part[:, 3, :], part[:, 1, :], 0.25, part[:, 1, :], ALU.mult, ALU.mult).then_inc(done, 1)
    dve.wait_ge(done, 3 * before + 2)
    dve.scalar_tensor_tensor(var[:], part[:, 2, :], 1.0 / D, part[:, 3, :], ALU.mult, ALU.add).then_inc(done, 1)


class Scope:

    def __init__(self, nc, ctx, tag):
        self.nc, self.ctx, self.tag = nc, ctx, tag

    def sb(self, name, shape, dt=F32):
        return self.ctx.enter_context(self.nc.sbuf_tensor(f"{self.tag}_{name}", shape, dt))

    def ps(self, name, shape, dt=F32):
        return self.ctx.enter_context(self.nc.psum_tensor(f"{self.tag}_{name}_ps", shape, dt))

    def sem(self, name):
        return self.ctx.enter_context(self.nc.semaphore(f"{self.tag}_{name}"))


def scan_phase(nc, x1, ident, xT_dram, w_proj_dram, w_bc_dram, w_dt_dram, b_dt_dram, a_log_dram, sel_dram, attention):
    with ExitStack() as ctx:
        s = Scope(nc, ctx, "scan")
        w_proj = s.sb("w_proj", [P, KH, R])
        w_bc = s.sb("w_bc", [P, KH, 96])
        w_dt = s.sb("w_dt", [R, D])
        b_dt = s.sb("b_dt", [P, KH])
        a_log = s.sb("a_log", [P, KH, NS])
        a_exp = s.sb("a_exp", [P, KH, NS])
        a_neg = s.sb("a_neg", [P, KH, NS])
        sel = s.sb("sel", [96, 2 * NS, P], BF16)
        xT = [s.sb(f"xT{i}", [P, KH, GT]) for i in range(2)]
        bcs = [s.sb(f"bcs{i}", [96, GT], BF16) for i in range(2)]
        bc_rest = s.sb("bc_rest", [96, GT])
        bc_mid = s.sb("bc_mid", [96, GT], BF16)
        dt_low = s.sb("dt_low", [R, GT])
        z_abs = s.sb("z_abs", [P, KH, GT])
        z_exp = s.sb("z_exp", [P, KH, GT])
        z_log = s.sb("z_log", [P, KH, GT])
        z_pos = s.sb("z_pos", [P, KH, GT])
        delta = [s.sb(f"delta{i}", [P, KH, GB, SEQ]) for i in range(2)]
        dx = [s.sb(f"dx{i}", [P, KH, GT]) for i in range(2)]
        decay = s.sb("decay", [P, RING, KH, GB, SEQ])
        drive = s.sb("drive", [P, RING, KH, GT])
        state = s.sb("state", [P, RING, KH, GT])
        c_sb = s.sb("c_sb", [P, RING, GT])
        hc = s.sb("hc", [P, RING, KH, GT])
        yT = s.sb("yT", [P, KH, GT])
        stats = s.sb("stats", [P, GB, 6])
        moment = s.sb("moment", [P, 4, GB])
        mean = s.sb("mean", [P, GB])
        var = s.sb("var", [P, GB])
        ln_var = s.sb("ln_var", [P, GB])
        rstd = s.sb("rstd", [P, GB])
        eps = s.sb("eps", [P, 1])

        b_ps = [s.ps(f"b{i}", [P, 512]) for i in range(2)]
        c_ps = [s.ps(f"c{i}", [P, 512]) for i in range(2)]
        y_ps = [s.ps(f"y{i}", [P, 512]) for i in range(KH)]
        m_ps = [s.ps(f"m{i}", [P, 512]) for i in range(2)]

        proj_loaded = s.sem("proj_loaded")
        const_loaded = s.sem("const_loaded")
        x_loaded = [s.sem(f"x_loaded{i}") for i in range(2)]
        zeroed = s.sem("zeroed")
        a_ready = s.sem("a_ready")
        proj_ready = s.sem("proj_ready")
        dt_copied = s.sem("dt_copied")
        bc_high = s.sem("bc_high")
        bc_step = s.sem("bc_step")
        bcs_ready = s.sem("bcs_ready")
        z_ready = s.sem("z_ready")
        z_abs_ready = s.sem("z_abs_ready")
        z_exp_ready = s.sem("z_exp_ready")
        z_log_ready = s.sem("z_log_ready")
        z_pos_ready = s.sem("z_pos_ready")
        delta_ready = s.sem("delta_ready")
        dx_ready = s.sem("dx_ready")
        decay_ready = s.sem("decay_ready")
        b_ready = s.sem("b_ready")
        c_ready = s.sem("c_ready")
        c_copied = s.sem("c_copied")
        drive_ready = s.sem("drive_ready")
        scanned = s.sem("scanned")
        hc_ready = s.sem("hc_ready")
        hc_summed = s.sem("hc_summed")
        y_started = s.sem("y_started")
        y_copied = s.sem("y_copied")
        turned = s.sem("turned")
        stats_ready = s.sem("stats_ready")
        mv_ready = s.sem("mv_ready")
        lv_ready = s.sem("lv_ready")
        rstd_ready = s.sem("rstd_ready")
        normed = s.sem("normed")
        consts = 5

        with nc.Block() as block:

            @block.sync
            def _(sp):
                sp.dma_start(w_proj[:], w_proj_dram).then_inc(proj_loaded, 16)
                sp.dma_start(w_bc[:], w_bc_dram).then_inc(proj_loaded, 16)
                sp.dma_start(xT[0][:], xT_dram[:, :, 0:GT]).then_inc(x_loaded[0], 16)
                sp.dma_start(w_dt[:], w_dt_dram).then_inc(const_loaded, 16)
                sp.dma_start(b_dt[:], b_dt_dram).then_inc(const_loaded, 16)
                sp.dma_start(a_log[:], a_log_dram).then_inc(const_loaded, 16)
                sp.dma_start(sel[:], sel_dram).then_inc(const_loaded, 16)
                sp.dma_start(ident[0][:], ident[1]).then_inc(const_loaded, 16)
                sp.dma_start(xT[1][:], xT_dram[:, :, GT:2 * GT]).then_inc(x_loaded[1], 16)
                attention.load(sp)
                with sp.Fori(1, GROUPS // 2) as i:
                    for par in range(2):
                        g = 2 * i + par
                        sp.wait_ge(y_started, g - 1)
                        sp.wait_ge(dx_ready, g - 1)
                        sp.dma_start(xT[par][:], xT_dram[:, :, ds(g * GT, GT)]).then_inc(x_loaded[par], 16)

            @block.tensor
            def _(pe):
                def project(i, par, first=False):
                    g = 2 * i + par
                    pe.wait_ge(x_loaded[par], 16 * (i + 1))
                    if not first:
                        pe.wait_ge(normed, g + 1)
                    for k in range(KH):
                        pe.matmul(m_ps[0][0:R, :], w_proj[:, k, :], xT[par][:, k, :], start=(k == 0), stop=(k == KH - 1))
                    for k in range(KH):
                        last = pe.matmul(m_ps[1][0:96, :], w_bc[:, k, :], xT[par][:, k, :], start=(k == 0), stop=(k == KH - 1))
                    last.then_inc(proj_ready, 1)

                def step_size(i, par):
                    g = 2 * i + par
                    pe.wait_ge(dt_copied, g + 1)
                    pe.wait_ge(bc_high, g + 1)
                    pe.wait_ge(bc_step, 5 * g + 1)
                    for k in range(KH):
                        last = pe.matmul(m_ps[k][:], w_dt[:, k * P:(k + 1) * P], dt_low[:], start=True, stop=True)
                    last.then_inc(z_ready, 1)

                def broadcast_b(i, par, n):
                    g = 2 * i + par
                    q = STEPS * g + n
                    if n == 0:
                        pe.wait_ge(bcs_ready, g + 1)
                    pe.wait_ge(drive_ready, q + 1)
                    pe.matmul(b_ps[n % 2][:], sel[:, n, :], bcs[par][:], start=True, stop=True).then_inc(b_ready, 1)

                def broadcast_c(i, par, n):
                    q = STEPS * (2 * i + par) + n
                    pe.wait_ge(c_copied, q + 1)
                    mm = pe.matmul(c_ps[n % 2][:], sel[:, NS + n, :], bcs[par][:], start=True, stop=True)
                    mm.then_inc(c_ready, 1)

                def add_state(q, n):
                    pe.wait_ge(hc_ready, q + 1 + RING)
                    for k in range(KH):
                        last = pe.matmul(y_ps[k][:], ident[0][:], hc[:, n % RING, k, :], start=False, stop=(n == NS - 1))
                    last.then_inc(hc_summed, 1)

                def start_y(i, par):
                    g = 2 * i + par
                    pe.wait_ge(y_copied, g + 1)
                    for k in range(KH):
                        last = pe.matmul(y_ps[k][:], ident[0][:], xT[par][:, k, :], start=True, stop=False)
                    last.then_inc(y_started, 1)

                def turn(g):
                    pe.wait_ge(y_copied, g + 1)
                    pe.wait_ge(z_abs_ready, 2 * (g + 1))
                    pe.wait_ge(z_pos_ready, 2 * (g + 1))
                    for j in range(GB):
                        for k in range(KH):
                            c = (j % 2) * D + k * P
                            last = pe.transpose(m_ps[j // 2][:, c:c + P], yT[:, k, j * P:(j + 1) * P], ident[0][:])
                    last.then_inc(turned, 1)

                def group(i, par, final=False):
                    g = 2 * i + par
                    for n in range(STEPS):
                        ahead = (i, par, n + 2) if n + 2 < STEPS else None if final else (i + par, 1 - par, n + 2 - STEPS)
                        if ahead:
                            broadcast_b(*ahead)
                        if n == 2:
                            start_y(i, par)
                        add_state(STEPS * g + n - 2, (n - 2) % STEPS)
                        if ahead:
                            broadcast_c(*ahead)
                        if n == 3:
                            turn(g)
                        if not final:
                            if n == 6:
                                project(i + par, 1 - par)
                            if n == 8:
                                step_size(i + par, 1 - par)

                pe.sem_inc(c_ready, 1)
                pe.wait_ge(proj_loaded, 16 * 2)
                project(0, 0, first=True)
                pe.wait_ge(const_loaded, 16 * consts)
                step_size(0, 0)
                for n in range(2):
                    broadcast_b(0, 0, n)
                    broadcast_c(0, 0, n)
                pe.wait_ge(zeroed, 3)
                for k in range(KH):
                    pe.matmul(y_ps[k][:], ident[0][:], hc[:, RING - 1, k, :], start=True, stop=False)
                with pe.Fori(0, GROUPS // 2 - 1) as i:
                    group(i, 0)
                    group(i, 1)
                group(GROUPS // 2 - 1, 0)
                group(GROUPS // 2 - 1, 1, final=True)
                add_state(STEPS * GROUPS - 2, NS - 2)
                add_state(STEPS * GROUPS - 1, NS - 1)
                turn_last = GROUPS
                pe.wait_ge(y_copied, turn_last + 1)
                for j in range(GB):
                    for k in range(KH):
                        c = (j % 2) * D + k * P
                        last = pe.transpose(m_ps[j // 2][:, c:c + P], yT[:, k, j * P:(j + 1) * P], ident[0][:])
                last.then_inc(turned, 1)

            @block.scalar
            def _(act):
                nc.scalar.preload_act_table_set("natural_log_exp_and_others")

                def copy_low(g):
                    act.wait_ge(proj_ready, g + 1)
                    act.activation(dt_low[:], m_ps[0][0:R, :], ACT.Copy).then_inc(dt_copied, 1)

                def high_part(i, par, first=False):
                    g = 2 * i + par
                    if not first:
                        act.wait_ge(c_ready, STEPS * (g - 1) + 1)
                    act.activation(bcs[par][:], m_ps[1][0:96, :], ACT.Copy).then_inc(bc_high, 1)

                def softplus_parts(g, first=False):
                    act.wait_ge(z_ready, g + 1)
                    if not first:
                        act.wait_ge(z_log_ready, g)
                        act.wait_ge(delta_ready, g)
                    for k in range(KH):
                        act.activation(z_abs[:, k, :], m_ps[k][:], ACT.Abs, bias=b_dt[:, k:k + 1]).then_inc(z_abs_ready, 1)
                        act.activation(z_pos[:, k, :], m_ps[k][:], ACT.Relu, bias=b_dt[:, k:k + 1]).then_inc(z_pos_ready, 1)

                def softplus_exp(g):
                    act.wait_ge(z_abs_ready, 2 * (g + 1))
                    act.activation(z_exp[:], z_abs[:], ACT.Exp, scale=-1.0).then_inc(z_exp_ready, 1)

                def softplus_log(g, first=False):
                    act.wait_ge(z_exp_ready, g + 1)
                    if not first:
                        act.wait_ge(delta_ready, g)
                    act.activation(z_log[:], z_exp[:], ACT.Ln, bias=1.0).then_inc(z_log_ready, 1)

                def decays(par, q, n):
                    act.wait_ge(scanned, q + 1)
                    for k in range(KH):
                        act.activation(decay[:, n % RING, k, :, 1:SEQ], delta[par][:, k, :, 1:SEQ], ACT.Exp,
                                       scale=a_neg[:, k, n:n + 1]).then_inc(decay_ready, 1)

                def copy_y(g):
                    act.wait_ge(hc_summed, STEPS * g + 4)
                    act.wait_ge(turned, g)
                    act.activation(yT[:, 0, :], y_ps[0][:], ACT.Copy)
                    act.activation(yT[:, 1, :], y_ps[1][:], ACT.Copy).then_inc(y_copied, 1)

                def inv_std(g):
                    act.wait_ge(mv_ready, 3 * (g + 1))
                    act.wait_ge(normed, g + 1)
                    act.activation(ln_var[:], var[:], ACT.Ln, bias=eps[:, 0:1]).then_inc(lv_ready, 1)
                    act.wait_ge(lv_ready, g + 1)
                    act.activation(rstd[:], ln_var[:], ACT.Exp, scale=-0.5).then_inc(rstd_ready, 1)

                def group(i, par, final=False):
                    g = 2 * i + par
                    for n in range(STEPS):
                        q = STEPS * g + n
                        if n + 2 < STEPS:
                            decays(par, q + 2, n + 2)
                        elif not final:
                            if n + 2 == STEPS:
                                act.wait_ge(delta_ready, g + 2)
                            decays(1 - par, q + 2, n + 2 - STEPS)
                        act.wait_ge(c_ready, q + 2)
                        act.wait_ge(hc_ready, q + 1)
                        act.activation(c_sb[:, n % RING, :], c_ps[n % 2][:], ACT.Copy).then_inc(c_copied, 1)
                        if n == 2:
                            copy_y(g)
                        if n == 5:
                            inv_std(g)
                        if not final:
                            if n == 7:
                                copy_low(g + 1)
                                high_part(i + par, 1 - par)
                            if n == 9:
                                softplus_parts(g + 1)
                            if n == 10:
                                softplus_exp(g + 1)
                            if n == 11:
                                softplus_log(g + 1)

                act.sem_inc(c_copied, 2)
                act.sem_inc(turned, 1)
                act.sem_inc(normed, 1)
                copy_low(0)
                high_part(0, 0, first=True)
                act.wait_ge(const_loaded, 16 * consts)
                act.activation(a_exp[:], a_log[:], ACT.Exp).then_inc(a_ready, 1)
                softplus_parts(0, first=True)
                softplus_exp(0)
                softplus_log(0, first=True)
                act.wait_ge(a_ready, 2)
                act.wait_ge(zeroed, 3)
                act.wait_ge(delta_ready, 1)
                for n in range(2):
                    decays(0, n, n)
                with act.Fori(0, GROUPS // 2 - 1) as i:
                    group(i, 0)
                    group(i, 1)
                group(GROUPS // 2 - 1, 0)
                group(GROUPS // 2 - 1, 1, final=True)
                copy_y(GROUPS)
                inv_std(GROUPS)

            @block.vector
            def _(dve):
                def split(i, par):
                    g = 2 * i + par
                    dve.wait_ge(bc_high, g + 1)
                    dve.tensor_tensor(bc_rest[:], m_ps[1][0:96, :], bcs[par][:], ALU.subtract).then_inc(bc_step, 1)
                    dve.wait_ge(bc_step, 5 * g + 1)
                    dve.tensor_copy(bcs[par][32:64, :], bc_rest[32:64, :]).then_inc(bc_step, 1)
                    dve.tensor_copy(bc_mid[64:96, :], bc_rest[64:96, :]).then_inc(bc_step, 1)
                    dve.wait_ge(bc_step, 5 * g + 3)
                    dve.tensor_tensor(bcs[par][64:96, :], bc_rest[64:96, :], bc_mid[64:96, :], ALU.subtract).then_inc(bc_step, 1)
                    dve.wait_ge(bc_step, 5 * g + 4)
                    dve.sem_inc(bc_step, 1)
                    dve.sem_inc(bcs_ready, 1)

                def step_inputs(i, par):
                    g = 2 * i + par
                    dve.wait_ge(delta_ready, g + 1)
                    dve.tensor_tensor(dx[par][:], delta[par][:].rearrange("p k b t -> p k (b t)"), xT[par][:], ALU.mult).then_inc(dx_ready, 1)

                def drives(i, par, n):
                    g = 2 * i + par
                    q = STEPS * g + n
                    if n == 0:
                        dve.wait_ge(dx_ready, g + 1)
                    dve.wait_ge(b_ready, q + 1)
                    dve.wait_ge(scanned, q + 1)
                    dve.tensor_tensor(drive[:, n % RING, :, :], dx[par][:],
                                      b_ps[n % 2][:].unsqueeze(1).broadcast_to([P, KH, GT]), ALU.mult).then_inc(drive_ready, 1)

                def scan(q, n):
                    dve.wait_ge(drive_ready, q + 3)
                    dve.wait_ge(decay_ready, KH * (q + 1) + KH)
                    dve.wait_ge(hc_ready, q + 1)
                    dve.tensor_tensor_scan(state[:, n % RING, :, :].rearrange("p k t -> p (k t)"),
                                           decay[:, n % RING, :, :, :].rearrange("p k b t -> p (k b t)"),
                                           drive[:, n % RING, :, :].rearrange("p k t -> p (k t)"),
                                           0.0, ALU.mult, ALU.add).then_inc(scanned, 1)

                def statistics(g):
                    dve.wait_ge(turned, g + 2)
                    for j in range(GB):
                        last = dve.bn_stats(stats[:, j, :], m_ps[j // 2][:, (j % 2) * D:(j % 2 + 1) * D])
                    last.then_inc(stats_ready, 1)
                    merge_moments(dve, stats, stats_ready, g + 1, moment, mean, var, mv_ready, g)

                def normalise(g):
                    dve.wait_ge(rstd_ready, g + 1)
                    for j in range(GB):
                        last = dve.tensor_scalar(x1[:, ds(GB * g + j, 1), :].rearrange("p o d -> p (o d)"),
                                                 m_ps[j // 2][:, (j % 2) * D:(j % 2 + 1) * D],
                                                 mean[:, j:j + 1], rstd[:, j:j + 1], ALU.subtract, ALU.mult)
                    last.then_inc(normed, 1)

                def group(i, par, final=False):
                    g = 2 * i + par
                    for n in range(STEPS):
                        q = STEPS * g + n
                        if n + 1 < STEPS:
                            drives(i, par, n + 1)
                        elif not final:
                            drives(i + par, 1 - par, 0)
                        scan(q, n)
                        if n == 4:
                            statistics(g)
                        if n == 5:
                            normalise(g)
                        if n == 7 and not final:
                            split(i + par, 1 - par)
                        if n == 13 and not final:
                            step_inputs(i + par, 1 - par)

                dve.sem_inc(drive_ready, 2)
                dve.sem_inc(scanned, RING)
                dve.memset(decay[:].rearrange("p r k b t -> p (r k b) t")[:, :, 0], 0.0).then_inc(zeroed, 1)
                dve.memset(eps[:], EPS).then_inc(zeroed, 1)
                split(0, 0)
                dve.wait_ge(a_ready, 1)
                dve.tensor_scalar(a_neg[:], a_exp[:], -1.0, None, ALU.mult).then_inc(a_ready, 1)
                step_inputs(0, 0)
                drives(0, 0, 0)
                with dve.Fori(0, GROUPS // 2 - 1) as i:
                    group(i, 0)
                    group(i, 1)
                group(GROUPS // 2 - 1, 0)
                group(GROUPS // 2 - 1, 1, final=True)
                dve.wait_ge(const_loaded, 16 * consts)
                attention.prepare(dve, ident[0])
                statistics(GROUPS)
                normalise(GROUPS)

            @block.gpsimd
            def _(pool):
                def step_sizes(i, par, first=False):
                    g = 2 * i + par
                    pool.wait_ge(z_log_ready, g + 1)
                    pool.wait_ge(z_pos_ready, 2 * (g + 1))
                    if not first:
                        pool.wait_ge(decay_ready, KH * STEPS * (g - 1) + KH)
                    pool.tensor_tensor(delta[par][:].rearrange("p k b t -> p k (b t)"), z_log[:], z_pos[:], ALU.add).then_inc(delta_ready, 1)

                def outputs(q, n):
                    pool.wait_ge(c_copied, q + 3)
                    pool.wait_ge(scanned, q + 1 + RING)
                    pool.wait_ge(hc_summed, q + 1)
                    pool.tensor_tensor(hc[:, n % RING, :, :], state[:, n % RING, :, :],
                                       c_sb[:, n % RING, :].unsqueeze(1).broadcast_to([P, KH, GT]), ALU.mult).then_inc(hc_ready, 1)

                def group(i, par, final=False):
                    g = 2 * i + par
                    for n in range(STEPS):
                        outputs(STEPS * g + n, n)
                        if not final:
                            if n == 11:
                                step_sizes(i + par, 1 - par)

                pool.sem_inc(hc_summed, RING - 2)
                pool.sem_inc(decay_ready, 2)
                pool.memset(hc[:, RING - 2:RING, :, :], 0.0).then_inc(zeroed, 1)
                pool.wait_ge(zeroed, 3)
                pool.sem_inc(hc_ready, RING)
                step_sizes(0, 0, first=True)
                with pool.Fori(0, GROUPS // 2 - 1) as i:
                    group(i, 0)
                    group(i, 1)
                group(GROUPS // 2 - 1, 0)
                group(GROUPS // 2 - 1, 1, final=True)


def products(pe, out, pairs, start, stop):
    for n, (a_hi, a_lo, b_hi, b_lo) in enumerate(pairs):
        pe.matmul(out, a_hi, b_hi, start=start and n == 0, stop=False, skip_group_check=True)
        pe.matmul(out, a_hi, b_lo, start=False, stop=False, skip_group_check=True)
        last = pe.matmul(out, a_lo, b_hi, start=False, stop=stop and n == len(pairs) - 1, skip_group_check=True)
    return last


class Seq:

    def __init__(self, pair, offset):
        self.pair, self.offset = pair, offset
        self.parity = offset % 2
        self.half = pair + offset // 2
        self.b = 2 * pair + offset

    def plus(self, n):
        return Seq(self.pair, self.offset + n)


def since(eng, sem, count):
    if not (isinstance(count, int) and count < 1):
        eng.wait_ge(sem, count)


def attention_phase(nc, x1, ident, gate_all, const, ctxT_dram, table_dram, acc_dram, choice, row, row_stored):
    with ExitStack() as ctx:
        s = Scope(nc, ctx, "attn")
        (q_w_hi, q_w_lo), (kv_w_hi, kv_w_lo), (o_w_hi, o_w_lo) = const.w_parts
        w_g, norm, affine, pick, eps, ident_bf = const.w_g, const.norm, const.affine, const.pick, const.eps, const.ident_bf
        x1b = [s.sb(f"x1b{i}", [P, D]) for i in range(2)]
        x1T_hi = s.sb("x1T_hi", [P, KH, P], F32R)
        x1T_lo = s.sb("x1T_lo", [P, KH, P], F32R)
        ctxT = [s.sb(f"ctxT{i}", [P, KH, P]) for i in range(2)]
        ctx_hi = [s.sb(f"ctx_hi{i}", [P, KH, P], F32R) for i in range(2)]
        ctx_lo = [s.sb(f"ctx_lo{i}", [P, KH, P], F32R) for i in range(2)]
        qk_stats = s.sb("qk_stats", [P, 2, 6])
        qk_part = s.sb("qk_part", [P, 4, 2])
        qk_mean = s.sb("qk_mean", [P, 2])
        qk_var = s.sb("qk_var", [P, 2])
        qk_lnv = s.sb("qk_lnv", [P, 2])
        qk_rstd = s.sb("qk_rstd", [P, 2])
        qkn = s.sb("qkn", [P, 2, D])
        qT = [s.sb(f"qT{i}", [P, KH, 2, P]) for i in range(2)]
        kT = [s.sb(f"kT{i}", [P, KH, P]) for i in range(2)]
        q_parts = [s.sb(f"q_parts{i}", [P, 2, KH, 2, P], F32R) for i in range(2)]
        k_hi = [s.sb(f"k_hi{i}", [P, KH, P], F32R) for i in range(2)]
        k_lo = [s.sb(f"k_lo{i}", [P, KH, P], F32R) for i in range(2)]
        qz = [s.sb(f"qz{i}", [P, 2, KH, HEADS // KH, P], F32R) for i in range(2)]
        qb = s.sb("qb", [P, KH, 2, P], BF16)
        kb = s.sb("kb", [P, KH, P], BF16)
        v1 = [s.sb(f"v1{i}", [P, HEADS, DK + 1]) for i in range(2)]
        top = s.sb("top", [P, HEADS])
        neg_top = s.sb("neg_top", [P, 4, 32], BF16)
        ntT = s.sb("ntT", [P, P], BF16)
        prob = [s.sb(f"prob{i}", [P, HEADS, P]) for i in range(2)]
        inv_sum = s.sb("inv_sum", [P, HEADS])
        mix = s.sb("mix", [P, HEADS, DK])
        mixT_hi = s.sb("mixT_hi", [P, KH, P], F32R)
        mixT_lo = s.sb("mixT_lo", [P, KH, P], F32R)
        res = s.sb("res", [P, D])
        o_stats = s.sb("o_stats", [P, 1, 6])
        o_part = s.sb("o_part", [P, 4, 1])
        o_mean = s.sb("o_mean", [P, 1])
        o_var = s.sb("o_var", [P, 1])
        o_lnv = s.sb("o_lnv", [P, 1])
        o_rstd = s.sb("o_rstd", [P, 1])
        x2T = s.sb("x2T", [P, KH, P])
        g_exp = s.sb("g_exp", [P, EXPERTS])
        g_den = s.sb("g_den", [P, EXPERTS])

        turn_ps = s.ps("turn", [P, 512])
        q_ps = s.ps("q", [P, D])
        kv_ps = s.ps("kv", [P, 2 * D])
        s_ps = [s.ps(f"s{j}", [P, 512]) for j in range(4)]
        o_ps = s.ps("o", [P, 512])

        names = ("x1T_high mixT_high ctx_seen ctx_high ctx_ready qk_high qk_low blank_ready x1b_ready x1_turned x1T_ready q_ready kv_ready qk_stats_ready qk_moments "
                 "qk_rstd_ready qk_lnv_ready v_ready qkn_ready qkn_turned qk_ready qk_seen qkb_ready s_ready top_done neg_ready nt_turned nt_ready "
                 "st_ready exp_done pv_done inv_ready mix_ready mix_turned mixT_ready o_ready res_ready o_stats_ready o_moments "
                 "o_lnv_ready o_rstd_ready x2_ready x2_turned x2T_ready g_ready g_exp_ready g_den_ready gate_ready").split()
        m = {n: s.sem(n) for n in names}
        ctx_loaded = [s.sem(f"ctx_loaded{i}") for i in range(2)]
        qz_moved = [s.sem(f"qz_moved{i}") for i in range(2)]
        LOOPED = (NT - 4) // 2
        BLANKS = 5

        def passes(eng, step):
            step(Seq(0, -1), "XA")
            step(Seq(0, 0), "XAB")
            step(Seq(0, 1), "XABC")
            with eng.Fori(0, LOOPED) as i:
                step(Seq(i, 2), "XABCD")
                step(Seq(i, 3), "XABCD")
            step(Seq(0, NT - 2), "ABCD")
            step(Seq(0, NT - 1), "BCD")
            step(Seq(0, NT), "CD")
            step(Seq(0, NT + 1), "D")

        with nc.Block() as block:

            @block.sync
            def _(sp):
                def load_ctx(q):
                    since(sp, m["ctx_ready"], q.b - 1)
                    sp.dma_start(ctxT[q.parity][:], ctxT_dram[:, :, ds(q.b * SEQ, SEQ)]).then_inc(ctx_loaded[q.parity], 16)

                def spread_queries(q):
                    sp.wait_ge(m["qk_low"], q.b + 1)
                    for j in range(4):
                        rows = slice(32 * j, 32 * j + 32)
                        sp.dma_start(qz[q.parity][rows, :, :, 2 * j:2 * j + 2, :].rearrange("p a k e t -> p (a k) (e t)").bitcast(F32),
                                     q_parts[q.parity][rows].rearrange("p a k e t -> p (a k) (e t)").bitcast(F32)).then_inc(qz_moved[q.parity], 16)

                def store(q):
                    sp.wait_ge(m["gate_ready"], q.b + 1)
                    sp.dma_start(table_dram[ds(q.b * SEQ, SEQ), :], row[q.parity][:]).then_inc(row_stored[q.parity], 16)
                    sp.dma_start(acc_dram[ds(q.b * SEQ, SEQ), :], row[q.parity][:, 0:D]).then_inc(row_stored[q.parity], 16)

                def step(q, stages):
                    if "X" in stages:
                        load_ctx(q.plus(2))
                    if "D" in stages:
                        store(q.plus(-2))
                    if "A" in stages:
                        spread_queries(q.plus(1))

                load_ctx(Seq(0, 0))
                choice.load(sp)
                sp.wait_ge(m["blank_ready"], BLANKS)
                passes(sp, step)

            @block.gpsimd
            def _(pool):
                def copy_x1(q):
                    since(pool, m["x1_turned"], q.b - 1)
                    pool.tensor_copy(x1b[q.parity][:], x1[:, ds(GB + q.b, 1), :].rearrange("p o d -> p (o d)")).then_inc(m["x1b_ready"], 1)

                def split_ctx(q):
                    pool.wait_ge(ctx_loaded[q.parity], 16 * (q.half + 1))
                    since(pool, m["kv_ready"], q.b - 1)
                    pool.sem_inc(m["ctx_seen"], 1)
                    pool.tensor_copy(ctx_hi[q.parity][:], ctxT[q.parity][:]).then_inc(m["ctx_high"], 1)
                    pool.wait_ge(m["ctx_high"], q.b + 1)
                    pool.tensor_tensor(ctx_lo[q.parity][:], ctxT[q.parity][:], ctx_hi[q.parity][:].bitcast(F32), ALU.subtract).then_inc(m["ctx_ready"], 1)

                def round_qk(q):
                    pool.wait_ge(m["qk_ready"], q.b + 1)
                    pool.sem_inc(m["qk_seen"], 1)
                    pool.tensor_copy(kb[:], kT[q.parity][:])
                    pool.tensor_copy(qb[:], qT[q.parity][:]).then_inc(m["qkb_ready"], 1)

                def rest_of_qk(q):
                    pool.wait_ge(m["qk_high"], q.b + 1)
                    pool.tensor_tensor(q_parts[q.parity][:, 1], qT[q.parity][:], q_parts[q.parity][:, 0].bitcast(F32), ALU.subtract)
                    pool.tensor_tensor(k_lo[q.parity][:], kT[q.parity][:], k_hi[q.parity][:].bitcast(F32), ALU.subtract).then_inc(m["qk_low"], 1)

                def step(q, stages):
                    if "X" in stages:
                        copy_x1(q.plus(2))
                        split_ctx(q.plus(2))
                    if "A" in stages:
                        round_qk(q.plus(1))
                        rest_of_qk(q.plus(1))

                copy_x1(Seq(0, 0))
                for i in range(2):
                    pool.memset(v1[i][:], 1.0).then_inc(m["blank_ready"], 1)
                pool.memset(neg_top[:], 0.0).then_inc(m["blank_ready"], 1)
                split_ctx(Seq(0, 0))
                for i in range(2):
                    pool.memset(qz[i][:].bitcast(F32), 0.0).then_inc(m["blank_ready"], 1)
                passes(pool, step)

            @block.tensor
            def _(pe):
                def turn_x1(q):
                    pe.wait_ge(m["x1b_ready"], q.b + 1)
                    since(pe, m["qk_ready"], q.b)
                    for k in range(KH):
                        last = pe.transpose(turn_ps[:, k * P:(k + 1) * P], x1b[q.parity][:, k * P:(k + 1) * P], ident[:])
                    last.then_inc(m["x1_turned"], 1)

                def project_q(q):
                    pe.wait_ge(m["x1T_ready"], q.b + 1)
                    since(pe, m["qkn_ready"], q.b)
                    products(pe, q_ps[:], [(x1T_hi[:, k, :], x1T_lo[:, k, :], q_w_hi[:, k, :], q_w_lo[:, k, :]) for k in range(KH)],
                             True, True).then_inc(m["q_ready"], 1)

                def project_kv(q, k):
                    if k == 0:
                        pe.wait_ge(m["ctx_ready"], q.b + 1)
                        since(pe, m["v_ready"], q.b)
                    last = products(pe, kv_ps[:], [(ctx_hi[q.parity][:, k, :], ctx_lo[q.parity][:, k, :], kv_w_hi[:, k, :], kv_w_lo[:, k, :])],
                                    k == 0, k == KH - 1)
                    if k == KH - 1:
                        last.then_inc(m["kv_ready"], 1)

                def turn_qk(q):
                    pe.wait_ge(m["qkn_ready"], q.b + 1)
                    since(pe, m["nt_ready"], q.b)
                    for i in range(2):
                        for k in range(KH):
                            c = (i * KH + k) * P
                            last = pe.transpose(turn_ps[:, c:c + P], qkn[:, i, k * P:(k + 1) * P], ident[:])
                    last.then_inc(m["qkn_turned"], 1)

                def scores(q):
                    pe.wait_ge(m["qkb_ready"], q.b + 1)
                    since(pe, m["exp_done"], 4 * q.b)
                    for k in range(KH):
                        for e in range(2):
                            c = (2 * k + e) * P
                            for j in range(4):
                                rows = slice(32 * j, 32 * j + 32)
                                last = pe.matmul(s_ps[j][:, c:c + P], qb[rows, k, e, :], kb[rows, k, :], start=True, stop=True)
                                if k == KH - 1 and e == 1:
                                    last.then_inc(m["s_ready"], 1)

                def turn_top(q):
                    pe.wait_ge(m["neg_ready"], q.b + 1)
                    since(pe, m["g_exp_ready"], q.b - 1)
                    pe.transpose(turn_ps[:, 0:P // 2].bitcast(BF16), neg_top[:].rearrange("p j h -> p (j h)"), ident_bf[:]).then_inc(m["nt_turned"], 1)

                def shifted_scores(q, i):
                    k, h = i // 2, i % 2 * 4
                    if i == 0:
                        pe.wait_ge(m["nt_ready"], q.b + 1)
                        pe.wait_ge(qz_moved[q.parity], 64 * (q.half + 1))
                        pe.wait_ge(m["qk_low"], q.b + 1)
                    hi, lo = (qz[q.parity][:, part, k, h:h + 4, :].rearrange("p h t -> p (h t)") for part in range(2))
                    products(pe, s_ps[i][:], [(k_hi[q.parity][:, k, :], k_lo[q.parity][:, k, :], hi, lo)], True, True)
                    for c in range(4):
                        last = pe.matmul(s_ps[i][:, c * P:(c + 1) * P], pick[:, 4 * i + c, :], ntT[:], start=False, stop=True,
                                         skip_group_check=True)
                    last.then_inc(m["st_ready"], 1)

                def mix_values(q, pair):
                    if pair == 0:
                        since(pe, m["res_ready"], q.b)
                        pe.wait_ge(m["v_ready"], q.b + 1)
                    if pair % 2 == 0:
                        pe.wait_ge(m["exp_done"], 4 * q.b + pair // 2 + 1)
                    for h in (2 * pair, 2 * pair + 1):
                        last = pe.matmul(o_ps[:, h * (DK + 1):(h + 1) * (DK + 1)], prob[q.parity][:, h, :],
                                         v1[q.parity][:, h, :], start=True, stop=True)
                    if 2 * pair == HEADS - 2:
                        last.then_inc(m["pv_done"], 1)

                def turn_mix(q):
                    pe.wait_ge(m["mix_ready"], q.b + 1)
                    for k in range(KH):
                        last = pe.transpose(o_ps[:, k * P:(k + 1) * P], mix[:, 8 * k:8 * k + 8, :].rearrange("p h d -> p (h d)"), ident[:])
                    last.then_inc(m["mix_turned"], 1)

                def project_out(q):
                    pe.wait_ge(m["mixT_ready"], q.b + 1)
                    products(pe, o_ps[:, D:2 * D], [(mixT_hi[:, k, :], mixT_lo[:, k, :], o_w_hi[:, k, :], o_w_lo[:, k, :]) for k in range(KH)],
                             True, True).then_inc(m["o_ready"], 1)

                def turn_x2(q):
                    pe.wait_ge(m["x2_ready"], q.b + 1)
                    pe.wait_ge(m["x1T_ready"], min(q.b + 4, NT) if isinstance(q.b, int) else q.b + 4)
                    for k in range(KH):
                        last = pe.transpose(turn_ps[:, (KH + k) * P:(KH + k + 1) * P], row[q.parity][:, k * P:(k + 1) * P], ident[:])
                    last.then_inc(m["x2_turned"], 1)

                def gates(q):
                    pe.wait_ge(m["x2T_ready"], q.b + 1)
                    for k in range(KH):
                        last = pe.matmul(turn_ps[:, 0:EXPERTS], x2T[:, k, :], w_g[:, k, :], start=(k == 0), stop=(k == KH - 1))
                    last.then_inc(m["g_ready"], 1)

                def step(q, stages):
                    n, p, g = q.plus(1), q.plus(-1), q.plus(-2)
                    if "A" in stages:
                        turn_x1(n)
                    if "C" in stages:
                        mix_values(p, 0)
                    if "B" in stages:
                        scores(q)
                    if "C" in stages:
                        mix_values(p, 1)
                    if "A" in stages:
                        project_q(n)
                        project_kv(n, 0)
                    if "C" in stages:
                        mix_values(p, 2)
                    if "A" in stages:
                        project_kv(n, 1)
                    if "C" in stages:
                        mix_values(p, 3)
                    if "D" in stages:
                        turn_x2(g)
                    if "C" in stages:
                        mix_values(p, 4)
                        mix_values(p, 5)
                    if "D" in stages:
                        gates(g)
                    if "C" in stages:
                        mix_values(p, 6)
                    if "B" in stages:
                        turn_top(q)
                    if "C" in stages:
                        mix_values(p, 7)
                    if "B" in stages:
                        shifted_scores(q, 0)
                    if "A" in stages:
                        turn_qk(n)
                    if "B" in stages:
                        shifted_scores(q, 1)
                    if "C" in stages:
                        turn_mix(p)
                    if "B" in stages:
                        shifted_scores(q, 2)
                    if "C" in stages:
                        project_out(p)
                    if "B" in stages:
                        shifted_scores(q, 3)

                pe.wait_ge(const.ready, const.steps)
                passes(pe, step)

            @block.scalar
            def _(act):
                nc.scalar.preload_act_table_set("natural_log_exp_and_others")

                def inv_std(q, var, moments, lnv, lnv_ready, rstd, rstd_ready):
                    act.wait_ge(moments, 3 * (q.b + 1))
                    act.activation(lnv[:], var[:], ACT.Ln, bias=eps[:, 0:1]).then_inc(lnv_ready, 1)
                    act.wait_ge(lnv_ready, q.b + 1)
                    act.activation(rstd[:], lnv[:], ACT.Exp, scale=-0.5).then_inc(rstd_ready, 1)

                def copy_turned(q, turned, bank, k, out, ready):
                    act.wait_ge(turned, q.b + 1)
                    act.activation(out[:].rearrange("p k t -> p (k t)"), bank[:, k * P:(k + KH) * P], ACT.Copy).then_inc(ready, 1)

                def scale_qk(q):
                    act.wait_ge(m["qkn_turned"], q.b + 1)
                    for k in range(KH):
                        for e in range(2):
                            act.activation(qT[q.parity][:, k, e, :], turn_ps[:, k * P:(k + 1) * P], ACT.Identity,
                                           bias=affine[:, 1, e, k:k + 1], scale=affine[:, 0, e, k:k + 1])
                        c = (KH + k) * P
                        last = act.activation(kT[q.parity][:, k, :], turn_ps[:, c:c + P], ACT.Identity,
                                              bias=norm[:, 1, k:k + 1], scale=norm[:, 0, k:k + 1])
                    last.then_inc(m["qk_ready"], 1)

                def round_parts(q):
                    act.wait_ge(m["qk_ready"], q.b + 1)
                    act.activation(q_parts[q.parity][:, 0], qT[q.parity][:], ACT.Copy)
                    act.activation(k_hi[q.parity][:], kT[q.parity][:], ACT.Copy).then_inc(m["qk_high"], 1)

                def copy_top(q):
                    act.wait_ge(m["nt_turned"], q.b + 1)
                    act.activation(ntT[:], turn_ps[:, 0:P // 2].bitcast(BF16), ACT.Copy).then_inc(m["nt_ready"], 1)

                def exps(q, j):
                    if j == 0:
                        since(act, m["pv_done"], q.b - 1)
                    act.wait_ge(m["st_ready"], 4 * q.b + j + 1)
                    act.activation(prob[q.parity][:, 4 * j:4 * j + 4, :].rearrange("p h q -> p (h q)"), s_ps[j][:], ACT.Exp,
                                   scale=DK ** -0.5).then_inc(m["exp_done"], 1)

                def gate_exp(q):
                    act.wait_ge(m["g_ready"], q.b + 1)
                    since(act, m["g_den_ready"], q.b)
                    act.activation(g_exp[:], turn_ps[:, 0:EXPERTS], ACT.Exp, scale=-1.0).then_inc(m["g_exp_ready"], 1)

                def step(q, stages):
                    n, p, g = q.plus(1), q.plus(-1), q.plus(-2)
                    if "A" in stages:
                        copy_turned(n, m["x1_turned"], turn_ps, 0, x1T_hi, m["x1T_high"])
                    if "D" in stages:
                        inv_std(g, o_var, m["o_moments"], o_lnv, m["o_lnv_ready"], o_rstd, m["o_rstd_ready"])
                        copy_turned(g, m["x2_turned"], turn_ps, KH, x2T, m["x2T_ready"])
                        gate_exp(g)
                    if "A" in stages:
                        inv_std(n, qk_var, m["qk_moments"], qk_lnv, m["qk_lnv_ready"], qk_rstd, m["qk_rstd_ready"])
                    if "B" in stages:
                        copy_top(q)
                    if "B" in stages:
                        exps(q, 0)
                    if "A" in stages:
                        scale_qk(n)
                    if "C" in stages:
                        copy_turned(p, m["mix_turned"], o_ps, 0, mixT_hi, m["mixT_high"])
                    if "A" in stages:
                        round_parts(n)
                    if "B" in stages:
                        exps(q, 1)
                        exps(q, 2)
                        exps(q, 3)

                act.wait_ge(const.ready, const.steps)
                passes(act, step)

            @block.vector
            def _(dve):
                def rest_of_x1(q):
                    dve.wait_ge(m["x1T_high"], q.b + 1)
                    dve.tensor_tensor(x1T_lo[:].rearrange("p k t -> p (k t)"), turn_ps[:, 0:KH * P],
                                      x1T_hi[:].rearrange("p k t -> p (k t)").bitcast(F32), ALU.subtract).then_inc(m["x1T_ready"], 1)

                def rest_of_mix(q):
                    dve.wait_ge(m["mixT_high"], q.b + 1)
                    dve.tensor_tensor(mixT_lo[:].rearrange("p k t -> p (k t)"), o_ps[:, 0:KH * P],
                                      mixT_hi[:].rearrange("p k t -> p (k t)").bitcast(F32), ALU.subtract).then_inc(m["mixT_ready"], 1)

                def moments(q):
                    since(dve, m["qk_rstd_ready"], q.b)
                    dve.wait_ge(m["q_ready"], q.b + 1)
                    dve.bn_stats(qk_stats[:, 0, :], q_ps[:])
                    dve.wait_ge(m["kv_ready"], q.b + 1)
                    dve.bn_stats(qk_stats[:, 1, :], kv_ps[:, 0:D]).then_inc(m["qk_stats_ready"], 1)
                    merge_moments(dve, qk_stats, m["qk_stats_ready"], q.b + 1, qk_part, qk_mean, qk_var, m["qk_moments"], q.b)

                def normalise_qk(q):
                    dve.wait_ge(m["qk_rstd_ready"], q.b + 1)
                    since(dve, m["qkn_turned"], q.b)
                    dve.tensor_scalar(qkn[:, 0, :], q_ps[:], qk_mean[:, 0:1], qk_rstd[:, 0:1], ALU.subtract, ALU.mult)
                    dve.tensor_scalar(qkn[:, 1, :], kv_ps[:, 0:D], qk_mean[:, 1:2], qk_rstd[:, 1:2], ALU.subtract,
                                      ALU.mult).then_inc(m["qkn_ready"], 1)

                def copy_values(q):
                    since(dve, m["pv_done"], q.b - 1)
                    dve.tensor_copy(v1[q.parity][:, :, 0:DK], kv_ps[:, D:2 * D].rearrange("p (h d) -> p h d", d=DK)).then_inc(m["v_ready"], 1)

                def maximum(q, j):
                    dve.wait_ge(m["s_ready"], 4 * q.b + j + 1)
                    dve.tensor_reduce(top[:, 4 * j:4 * j + 4], s_ps[j][:].rearrange("p (h k) -> p h k", k=P), AX.X,
                                      ALU.max).then_inc(m["top_done"], 1)

                def negate(q):
                    dve.wait_ge(m["top_done"], 4 * (q.b + 1))
                    dve.tensor_scalar(neg_top[:, :, 0:4], top[:].rearrange("p (j h) -> p j h", h=4), -1.0, None, ALU.mult).then_inc(m["neg_ready"], 1)

                def divide(q):
                    dve.wait_ge(m["pv_done"], q.b + 1)
                    pv = o_ps[:, 0:HEADS * (DK + 1)].rearrange("p (h d) -> p h d", d=DK + 1)
                    dve.reciprocal(inv_sum[:], pv[:, :, DK]).then_inc(m["inv_ready"], 1)
                    dve.wait_ge(m["inv_ready"], q.b + 1)
                    dve.tensor_tensor(mix[:], pv[:, :, 0:DK], inv_sum[:].unsqueeze(2).broadcast_to([P, HEADS, DK]),
                                      ALU.mult).then_inc(m["mix_ready"], 1)

                def residual(q):
                    dve.wait_ge(m["o_ready"], q.b + 1)
                    dve.tensor_tensor(res[:], o_ps[:, D:2 * D], x1[:, ds(GB + q.b, 1), :].rearrange("p o d -> p (o d)"),
                                      ALU.add).then_inc(m["res_ready"], 1)
                    dve.wait_ge(m["res_ready"], q.b + 1)
                    dve.bn_stats(o_stats[:, 0, :], res[:]).then_inc(m["o_stats_ready"], 1)
                    merge_moments(dve, o_stats, m["o_stats_ready"], q.b + 1, o_part, o_mean, o_var, m["o_moments"], q.b)

                def normalise(q):
                    dve.wait_ge(m["o_rstd_ready"], q.b + 1)
                    since(dve, row_stored[q.parity], 32 * q.half)
                    dve.tensor_scalar(row[q.parity][:, 0:D], res[:], o_mean[:, 0:1], o_rstd[:, 0:1], ALU.subtract,
                                      ALU.mult).then_inc(m["x2_ready"], 1)

                def sigmoid(q):
                    dve.wait_ge(m["g_exp_ready"], q.b + 1)
                    dve.tensor_scalar(g_den[:], g_exp[:], 1.0, None, ALU.add).then_inc(m["g_den_ready"], 1)
                    dve.wait_ge(m["g_den_ready"], q.b + 1)
                    dve.reciprocal(row[q.parity][:, D:D + EXPERTS], g_den[:])
                    dve.reciprocal(gate_all[:, q.parity, :, ds(q.half, 1)].rearrange("p e o -> p (e o)"), g_den[:]).then_inc(m["gate_ready"], 1)

                def step(q, stages):
                    n, p, g = q.plus(1), q.plus(-1), q.plus(-2)
                    if "A" in stages:
                        rest_of_x1(n)
                    if "D" in stages:
                        normalise(g)
                    if "B" in stages:
                        for j in range(4):
                            maximum(q, j)
                        negate(q)
                    if "A" in stages:
                        moments(n)
                        normalise_qk(n)
                    if "C" in stages:
                        divide(p)
                    if "A" in stages:
                        copy_values(n)
                    if "D" in stages:
                        sigmoid(g)
                    if "C" in stages:
                        rest_of_mix(p)
                        residual(p)

                passes(dve, step)



class AttentionConstants:

    def __init__(self, s, w_q, w_kv, w_o, w_g, norm, even_odd, pick):
        self.drams = (w_q, w_kv, w_o, w_g, norm, even_odd, pick)
        self.w = [s.sb(f"w_{name}", [P, KH, cols]) for name, cols in (("q", D), ("kv", 2 * D), ("o", D))]
        self.w_parts = [[s.sb(f"w_{name}_{part}", [P, KH, cols], F32R) for part in ("hi", "lo")]
                        for name, cols in (("q", D), ("kv", 2 * D), ("o", D))]
        self.w_g = s.sb("w_g", [P, KH, EXPERTS])
        self.norm = s.sb("norm", [P, 2, KH])
        self.even_odd = s.sb("even_odd", [P, 2])
        self.affine = s.sb("affine", [P, 2, 2, KH])
        self.pick = s.sb("pick", [P, HEADS, P], BF16)
        self.eps = s.sb("eps", [P, 1])
        self.ident_bf = s.sb("ident_bf", [P, P], BF16)
        self.loaded = s.sem("attention_loaded")
        self.w_high = s.sem("attention_w_high")
        self.ready = s.sem("attention_ready")
        self.count = 16 * len(self.drams)
        self.steps = len(self.w) + 4 + 2

    def load(self, sp):
        for sbuf, dram in zip((*self.w, self.w_g, self.norm, self.even_odd, self.pick), self.drams):
            sp.dma_start(sbuf[:], dram).then_inc(self.loaded, 16)

    def prepare(self, dve, ident):
        dve.wait_ge(self.loaded, self.count)
        for w, (hi, _) in zip(self.w, self.w_parts):
            dve.tensor_copy(hi[:], w[:]).then_inc(self.w_high, 1)
        for i in range(2):
            for e in range(2):
                dve.tensor_scalar(self.affine[:, i, e, :], self.norm[:, i, :], self.even_odd[:, e:e + 1], None, ALU.mult).then_inc(self.ready, 1)
        dve.memset(self.eps[:], EPS).then_inc(self.ready, 1)
        dve.tensor_copy(self.ident_bf[:], ident[:]).then_inc(self.ready, 1)
        for n, (w, (hi, lo)) in enumerate(zip(self.w, self.w_parts)):
            dve.wait_ge(self.w_high, n + 1)
            dve.tensor_tensor(lo[:], w[:], hi[:].bitcast(F32), ALU.subtract).then_inc(self.ready, 1)


class ChoiceConstants:

    def __init__(self, s, bits_i, bits_f, same, before, iota, place):
        self.drams = (bits_i, bits_f, same, before, iota, place)
        self.bits_i = s.sb("bits_i", list(bits_i.shape), I32)
        self.bits_f = s.sb("bits_f", list(bits_f.shape))
        self.same = s.sb("same", [P, P])
        self.before = s.sb("before", [P, P])
        self.iota = s.sb("iota", [P, 32])
        self.place = s.sb("place", [P, 1 + 2 * 16])
        self.loaded = s.sem("choice_loaded")
        self.count = 16 * len(self.drams)

    def load(self, sp):
        for sbuf, dram in zip((self.bits_i, self.bits_f, self.same, self.before, self.iota, self.place), self.drams):
            sp.dma_start(sbuf[:], dram).then_inc(self.loaded, 16)


class Weights:

    PIECES = 8
    PIECE = KH * FF // PIECES

    def __init__(self, s):
        self.w1 = s.sb("w1", [P, KH * FF])
        self.w2 = s.sb("w2", [P, FF // P * D])
        self.w1_hi = [s.sb(f"w1_hi{i}", [P, KH * FF], F32R) for i in range(2)]
        self.w1_lo = [s.sb(f"w1_lo{i}", [P, KH * FF], F32R) for i in range(2)]
        self.w2_hi = [s.sb(f"w2_hi{i}", [P, FF // P * D], F32R) for i in range(2)]
        self.w2_lo = [s.sb(f"w2_lo{i}", [P, FF // P * D], F32R) for i in range(2)]
        self.w1_loaded = s.sem("w1_loaded")
        self.w2_loaded = s.sem("w2_loaded")
        self.w_high = s.sem("w_high")
        self.w1_ready = s.sem("w1_ready")
        self.w2_ready = s.sem("w2_ready")

    def piece(self, number, parity):
        first = number < self.PIECES
        stage, hi, lo, loaded, ready = ((self.w1, self.w1_hi, self.w1_lo, self.w1_loaded, self.w1_ready) if first else
                                        (self.w2, self.w2_hi, self.w2_lo, self.w2_loaded, self.w2_ready))
        c = slice(number % self.PIECES * self.PIECE, (number % self.PIECES + 1) * self.PIECE)
        return stage[:, c], hi[parity][:, c], lo[parity][:, c], loaded, ready

    def round(self, act, pair, parity, number):
        stage, hi, _, loaded, _ = self.piece(number, parity)
        act.wait_ge(loaded, 16 * (2 * pair + parity + 1))
        act.activation(hi, stage, ACT.Copy).then_inc(self.w_high, 1)

    def rest(self, engine, pair, parity, number):
        stage, hi, lo, _, ready = self.piece(number, parity)
        engine.wait_ge(self.w_high, 2 * self.PIECES * (2 * pair + parity) + number + 1)
        engine.tensor_tensor(lo, stage, hi.bitcast(F32), ALU.subtract).then_inc(ready, 1)


def choose_phase(nc, ident, gate_all, row_stored, lists_dram, const, weights, w1_dram, w2_dram):
    CH = P // EXPERTS
    J = T // CH
    ROUNDS = 15
    UNROLL = 3
    LO = 32
    HI = TOPK // LO
    M = 2 * P
    with ExitStack() as ctx:
        s = Scope(nc, ctx, "choose")
        bits_i, bits_f, same, before, place = const.bits_i, const.bits_f, const.same, const.before, const.place
        same_bf = s.sb("same_bf", [P, P], BF16)
        iota_bf = s.sb("iota_bf", [P, LO], BF16)
        tile_bf = s.sb("tile_bf", [P, 2 * CH], BF16)
        gate = s.sb("gate", [P, J])
        hit = s.sb("hit", [P, 3, J])
        count = s.sb("count", [P, 3], BF16)
        reach = s.sb("reach", [P, 3])
        digit = s.sb("digit", [P, 1])
        limit = s.sb("limit", [P, 1], I32)
        base = s.sb("base", [P, 3], I32)
        trial = s.sb("trial", [P, 3], I32)
        gain = s.sb("gain", [P, 1], I32)
        above = s.sb("above", [P, J])
        n_above = s.sb("n_above", [P, 1])
        equal = s.sb("equal", [P, J])
        ones = s.sb("ones", [P, J])
        cum = s.sb("cum", [P, J])
        room = s.sb("room", [P, 1])
        start = s.sb("start", [P, 1])
        taken = s.sb("taken", [P, J])
        chosen = s.sb("chosen", [P, J])
        cum2 = s.sb("cum2", [P, J])
        start2 = s.sb("start2", [P, 1])
        slot = s.sb("slot", [P, J])
        slot_i = s.sb("slot_i", [P, J], I32)
        part_i = s.sb("part_i", [P, 2, J], I32)
        part_f = s.sb("part_f", [P, 2, J])
        turned = s.sb("turned", [P, 2, M], BF16)
        hi_hot = s.sb("hi_hot", [P, M, HI], BF16)
        lo_hot = s.sb("lo_hot", [P, M, LO], BF16)
        lo_val = s.sb("lo_val", [P, M, 2, LO], BF16)
        tiles = s.sb("tiles", [P, EXPERTS, 2, LO])
        token = s.sb("token", [HI, EXPERTS, LO], I32)

        gate_ps = s.ps("gate", [P, J])
        count_ps = s.ps("count", [P, 4])
        turn_ps = s.ps("turn", [P, 2 * M])
        list_ps = s.ps("list", [HI, EXPERTS, 2 * LO])

        gate_turned = s.sem("gate_turned")
        started = s.sem("started")
        counted = s.sem("counted")
        totalled = s.sem("totalled")
        stepped = s.sem("stepped")
        chain = s.sem("chain")
        stage = s.sem("stage")
        above_summed = s.sem("above_summed")
        starts_ready = s.sem("starts_ready")
        starts2_ready = s.sem("starts2_ready")
        parts_turned = s.sem("parts_turned")
        turned_ready = s.sem("turned_ready")
        hi_ready = s.sem("hi_ready")
        lo_ready = s.sem("lo_ready")
        place_ready = s.sem("place_ready")
        tile_ready = s.sem("tile_ready")
        last_tile_ready = s.sem("last_tile_ready")
        list_ready = s.sem("list_ready")
        token_ready = s.sem("token_ready")
        list_stored = s.sem("list_stored")
        BLOCK = 2 * CH
        BLOCKS = EXPERTS // 2

        def times_tile(engine, b, par, ready):
            c = slice(par * P + b * BLOCK, par * P + (b + 1) * BLOCK)
            engine.tensor_tensor(lo_val[:, c, 1, :].rearrange("p (e c) l -> p e c l", e=2),
                                 lo_hot[:, c, :].rearrange("p (e c) l -> p e c l", e=2),
                                 tile_bf[:, par * CH:(par + 1) * CH].unsqueeze(1).unsqueeze(3).broadcast_to([P, 2, CH, LO]),
                                 ALU.mult).then_inc(ready, 1)

        with nc.Block() as block:

            @block.sync
            def _(sp):
                sp.dma_start(weights.w1[:], w1_dram[0].rearrange("p a b -> p (a b)")).then_inc(weights.w1_loaded, 16)
                sp.dma_start(weights.w2[:], w2_dram[0].rearrange("p a b -> p (a b)")).then_inc(weights.w2_loaded, 16)
                for r in row_stored:
                    sp.wait_ge(r, 32 * (NT // 2))
                sp.wait_ge(token_ready, 1)
                sp.dma_start(lists_dram.rearrange("e (h l) -> h e l", l=LO), token[:]).then_inc(list_stored, 16)
                sp.wait_ge(list_stored, 16)

            @block.tensor
            def _(pe):
                for par in range(2):
                    last = pe.transpose(gate_ps[:, par * P:(par + 1) * P], gate_all[:, par, :, :].rearrange("p e c -> p (e c)"), ident[:])
                last.then_inc(gate_turned, 1)
                pe.wait_ge(const.loaded, const.count)
                pe.wait_ge(started, 4)
                with pe.Fori(0, ROUNDS // UNROLL) as i:
                    for n in range(UNROLL):
                        pe.wait_ge(counted, UNROLL * i + n + 1)
                        pe.matmul(count_ps[:, 0:3], same_bf[:], count[:], start=True, stop=True).then_inc(totalled, 1)
                pe.wait_ge(stage, 3)
                pe.matmul(count_ps[:, 0:1], same[:], n_above[:], start=True, stop=True).then_inc(above_summed, 1)
                pe.wait_ge(stage, 4)
                pe.matmul(count_ps[:, 1:2], before[:], cum[:, J - 1:J], start=True, stop=True).then_inc(starts_ready, 1)
                pe.wait_ge(stage, 8)
                pe.matmul(count_ps[:, 2:3], before[:], cum2[:, J - 1:J], start=True, stop=True).then_inc(starts2_ready, 1)
                pe.wait_ge(stage, 13)
                for h in range(2):
                    for par in range(2):
                        c = (2 * h + par) * P
                        last = pe.transpose(turn_ps[:, c:c + P], part_f[:, h, par * P:(par + 1) * P], ident[:])
                last.then_inc(parts_turned, 1)
                for e in range(EXPERTS):
                    pe.wait_ge(hi_ready, e // 2 + 1)
                    pe.wait_ge(place_ready, e // 2 + 1)
                    pe.wait_ge(tile_ready, min(2 * (e // 2 + 1), EXPERTS - 1))
                    if e == EXPERTS - 2:
                        pe.wait_ge(last_tile_ready, 1)
                    for par in range(2):
                        for c in range(CH):
                            col = par * P + e * CH + c
                            last = pe.matmul(list_ps[:, e, :], hi_hot[:, col, :], lo_val[:, col, :, :],
                                             start=(par == 0 and c == 0), stop=(par == 1 and c == CH - 1))
                last.then_inc(list_ready, 1)

            @block.gpsimd
            def _(pool):
                pool.wait_ge(const.loaded, const.count)
                pool.tensor_copy(same_bf[:], same[:]).then_inc(started, 1)
                pool.tensor_copy(iota_bf[:], const.iota[:]).then_inc(started, 1)
                pool.tensor_copy(tile_bf[:], place[:, 1:1 + 2 * CH]).then_inc(started, 1)
                pool.memset(ones[:], 1.0).then_inc(started, 1)
                for number in range(2 * weights.PIECES):
                    weights.rest(pool, 0, 0, number)
                for b in range(BLOCKS):
                    pool.wait_ge(lo_ready, b + 1)
                    times_tile(pool, b, 0, tile_ready)
                    if b < BLOCKS - 1:
                        times_tile(pool, b, 1, tile_ready)

            @block.scalar
            def _(act):
                for number in range(2 * weights.PIECES):
                    weights.round(act, 0, 0, number)

            @block.vector
            def _(dve):
                dve.memset(limit[:], 0)
                dve.wait_ge(const.loaded, const.count)
                dve.tensor_copy(trial[:], bits_i[:, 0, :])
                dve.wait_ge(gate_turned, 1)
                dve.tensor_copy(gate[:], gate_ps[:]).then_inc(stepped, 1)
                with dve.Fori(0, ROUNDS // UNROLL) as i:
                    for n in range(UNROLL):
                        q = UNROLL * i + n
                        dve.wait_ge(stepped, 2 * q + 1)
                        for j in range(3):
                            last = dve.tensor_scalar(hit[:, j, :], gate[:], trial[:, j:j + 1].bitcast(F32), None, ALU.is_ge, ALU.add,
                                                     accum_out=count[:, j:j + 1])
                        last.then_inc(counted, 1)
                        dve.tensor_tensor(base[:], limit[:].broadcast_to([P, 3]), bits_i[:, ds(q + 1, 1), :].rearrange("p o b -> p (o b)"),
                                          ALU.bitwise_or).then_inc(chain, 1)
                        dve.wait_ge(totalled, q + 1)
                        dve.tensor_scalar(reach[:], count_ps[:, 0:3], float(TOPK), None, ALU.is_ge, ALU.add, accum_out=digit[:]).then_inc(chain, 1)
                        dve.wait_ge(chain, 3 * q + 2)
                        dve.tensor_scalar(gain[:], digit[:], bits_f[:, ds(q, 1)], None, ALU.mult).then_inc(chain, 1)
                        dve.wait_ge(chain, 3 * q + 3)
                        dve.tensor_tensor(trial[:], base[:], gain[:].broadcast_to([P, 3]), ALU.bitwise_or).then_inc(stepped, 1)
                        dve.tensor_tensor(limit[:], limit[:], gain[:], ALU.bitwise_or).then_inc(stepped, 1)
                dve.wait_ge(stepped, 2 * ROUNDS + 1)
                dve.tensor_scalar(above[:], gate[:], trial[:, 0:1].bitcast(F32), None, ALU.is_gt, ALU.add, accum_out=n_above[:]).then_inc(stage, 3)
                dve.tensor_scalar(equal[:], gate[:], trial[:, 0:1].bitcast(F32), None, ALU.is_equal).then_inc(started, 1)
                dve.wait_ge(started, 5)
                dve.tensor_tensor_scan(cum[:], ones[:], equal[:], 0.0, ALU.mult, ALU.add).then_inc(stage, 1)
                dve.wait_ge(above_summed, 1)
                dve.wait_ge(starts_ready, 1)
                dve.tensor_scalar(room[:], count_ps[:, 0:1], -1.0, float(TOPK), ALU.mult, ALU.add)
                dve.tensor_copy(start[:], count_ps[:, 1:2]).then_inc(stage, 1)
                dve.wait_ge(stage, 5)
                dve.tensor_scalar(taken[:], cum[:], start[:, 0:1], room[:, 0:1], ALU.add, ALU.is_le).then_inc(stage, 1)
                dve.wait_ge(stage, 6)
                dve.tensor_tensor(equal[:], equal[:], taken[:], ALU.mult).then_inc(stage, 1)
                dve.wait_ge(stage, 7)
                dve.tensor_tensor(chosen[:], above[:], equal[:], ALU.add).then_inc(started, 1)
                dve.wait_ge(started, 6)
                dve.tensor_tensor_scan(cum2[:], ones[:], chosen[:], 0.0, ALU.mult, ALU.add).then_inc(stage, 1)
                dve.wait_ge(starts2_ready, 1)
                dve.tensor_copy(start2[:], count_ps[:, 2:3]).then_inc(stage, 1)
                dve.wait_ge(stage, 9)
                dve.scalar_tensor_tensor(slot[:], cum2[:], start2[:, 0:1], chosen[:], ALU.add, ALU.mult).then_inc(stage, 1)
                dve.wait_ge(stage, 10)
                dve.tensor_scalar(slot_i[:], slot[:], -1.0, None, ALU.add).then_inc(stage, 1)
                dve.wait_ge(stage, 11)
                dve.tensor_scalar(part_i[:, 0, :], slot_i[:], 5, None, ALU.arith_shift_right)
                dve.tensor_scalar(part_i[:, 1, :], slot_i[:], LO - 1, None, ALU.bitwise_and).then_inc(stage, 1)
                dve.wait_ge(stage, 12)
                dve.tensor_copy(part_f[:], part_i[:]).then_inc(stage, 1)
                dve.wait_ge(parts_turned, 1)
                dve.tensor_copy(turned[:].rearrange("p h m -> p (h m)"), turn_ps[:]).then_inc(turned_ready, 1)
                dve.wait_ge(turned_ready, 1)
                for b in range(BLOCKS):
                    cols = slice(b * BLOCK, (b + 1) * BLOCK)
                    for hot, n, ready in ((lo_hot, 1, lo_ready), (hi_hot, 0, hi_ready)):
                        dve.tensor_tensor(hot[:].rearrange("p (r m) l -> p r m l", r=2)[:, :, cols, :],
                                          turned[:, n, :].rearrange("p (r m) -> p r m", r=2)[:, :, cols].unsqueeze(3).broadcast_to([P, 2, BLOCK, LO]),
                                          iota_bf[:].unsqueeze(1).unsqueeze(1).broadcast_to([P, 2, BLOCK, LO]), ALU.is_equal).then_inc(ready, 1)
                    dve.wait_ge(lo_ready, b + 1)
                    dve.tensor_scalar(lo_val[:].rearrange("p (r m) a l -> p r m a l", r=2)[:, :, cols, 0, :],
                                      lo_hot[:].rearrange("p (r m) l -> p r m l", r=2)[:, :, cols, :], place[:, 0:1], None, ALU.mult).then_inc(place_ready, 1)
                    if b == BLOCKS - 1:
                        times_tile(dve, b, 1, last_tile_ready)
                dve.wait_ge(list_ready, 1)
                dve.tensor_copy(tiles[:HI].rearrange("p e a l -> p e (a l)"), list_ps[:]).then_inc(stepped, 1)
                dve.wait_ge(stepped, 2 * ROUNDS + 2)
                dve.scalar_tensor_tensor(token[:], tiles[:HI, :, 1, :], float(P), tiles[:HI, :, 0, :], ALU.mult, ALU.add).then_inc(token_ready, 1)


class Half:

    def __init__(self, pair, number):
        self.pair, self.number = pair + number // 4, number % 4
        self.parity = self.number // 2
        self.part = self.number % 2
        self.expert = 2 * self.pair + self.parity
        self.u = 4 * self.pair + self.number

    def plus(self, n):
        return Half(self.pair, self.number + n)


def expert_phase(nc, ident, weights, lists_dram, table_dram, acc_dram, w1_dram, b1_dram, w2_dram, b2_dram):
    FT = FF // P
    ST = TOPK // P
    HS = ST // 2
    W = HS * P
    PIECES = weights.PIECES
    LAG = 2
    RING_H = 4
    with ExitStack() as ctx:
        s = Scope(nc, ctx, "expert")
        lists = s.sb("lists", [P, EXPERTS, ST], I32)
        lst = [s.sb(f"lst{i}", [P, ST], I32) for i in range(2)]
        w1_hi, w1_lo, w2_hi, w2_lo = weights.w1_hi, weights.w1_lo, weights.w2_hi, weights.w2_lo
        w1_ready, w2_ready = weights.w1_ready, weights.w2_ready
        b1 = [s.sb(f"b1{i}", [P, FT]) for i in range(2)]
        b2 = [s.sb(f"b2{i}", [P, D]) for i in range(2)]
        xg = [s.sb(f"xg{i}", [P, ST, ROW]) for i in range(2)]
        gate = [s.sb(f"gate{i}", [P, ST]) for i in range(2)]
        x_hi = [s.sb(f"x_hi{i}", [P, KH, W], F32R) for i in range(2)]
        x_lo = [s.sb(f"x_lo{i}", [P, KH, W], F32R) for i in range(2)]
        hid = s.sb("hid", [P, 2, W])
        hid_hi = s.sb("hid_hi", [P, RING_H, W], F32R)
        hid_lo = s.sb("hid_lo", [P, RING_H, W], F32R)
        rows = [s.sb(f"rows{i}", [P, HS, D]) for i in range(2)]

        h_ps = [s.ps(f"h{i}", [P, W]) for i in range(2)]
        o_ps = [s.ps(f"o{i}", [P, 2 * D]) for i in range(4)]
        t_ps = [s.ps(f"t{i}", [P, W]) for i in range(2)]

        lists_loaded = s.sem("lists_loaded")
        b1_loaded = [s.sem(f"b1_loaded{i}") for i in range(2)]
        b2_loaded = [s.sem(f"b2_loaded{i}") for i in range(2)]
        gathered = [[s.sem(f"gathered{i}{part}") for part in range(2)] for i in range(2)]
        scattered = [s.sem(f"scattered{i}") for i in range(2)]
        lst_ready = s.sem("lst_ready")
        gate_ready = s.sem("gate_ready")
        turned = s.sem("turned")
        x_high = s.sem("x_high")
        x_ready = s.sem("x_ready")
        h_ready = s.sem("h_ready")
        gelu_done = s.sem("gelu_done")
        hid_high = s.sem("hid_high")
        hid_ready = s.sem("hid_ready")
        hid_used = s.sem("hid_used")
        biased = s.sem("biased")
        rows_ready = s.sem("rows_ready")
        waited = s.sem("waited")
        PAIRS = EXPERTS // 2

        def halves(eng, half):
            half(Half(0, 0), before=False)
            for n in range(1, 4):
                half(Half(0, n))
            with eng.Fori(1, PAIRS - 1) as i:
                for n in range(4):
                    half(Half(i, n))
            for n in range(3):
                half(Half(PAIRS - 1, n))
            half(Half(PAIRS - 1, 3), after=False)

        def has_next_expert(h):
            return not (isinstance(h.pair, int) and h.pair == PAIRS - 1 and h.parity == 1)

        with nc.Block() as block:

            @block.sync
            def _(sp):
                sp.dma_start(lists[:], lists_dram.rearrange("e (p s) -> p e s", s=ST)).then_inc(lists_loaded, 16)

                def load(pair, par, first=False):
                    e = 2 * pair + par
                    if not (first and par == 0):
                        sp.wait_ge(w1_ready, PIECES * e)
                        sp.dma_start(weights.w1[:], w1_dram[ds(e, 1)].rearrange("o p a b -> (o p) (a b)")).then_inc(weights.w1_loaded, 16)
                        sp.wait_ge(w2_ready, PIECES * e)
                        sp.dma_start(weights.w2[:], w2_dram[ds(e, 1)].rearrange("o p a b -> (o p) (a b)")).then_inc(weights.w2_loaded, 16)
                    if not first:
                        sp.wait_ge(gelu_done, 2 * FT * (e - 1))
                    sp.dma_start(b1[par][:], b1_dram[ds(e, 1)].rearrange("o p a -> (o p) a")).then_inc(b1_loaded[par], 16)
                    if not first:
                        sp.wait_ge(rows_ready, ST * (e - 1))
                    sp.dma_start(b2[par][:], b2_dram[ds(e, 1)].broadcast_to([P, D])).then_inc(b2_loaded[par], 16)

                load(0, 0, first=True)
                load(0, 1, first=True)
                with sp.Fori(1, PAIRS) as i:
                    load(i, 0)
                    load(i, 1)

            @block.gpsimd
            def _(pool):
                def gather(pair, par, first=False):
                    e = 2 * pair + par
                    if not first:
                        for part in range(2):
                            pool.wait_ge(scattered[part], 16 * HS * (e - 1))
                        pool.wait_ge(turned, 4 * (e - 1))
                        pool.wait_ge(gate_ready, e - 1)
                    pool.tensor_copy(lst[par][:], lists[:, ds(e, 1), :].rearrange("p o s -> p (o s)")).then_inc(lst_ready, 1)
                    pool.wait_ge(lst_ready, e + 1)
                    pool.sem_inc(waited, 1)
                    for t in range(ST):
                        pool.indirect_dma_start(out=xg[par][:, t, :], out_offset=None, in_=table_dram,
                                                in_offset=bass.IndirectOffsetOnAxis(ap=lst[par][:, t:t + 1], axis=0)
                                                ).then_inc(gathered[par][t // HS], 16)

                def scatter(h):
                    for t in range(HS):
                        pool.wait_ge(rows_ready, HS * h.u + t + 1)
                        if t == 0 and h.part == 0:
                            for part in range(2):
                                since(pool, scattered[part], 16 * HS * h.expert)
                        pool.sem_inc(waited, 1)
                        n = HS * h.part + t
                        pool.indirect_dma_start(out=acc_dram, out_offset=bass.IndirectOffsetOnAxis(ap=lst[h.parity][:, n:n + 1], axis=0),
                                                in_=rows[h.part][:, t, :], in_offset=None, compute_op=ALU.add
                                                ).then_inc(scattered[h.part], 16)

                pool.wait_ge(lists_loaded, 16)
                gather(0, 0, first=True)
                gather(0, 1, first=True)
                scatter(Half(0, 0))
                scatter(Half(0, 1))
                with pool.Fori(1, PAIRS) as i:
                    gather(i, 0)
                    scatter(Half(i - 1, 2))
                    scatter(Half(i - 1, 3))
                    gather(i, 1)
                    scatter(Half(i, 0))
                    scatter(Half(i, 1))
                scatter(Half(PAIRS - 1, 2))
                scatter(Half(PAIRS - 1, 3))
                for part in range(2):
                    pool.wait_ge(scattered[part], 16 * HS * EXPERTS)

            @block.tensor
            def _(pe):
                def turn(h, k):
                    pe.wait_ge(gathered[h.parity][h.part], 16 * HS * (h.pair + 1))
                    since(pe, x_ready, KH * h.u + k - 1)
                    for t in range(HS):
                        last = pe.transpose(t_ps[k][:, t * P:(t + 1) * P], xg[h.parity][:, HS * h.part + t, k * P:(k + 1) * P], ident[:])
                    last.then_inc(turned, 1)

                def first(h, f):
                    if f == 0:
                        pe.wait_ge(x_ready, KH * (h.u + 1))
                        pe.wait_ge(w1_ready, PIECES * (h.expert + 1))
                    since(pe, gelu_done, FT * h.u + f - 1)
                    pairs = []
                    for k in range(KH):
                        c = slice(k * FF + f * P, k * FF + (f + 1) * P)
                        pairs.append((w1_hi[h.parity][:, c], w1_lo[h.parity][:, c], x_hi[h.part][:, k, :], x_lo[h.part][:, k, :]))
                    products(pe, h_ps[f % 2][:], pairs, True, True).then_inc(h_ready, 1)

                def second(h, f):
                    if f == 0:
                        pe.wait_ge(w2_ready, PIECES * (h.expert + 1))
                        since(pe, biased, 2 * h.u - 2)
                    pe.wait_ge(hid_ready, FT * h.u + f + 1)
                    w = slice(f * D, (f + 1) * D)
                    for t in range(HS):
                        c = slice(t * P, (t + 1) * P)
                        out = o_ps[2 * h.part + t // 2][:, t % 2 * D:(t % 2 + 1) * D]
                        last = products(pe, out, [(hid_hi[:, f % RING_H, c], hid_lo[:, f % RING_H, c], w2_hi[h.parity][:, w],
                                               w2_lo[h.parity][:, w])],
                                        f == 0 and t % 2 == 0, f == FT - 1)
                    last.then_inc(hid_used, 1)

                def half(h, before=True, after=True):
                    for f in range(FT):
                        first(h, f)
                        if f >= LAG:
                            second(h, f - LAG)
                        elif before:
                            second(h.plus(-1), FT + f - LAG)
                        if after and f == 3:
                            turn(h.plus(1), 0)
                        if after and f == 5:
                            turn(h.plus(1), 1)

                turn(Half(0, 0), 0)
                turn(Half(0, 0), 1)
                halves(pe, half)
                for f in range(FT - LAG, FT):
                    second(Half(PAIRS - 1, 3), f)

            @block.scalar
            def _(act):
                nc.scalar.preload_act_table_set("gelu_and_others")

                def gelu(h, f):
                    if f == 0:
                        act.wait_ge(b1_loaded[h.parity], 16 * (h.pair + 1))
                    since(act, hid_ready, FT * h.u + f - 1)
                    act.wait_ge(h_ready, FT * h.u + f + 1)
                    act.activation(hid[:, f % 2, :], h_ps[f % 2][:], ACT.Gelu, bias=b1[h.parity][:, f:f + 1]).then_inc(gelu_done, 1)

                def round_hidden(h, f):
                    act.wait_ge(gelu_done, FT * h.u + f + 1)
                    since(act, hid_used, FT * h.u + f + 1 - RING_H)
                    act.activation(hid_hi[:, f % RING_H, :], hid[:, f % 2, :], ACT.Copy).then_inc(hid_high, 1)

                def half(h, before=True, after=True):
                    for f in range(FT):
                        gelu(h, f)
                        if has_next_expert(h):
                            n = h.plus(2)
                            weights.round(act, n.pair, n.parity, FT * h.part + f)
                        round_hidden(h, f)

                halves(act, half)

            @block.vector
            def _(dve):
                def rest_of_hidden(h, f):
                    dve.wait_ge(hid_high, FT * h.u + f + 1)
                    dve.tensor_tensor(hid_lo[:, f % RING_H, :], hid[:, f % 2, :], hid_hi[:, f % RING_H, :].bitcast(F32),
                                      ALU.subtract).then_inc(hid_ready, 1)

                def take_gates(h):
                    for part in range(2):
                        dve.wait_ge(gathered[h.parity][part], 16 * HS * (h.pair + 1))
                    dve.tensor_copy(gate[h.parity][:], xg[h.parity][:, :, ds(D + h.expert, 1)].rearrange("p s o -> p (s o)")).then_inc(gate_ready, 1)

                def split_rows(h, k):
                    dve.wait_ge(turned, KH * h.u + k + 1)
                    dve.tensor_copy(x_hi[h.part][:, k, :], t_ps[k][:]).then_inc(x_high, 1)
                    dve.wait_ge(x_high, KH * h.u + k + 1)
                    dve.tensor_tensor(x_lo[h.part][:, k, :], t_ps[k][:], x_hi[h.part][:, k, :].bitcast(F32), ALU.subtract).then_inc(x_ready, 1)

                def weigh(h):
                    dve.wait_ge(hid_used, FT * (h.u + 1))
                    since(dve, scattered[h.part], 16 * HS * h.expert)
                    dve.wait_ge(b2_loaded[h.parity], 16 * (h.pair + 1))
                    for b in range(2):
                        dve.tensor_tensor(rows[h.part][:, 2 * b:2 * b + 2, :], o_ps[2 * h.part + b][:].rearrange("p (t d) -> p t d", d=D),
                                          b2[h.parity][:].unsqueeze(1).broadcast_to([P, 2, D]), ALU.add).then_inc(biased, 1)
                    dve.wait_ge(gate_ready, h.expert + 1)
                    for t in range(HS):
                        if t % 2 == 0:
                            dve.wait_ge(biased, 2 * h.u + t // 2 + 1)
                        n = HS * h.part + t
                        dve.tensor_scalar(rows[h.part][:, t, :], rows[h.part][:, t, :], gate[h.parity][:, n:n + 1], None,
                                          ALU.mult).then_inc(rows_ready, 1)

                def half(h, before=True, after=True):
                    for f in range(FT):
                        rest_of_hidden(h, f)
                        if has_next_expert(h):
                            n = h.plus(2)
                            weights.rest(dve, n.pair, n.parity, FT * h.part + f)
                        if before and f == LAG:
                            weigh(h.plus(-1))
                        if after and f == 4:
                            if h.part == 1:
                                take_gates(h.plus(1))
                            split_rows(h.plus(1), 0)
                        if after and f == 6:
                            split_rows(h.plus(1), 1)

                split_rows(Half(0, 0), 0)
                split_rows(Half(0, 0), 1)
                take_gates(Half(0, 0))
                halves(dve, half)
                weigh(Half(PAIRS - 1, 3))


def final_phase(nc, acc_dram, out_dram):
    C = 8
    CHUNKS = T // (P * C)
    with ExitStack() as ctx:
        s = Scope(nc, ctx, "final")
        a = [s.sb(f"a{i}", [P, C, D]) for i in range(2)]
        o = [s.sb(f"o{i}", [P, C, D]) for i in range(2)]
        stats = s.sb("stats", [P, C, 6])
        part = s.sb("part", [P, 4, C])
        mean = s.sb("mean", [P, C])
        var = s.sb("var", [P, C])
        lnv = s.sb("lnv", [P, C])
        rstd = s.sb("rstd", [P, C])
        shift = s.sb("shift", [P, C])
        eps = s.sb("eps", [P, 1])
        shift_ready = s.sem("shift_ready")
        loaded = [s.sem(f"loaded{i}") for i in range(2)]
        stored = [s.sem(f"stored{i}") for i in range(2)]
        stats_ready = s.sem("stats_ready")
        moments = s.sem("moments")
        lnv_ready = s.sem("lnv_ready")
        rstd_ready = s.sem("rstd_ready")
        normed = s.sem("normed")
        set_up = s.sem("set_up")

        def both(eng, step):
            step(0, 0)
            step(0, 1)
            with eng.Fori(1, CHUNKS // 2) as i:
                step(i, 0)
                step(i, 1)

        with nc.Block() as block:

            @block.sync
            def _(sp):
                def load(i, par):
                    c = 2 * i + par
                    since(sp, normed, c - 1)
                    sp.dma_start(a[par][:], acc_dram[ds(c * P * C, P * C), :].rearrange("(p t) d -> p t d", t=C)).then_inc(loaded[par], 16)

                both(sp, load)

            @block.scalar
            def _(act):
                def step(i, par):
                    c = 2 * i + par
                    act.wait_ge(moments, 3 * (c + 1))
                    act.activation(lnv[:], var[:], ACT.Ln, bias=eps[:, 0:1]).then_inc(lnv_ready, 1)
                    act.wait_ge(lnv_ready, c + 1)
                    act.activation(rstd[:], lnv[:], ACT.Exp, scale=-0.5).then_inc(rstd_ready, 1)
                    act.wait_ge(shift_ready, c + 1)
                    since(act, stored[par], 16 * i)
                    for t in range(C):
                        last = act.activation(o[par][:, t, :], a[par][:, t, :], ACT.Identity, bias=shift[:, t:t + 1], scale=rstd[:, t:t + 1])
                    last.then_inc(normed, 1)
                    act.wait_ge(normed, c + 1)
                    act.dma_start(out_dram[ds(c * P * C, P * C), :].rearrange("(p t) d -> p t d", t=C), o[par][:]).then_inc(stored[par], 16)

                nc.scalar.preload_act_table_set("natural_log_exp_and_others")
                act.wait_ge(set_up, 1)
                both(act, step)
                for q in stored:
                    act.wait_ge(q, 16 * (CHUNKS // 2))

            @block.vector
            def _(dve):
                def step(i, par):
                    c = 2 * i + par
                    dve.wait_ge(loaded[par], 16 * (i + 1))
                    for t in range(C):
                        last = dve.bn_stats(stats[:, t, :], a[par][:, t, :])
                    last.then_inc(stats_ready, 1)
                    merge_moments(dve, stats, stats_ready, c + 1, part, mean, var, moments, c)
                    dve.wait_ge(rstd_ready, c + 1)
                    since(dve, normed, c)
                    dve.scalar_tensor_tensor(shift[:], mean[:], -1.0, rstd[:], ALU.mult, ALU.mult).then_inc(shift_ready, 1)

                dve.memset(eps[:], EPS).then_inc(set_up, 1)
                both(dve, step)


def build(nc, xT, w_proj, w_bc, w_dt, b_dt, a_log, sel, ident_dram, ctxT, w_q, w_kv, w_o, w_g, norm, even_odd, pick,
          bits_i, bits_f, same, before, iota, place, w1, b1, w2, b2, out):
    table = nc.dram_tensor("table", (T, ROW), F32, kind="Internal").ap()
    acc = nc.dram_tensor("acc", (T, D), F32, kind="Internal").ap()
    lists = nc.dram_tensor("lists", (EXPERTS, TOPK), I32, kind="Internal").ap()
    with ExitStack() as ctx:
        s = Scope(nc, ctx, "all")
        ident = s.sb("ident", [P, P])
        gate_all = s.sb("gate_all", [P, 2, EXPERTS, NT // 2])
        row = [s.sb(f"row{i}", [P, ROW]) for i in range(2)]
        row_stored = [s.sem(f"row_stored{i}") for i in range(2)]
        choice = ChoiceConstants(s, bits_i, bits_f, same, before, iota, place)
        with ExitStack() as front:
            x1 = Scope(nc, front, "front").sb("x1", [P, GB + NT, D])
            attention = AttentionConstants(Scope(nc, front, "xattn"), w_q, w_kv, w_o, w_g, norm, even_odd, pick)
            scan_phase(nc, x1, (ident, ident_dram), xT, w_proj, w_bc, w_dt, b_dt, a_log, sel, attention)
            attention_phase(nc, x1, ident, gate_all, attention, ctxT, table, acc, choice, row, row_stored)
        with ExitStack() as back:
            weights = Weights(Scope(nc, back, "weights"))
            choose_phase(nc, ident, gate_all, row_stored, lists, choice, weights, w1, w2)
            expert_phase(nc, ident, weights, lists, table, acc, w1, b1, w2, b2)
        final_phase(nc, acc, out)


def kernel(x, ctx_1024, L0_attn_W_xproj, L0_attn_W_dt, L0_attn_b_dt, L0_attn_A_log, L0_xattn_Wq, L0_xattn_Wk,
           L0_xattn_Wv, L0_xattn_Wo, L0_xattn_ln_gamma, L0_xattn_ln_beta, L0_ffn_Wg, L0_ffn_W1, L0_ffn_b1,
           L0_ffn_W2, L0_ffn_b2):
    import ml_dtypes
    import concourse.bacc as bacc
    from concourse.bass_utils import run_bass_kernel_spmd

    def halves(a):
        return np.ascontiguousarray(a.reshape(KH, P, -1).transpose(1, 0, 2))

    x = np.asarray(x)
    w_xproj = np.asarray(L0_attn_W_xproj)
    w_bc = np.concatenate([w_xproj[R:]] * 3, axis=0)
    sel = np.zeros((96, 2 * NS, P), ml_dtypes.bfloat16)
    for part in range(3):
        for n in range(2 * NS):
            sel[32 * part + n, n, :] = 1
    bits = np.array([[n << shift for n in (1, 2, 3)] for shift in range(28, -1, -2)] + [[0, 0, 0]], np.int32)
    expert_of = np.arange(P) // (P // EXPERTS)
    same = expert_of[:, None] == expert_of[None, :]
    place = np.zeros((P, 1 + NT), np.float32)
    place[:, 0] = np.arange(P)
    for parity in range(2):
        place[:, 1 + parity * 16:1 + (parity + 1) * 16] = 2 * np.arange(16) + parity
    head_of = np.arange(P) // DK % 2
    even_odd = np.stack([head_of == 0, head_of == 1], axis=1).astype(np.float32)
    pick = np.zeros((P, HEADS, P), ml_dtypes.bfloat16)
    for h in range(HEADS):
        strip, k, e = h % 8 // 2, h // 8, h % 2
        pick[32 * strip + 2 * k + e, h, :] = 1
    arrays = {
        "xT": halves(x.reshape(T, D).T),
        "w_proj": halves(w_xproj[:R].T),
        "w_bc": halves(w_bc.T),
        "w_dt": np.ascontiguousarray(np.asarray(L0_attn_W_dt).T),
        "b_dt": np.ascontiguousarray(np.asarray(L0_attn_b_dt).reshape(KH, P).T),
        "a_log": halves(np.asarray(L0_attn_A_log)),
        "sel": sel,
        "ident": np.eye(P, dtype=np.float32),
        "ctxT": halves(np.asarray(ctx_1024).reshape(T, D).T),
        "w_q": halves(np.asarray(L0_xattn_Wq).T),
        "w_kv": halves(np.concatenate([np.asarray(L0_xattn_Wk).T, np.asarray(L0_xattn_Wv).T], axis=1)),
        "w_o": halves(np.asarray(L0_xattn_Wo).T),
        "w_g": halves(np.asarray(L0_ffn_Wg)),
        "norm": np.ascontiguousarray(np.stack([np.asarray(a).reshape(KH, P) for a in (L0_xattn_ln_gamma, L0_xattn_ln_beta)]).transpose(2, 0, 1)),
        "even_odd": even_odd,
        "pick": pick,
        "bits_i": np.tile(bits, (P, 1, 1)),
        "bits_f": np.tile(bits[:-1, 0].astype(np.float32), (P, 1)),
        "same": same.astype(np.float32),
        "before": (same & (np.arange(P)[:, None] < np.arange(P)[None, :])).astype(np.float32),
        "iota": np.tile(np.arange(32, dtype=np.float32), (P, 1)),
        "place": place,
        "w1": np.ascontiguousarray(np.asarray(L0_ffn_W1).reshape(EXPERTS, KH, P, FF).transpose(0, 2, 1, 3)),
        "b1": np.ascontiguousarray(np.asarray(L0_ffn_b1).reshape(EXPERTS, FF // P, P).transpose(0, 2, 1)),
        "w2": np.ascontiguousarray(np.asarray(L0_ffn_W2).reshape(EXPERTS, FF // P, P, D).transpose(0, 2, 1, 3)),
        "b2": np.ascontiguousarray(np.asarray(L0_ffn_b2)),
    }
    nc = bacc.Bacc("TRN2", target_bir_lowering=False, num_devices=1)
    args = [nc.dram_tensor(n, a.shape, mybir.dt.from_np(a.dtype), kind="ExternalInput").ap() for n, a in arrays.items()]
    out = nc.dram_tensor("out", (T, D), F32, kind="ExternalOutput").ap()
    build(nc, *args, out)
    r = run_bass_kernel_spmd(nc, [arrays], core_ids=[0])
    return np.asarray(r.results[0]["out"]).reshape(BATCH, SEQ, D)
```
